# Optimizing a Trainium2 kernel written in Bass

```python
import numpy as np
import jax
import jax.numpy as jnp

def _softmax(x, axis=-1):
    return jax.nn.softmax(x, axis=axis)

def _gelu(x):
    return jax.nn.gelu(x, approximate=True)

def _silu(x):
    return jax.nn.silu(x)

def _sigmoid(x):
    return jax.nn.sigmoid(x)

def _layernorm(x, axis=-1, eps=1e-05):
    m = jnp.mean(x, axis=axis, keepdims=True)
    v = jnp.var(x, axis=axis, keepdims=True)
    return (x - m) / jnp.sqrt(v + eps)

def _scatter_add(tgt, idx, src, axis=0):
    return tgt.at[idx].add(src)

def _segment_sum(src, seg, n):
    return jax.ops.segment_sum(src, seg, n)
kernel_name = 'mk_seq_postln_d2_jaxref_r8_2e33f5'

def setup_inputs(seed: int=0):
    np.random.seed(seed)
    _w = jnp.asarray

    def _L0_attn_setup():
        import jax, jax.numpy as jnp
        import numpy as np
        import math
        D_MODEL = 128
        D_INNER = 256
        D_HALF = D_INNER // 2
        D_STATE = 16
        D_CONV = 4
        DT_RANK = 64
        B_SZ = 4
        L = 256

        def _dw_conv(x, w, b):
            y = jax.lax.conv_general_dilated(x, w, window_strides=(1,), padding='SAME', feature_group_count=x.shape[-1], dimension_numbers=('NWC', 'WIO', 'NWC'))
            return y + b

        def _selective_scan(u, delta, A, Bc, Cc, D):
            b, l, d = u.shape
            n = A.shape[1]

            def step(h, inp):
                d_t, u_t, B_t, C_t = inp
                dA = jnp.exp(d_t[..., None] * A)
                h = dA * h + (d_t * u_t)[..., None] * B_t[:, None, :]
                y = jnp.einsum('bdn,bn->bd', h, C_t)
                return (h, y)
            h0 = jnp.zeros((b, d, n), u.dtype)
            xs = (jnp.moveaxis(delta, 1, 0), jnp.moveaxis(u, 1, 0), jnp.moveaxis(Bc, 1, 0), jnp.moveaxis(Cc, 1, 0))
            _, ys = jax.lax.scan(step, h0, xs)
            return jnp.moveaxis(ys, 0, 1) + u * D
        key = jax.random.key(seed)
        ks = jax.random.split(key, 12)
        x = jax.random.normal(ks[0], (B_SZ, L, D_MODEL), jnp.float32)
        W_in = jax.random.normal(ks[1], (D_MODEL, D_INNER), jnp.float32) * D_MODEL ** (-0.5)
        conv_x_w = jax.random.normal(ks[2], (D_CONV, 1, D_HALF), jnp.float32) * D_CONV ** (-0.5)
        conv_x_b = jnp.zeros((D_HALF,), jnp.float32)
        conv_z_w = jax.random.normal(ks[3], (D_CONV, 1, D_HALF), jnp.float32) * D_CONV ** (-0.5)
        conv_z_b = jnp.zeros((D_HALF,), jnp.float32)
        W_xdbl = jax.random.normal(ks[4], (D_HALF, DT_RANK + 2 * D_STATE), jnp.float32) * D_HALF ** (-0.5)
        dt_init_std = DT_RANK ** (-0.5)
        W_dt = jax.random.uniform(ks[5], (DT_RANK, D_HALF), jnp.float32, -dt_init_std, dt_init_std)
        rand_vals = jax.random.uniform(ks[6], (D_HALF,))
        dt_bias = jnp.exp(rand_vals * (math.log(0.1) - math.log(0.001)) + math.log(0.001))
        dt_bias = jnp.clip(dt_bias, 0.0001)
        inv_dt = dt_bias + jnp.log(-jnp.expm1(-dt_bias))
        D = jnp.ones((D_HALF,), jnp.float32)
        W_out = jax.random.normal(ks[7], (D_INNER, D_MODEL), jnp.float32) * D_INNER ** (-0.5)
        b_out = jnp.zeros((D_MODEL,), jnp.float32)
        return dict(x=x, W_in=W_in, conv_x_w=conv_x_w, conv_x_b=conv_x_b, conv_z_w=conv_z_w, conv_z_b=conv_z_b, W_xdbl=W_xdbl, W_dt=W_dt, inv_dt=inv_dt, D=D, W_out=W_out, b_out=b_out)
    _L0_attn_in = _L0_attn_setup()

    def _L0_ffn_setup():
        import jax, jax.numpy as jnp
        import numpy as np
        import math
        GOLDEN_CENTER = 1.0 / math.e
        GOLDEN_LOWER = 0.5 - math.log(4.0 / 3.0)
        GOLDEN_UPPER = 0.5
        B, T, D = (4, 256, 128)
        E = 8
        I = 512 // (E // 2)

        def _routing_weights(x, Wr, temperature):
            inh = jax.nn.sigmoid(x @ Wr / temperature)
            in_zone = (inh >= GOLDEN_LOWER) & (inh <= GOLDEN_UPPER)
            dist = jnp.abs(inh - GOLDEN_CENTER)
            w = jnp.exp(-dist / 0.1) * in_zone.astype(x.dtype)
            wsum = w.sum(axis=-1, keepdims=True)
            no_expert = wsum < 1e-08
            fb = jnp.exp(-dist / 0.3)
            _, top2 = jax.lax.top_k(fb, 2)
            fb_mask = jax.nn.one_hot(top2, E, dtype=x.dtype).sum(axis=-2)
            fb_w = fb * fb_mask
            fb_w = fb_w / jnp.clip(fb_w.sum(axis=-1, keepdims=True), 1e-08)
            w = jnp.where(no_expert, fb_w, w)
            wsum = w.sum(axis=-1, keepdims=True)
            return w / jnp.clip(wsum, 1e-08)
        key = jax.random.key(seed)
        k = jax.random.split(key, 6)
        s_d = 1.0 / math.sqrt(D)
        s_i = 1.0 / math.sqrt(I)
        return {'x': jax.random.normal(k[0], (B, T, D), jnp.float32), 'Wg': jax.random.normal(k[1], (E, D, I), jnp.float32) * s_d, 'Wu': jax.random.normal(k[2], (E, D, I), jnp.float32) * s_d, 'Wd': jax.random.normal(k[3], (E, I, D), jnp.float32) * s_i, 'Wr': jax.random.normal(k[4], (D, E), jnp.float32) * s_d, 'temperature': jnp.ones((1,), jnp.float32)}
    _L0_ffn_in = _L0_ffn_setup()

    def _L1_attn_setup():
        import jax, jax.numpy as jnp
        import numpy as np
        EPS = 1e-06
        key = jax.random.key(seed)
        ks = jax.random.split(key, 8)
        B, S, D = (4, 256, 128)
        sc = 1.0 / np.sqrt(D)
        return {'x_seq': jax.random.normal(ks[0], (B, S, D), jnp.float32), 'Wq': jax.random.normal(ks[1], (D, D), jnp.float32) * sc, 'bq': jax.random.normal(ks[2], (D,), jnp.float32) * 0.01, 'Wk': jax.random.normal(ks[3], (D, D), jnp.float32) * sc, 'bk': jax.random.normal(ks[4], (D,), jnp.float32) * 0.01, 'Wv': jax.random.normal(ks[5], (D, D), jnp.float32) * sc, 'bv': jax.random.normal(ks[6], (D,), jnp.float32) * 0.01, 'gamma': jnp.float32(0.9)}
    _L1_attn_in = _L1_attn_setup()

    def _L1_ffn_setup():
        import jax, jax.numpy as jnp
        import numpy as np
        HID = 128
        INTER = 512
        RDIM = 128
        HEADS = 4
        NUM_EXPERTS = 2048
        NUM_KEYS = 128
        TOPK = 8
        B, T = (2, 256)
        key = jax.random.key(seed)
        ks = jax.random.split(key, 8)
        s = lambda fan_in: 1.0 / np.sqrt(fan_in)
        return {'hidden_states': jax.random.normal(ks[0], (B, T, HID), jnp.float32), 'Wq': jax.random.normal(ks[1], (HEADS * RDIM, HID), jnp.float32) * s(HID), 'keys': jax.random.normal(ks[2], (HEADS, NUM_KEYS, 2, RDIM // 2), jnp.float32) * s(RDIM // 2), 'down_embed': jax.random.normal(ks[3], (NUM_EXPERTS, HID), jnp.float32) * 0.02, 'up_embed': jax.random.normal(ks[4], (NUM_EXPERTS, HID), jnp.float32) * 0.02, 'Wg': jax.random.normal(ks[5], (INTER, HID), jnp.float32) * s(HID), 'Wu': jax.random.normal(ks[6], (INTER, HID), jnp.float32) * s(HID), 'Wd': jax.random.normal(ks[7], (HID, INTER), jnp.float32) * s(INTER)}
    _L1_ffn_in = _L1_ffn_setup()
    _d = {'L0_attn_x': _L0_attn_in['x'], 'L0_attn_W_in': _L0_attn_in['W_in'], 'L0_attn_conv_x_w': _L0_attn_in['conv_x_w'], 'L0_attn_conv_x_b': _L0_attn_in['conv_x_b'], 'L0_attn_conv_z_w': _L0_attn_in['conv_z_w'], 'L0_attn_conv_z_b': _L0_attn_in['conv_z_b'], 'L0_attn_W_xdbl': _L0_attn_in['W_xdbl'], 'L0_attn_W_dt': _L0_attn_in['W_dt'], 'L0_attn_inv_dt': _L0_attn_in['inv_dt'], 'L0_attn_D': _L0_attn_in['D'], 'L0_attn_W_out': _L0_attn_in['W_out'], 'L0_attn_b_out': _L0_attn_in['b_out'], 'L0_ffn_Wg': _L0_ffn_in['Wg'], 'L0_ffn_Wu': _L0_ffn_in['Wu'], 'L0_ffn_Wd': _L0_ffn_in['Wd'], 'L0_ffn_Wr': _L0_ffn_in['Wr'], 'L0_ffn_temperature': _L0_ffn_in['temperature'], 'L1_attn_Wq': _L1_attn_in['Wq'], 'L1_attn_bq': _L1_attn_in['bq'], 'L1_attn_Wk': _L1_attn_in['Wk'], 'L1_attn_bk': _L1_attn_in['bk'], 'L1_attn_Wv': _L1_attn_in['Wv'], 'L1_attn_bv': _L1_attn_in['bv'], 'L1_attn_gamma': _L1_attn_in['gamma'], 'L1_ffn_Wq': _L1_ffn_in['Wq'], 'L1_ffn_keys': _L1_ffn_in['keys'], 'L1_ffn_down_embed': _L1_ffn_in['down_embed'], 'L1_ffn_up_embed': _L1_ffn_in['up_embed'], 'L1_ffn_Wg': _L1_ffn_in['Wg'], 'L1_ffn_Wu': _L1_ffn_in['Wu'], 'L1_ffn_Wd': _L1_ffn_in['Wd']}
    _x0 = _d['L0_attn_x']
    _d['L0_attn_x'] = jax.random.normal(jax.random.fold_in(jax.random.key(seed), 1), (32, 256, 128), dtype=_x0.dtype)
    del _x0
    return _d

def reference(L0_attn_x, L0_attn_W_in, L0_attn_conv_x_w, L0_attn_conv_x_b, L0_attn_conv_z_w, L0_attn_conv_z_b, L0_attn_W_xdbl, L0_attn_W_dt, L0_attn_inv_dt, L0_attn_D, L0_attn_W_out, L0_attn_b_out, L0_ffn_Wg, L0_ffn_Wu, L0_ffn_Wd, L0_ffn_Wr, L0_ffn_temperature, L1_attn_Wq, L1_attn_bq, L1_attn_Wk, L1_attn_bk, L1_attn_Wv, L1_attn_bv, L1_attn_gamma, L1_ffn_Wq, L1_ffn_keys, L1_ffn_down_embed, L1_ffn_up_embed, L1_ffn_Wg, L1_ffn_Wu, L1_ffn_Wd):

    def _L0_attn_ref(x, W_in, conv_x_w, conv_x_b, conv_z_w, conv_z_b, W_xdbl, W_dt, inv_dt, D, W_out, b_out):
        import jax, jax.numpy as jnp
        import numpy as np
        import math
        D_MODEL = 128
        D_INNER = 256
        D_HALF = D_INNER // 2
        D_STATE = 16
        D_CONV = 4
        DT_RANK = 64
        B_SZ = 4
        L = 256

        def _dw_conv(x, w, b):
            y = jax.lax.conv_general_dilated(x, w, window_strides=(1,), padding='SAME', feature_group_count=x.shape[-1], dimension_numbers=('NWC', 'WIO', 'NWC'))
            return y + b

        def _selective_scan(u, delta, A, Bc, Cc, D):
            b, l, d = u.shape
            n = A.shape[1]

            def step(h, inp):
                d_t, u_t, B_t, C_t = inp
                dA = jnp.exp(d_t[..., None] * A)
                h = dA * h + (d_t * u_t)[..., None] * B_t[:, None, :]
                y = jnp.einsum('bdn,bn->bd', h, C_t)
                return (h, y)
            h0 = jnp.zeros((b, d, n), u.dtype)
            xs = (jnp.moveaxis(delta, 1, 0), jnp.moveaxis(u, 1, 0), jnp.moveaxis(Bc, 1, 0), jnp.moveaxis(Cc, 1, 0))
            _, ys = jax.lax.scan(step, h0, xs)
            return jnp.moveaxis(ys, 0, 1) + u * D
        xz = x @ W_in
        xs, z = jnp.split(xz, 2, axis=-1)
        A = -jnp.tile(jnp.arange(1, D_STATE + 1, dtype=jnp.float32), (D_HALF, 1))
        xs = jax.nn.silu(_dw_conv(xs, conv_x_w, conv_x_b))
        z = jax.nn.silu(_dw_conv(z, conv_z_w, conv_z_b))
        x_dbl = xs @ W_xdbl
        dt_low, Bc, Cc = jnp.split(x_dbl, [DT_RANK, DT_RANK + D_STATE], axis=-1)
        dt = dt_low @ W_dt + inv_dt
        delta = jax.nn.softplus(dt + inv_dt)
        y = _selective_scan(xs, delta, A, Bc, Cc, D)
        y = jnp.concatenate([y, z], axis=-1)
        return y @ W_out + b_out

    def _L0_ffn_ref(x, Wg, Wu, Wd, Wr, temperature):
        import jax, jax.numpy as jnp
        import numpy as np
        import math
        GOLDEN_CENTER = 1.0 / math.e
        GOLDEN_LOWER = 0.5 - math.log(4.0 / 3.0)
        GOLDEN_UPPER = 0.5
        B, T, D = (4, 256, 128)
        E = 8
        I = 512 // (E // 2)

        def _routing_weights(x, Wr, temperature):
            inh = jax.nn.sigmoid(x @ Wr / temperature)
            in_zone = (inh >= GOLDEN_LOWER) & (inh <= GOLDEN_UPPER)
            dist = jnp.abs(inh - GOLDEN_CENTER)
            w = jnp.exp(-dist / 0.1) * in_zone.astype(x.dtype)
            wsum = w.sum(axis=-1, keepdims=True)
            no_expert = wsum < 1e-08
            fb = jnp.exp(-dist / 0.3)
            _, top2 = jax.lax.top_k(fb, 2)
            fb_mask = jax.nn.one_hot(top2, E, dtype=x.dtype).sum(axis=-2)
            fb_w = fb * fb_mask
            fb_w = fb_w / jnp.clip(fb_w.sum(axis=-1, keepdims=True), 1e-08)
            w = jnp.where(no_expert, fb_w, w)
            wsum = w.sum(axis=-1, keepdims=True)
            return w / jnp.clip(wsum, 1e-08)
        weights = _routing_weights(x, Wr, temperature)
        gate = jnp.einsum('btd,edi->beti', x, Wg)
        up = jnp.einsum('btd,edi->beti', x, Wu)
        h = jax.nn.silu(gate) * up
        e_out = jnp.einsum('beti,eid->betd', h, Wd)
        out = jnp.einsum('bte,betd->btd', weights, e_out)
        return out

    def _L1_attn_ref(x_seq, Wq, bq, Wk, bk, Wv, bv, gamma):
        import jax, jax.numpy as jnp
        import numpy as np
        EPS = 1e-06
        B, S, D = x_seq.shape
        q = jax.nn.relu(jnp.einsum('bsd,ed->bse', x_seq, Wq) + bq)
        k = jax.nn.relu(jnp.einsum('bsd,ed->bse', x_seq, Wk) + bk)
        v = jnp.einsum('bsd,ed->bse', x_seq, Wv) + bv

        def step(carry, qkv):
            s, z = carry
            q_t, k_t, v_t = qkv
            s = gamma * s + jnp.einsum('bi,bj->bij', k_t, v_t)
            z = gamma * z + k_t
            num = jnp.einsum('bi,bij->bj', q_t, s)
            denom = jnp.sum(q_t * z, axis=-1, keepdims=True) + EPS
            return ((s, z), num / denom)
        s0 = jnp.zeros((B, D, D), x_seq.dtype)
        z0 = jnp.zeros((B, D), x_seq.dtype)
        qkv = (jnp.swapaxes(q, 0, 1), jnp.swapaxes(k, 0, 1), jnp.swapaxes(v, 0, 1))
        _, ys = jax.lax.scan(step, (s0, z0), qkv)
        return jnp.swapaxes(ys, 0, 1)

    def _L1_ffn_ref(hidden_states, Wq, keys, down_embed, up_embed, Wg, Wu, Wd):
        import jax, jax.numpy as jnp
        import numpy as np
        HID = 128
        INTER = 512
        RDIM = 128
        HEADS = 4
        NUM_EXPERTS = 2048
        NUM_KEYS = 128
        TOPK = 8
        B, T = (2, 256)
        b, t, _ = hidden_states.shape
        q = hidden_states @ Wq.T
        q = q.reshape(b, t, 2, HEADS, RDIM // 2)
        q = jnp.transpose(q, (2, 0, 1, 3, 4))
        sim = jnp.einsum('pbthn,hkpn->pbthk', q, keys)
        sx, ix = jax.lax.top_k(sim[0], TOPK)
        sy, iy = jax.lax.top_k(sim[1], TOPK)
        all_scores = (sx[..., :, None] + sy[..., None, :]).reshape(b, t, HEADS, TOPK * TOPK)
        all_indices = (ix[..., :, None] * NUM_KEYS + iy[..., None, :]).reshape(b, t, HEADS, TOPK * TOPK)
        scores, pk = jax.lax.top_k(all_scores, TOPK)
        indices = jnp.take_along_axis(all_indices, pk, axis=-1)
        down = down_embed[indices]
        up = up_embed[indices]
        w = jnp.einsum('btd,bthkd->bthk', hidden_states, down)
        w = jax.nn.silu(w) * jax.nn.softmax(scores, axis=-1)
        experts_states = jnp.einsum('bthk,bthkd->btd', w, up)
        mlp = jax.nn.silu(hidden_states @ Wg.T) * (hidden_states @ Wu.T) @ Wd.T
        return mlp + experts_states
    x = L0_attn_x
    x = _layernorm(x + _L0_attn_ref(x, L0_attn_W_in, L0_attn_conv_x_w, L0_attn_conv_x_b, L0_attn_conv_z_w, L0_attn_conv_z_b, L0_attn_W_xdbl, L0_attn_W_dt, L0_attn_inv_dt, L0_attn_D, L0_attn_W_out, L0_attn_b_out), axis=-1)
    x = _layernorm(x + _L0_ffn_ref(x, L0_ffn_Wg, L0_ffn_Wu, L0_ffn_Wd, L0_ffn_Wr, L0_ffn_temperature), axis=-1)
    x = _layernorm(x + _L1_attn_ref(x, L1_attn_Wq, L1_attn_bq, L1_attn_Wk, L1_attn_bk, L1_attn_Wv, L1_attn_bv, L1_attn_gamma), axis=-1)
    x = _layernorm(x + _L1_ffn_ref(x, L1_ffn_Wq, L1_ffn_keys, L1_ffn_down_embed, L1_ffn_up_embed, L1_ffn_Wg, L1_ffn_Wu, L1_ffn_Wd), axis=-1)
    return x

_drawn_inputs = setup_inputs


def setup_inputs(seed=0):
    import zlib

    import numpy as np

    out = dict(_drawn_inputs(seed))
    spreads = {'L0_attn_conv_x_b': (0.0, 0.1),
     'L0_attn_conv_z_b': (0.0, 0.1),
     'L0_attn_D': (1.0, 0.2),
     'L0_attn_b_out': (0.0, 0.1)}
    factors = {'L0_attn_W_dt': 3.435,
     'L1_attn_bq': 62.566,
     'L1_attn_bk': 64.0,
     'L1_attn_bv': 4.996,
     'L1_ffn_Wq': 8.0,
     'L1_ffn_keys': 8.0,
     'L1_ffn_down_embed': 8.0,
     'L1_ffn_up_embed': 8.0}
    for name, (base, spread) in spreads.items():
        noise = np.random.default_rng([zlib.crc32(name.encode()), seed]).standard_normal(out[name].shape)
        drawn = base * np.exp(spread * noise) if base else spread * noise
        out[name] = jnp.asarray(drawn.astype(out[name].dtype))
    for name, factor in factors.items():
        out[name] = (out[name] * factor).astype(out[name].dtype)
    return out
```

```python
from contextlib import ExitStack

import numpy as np

import concourse.bass as bass
from concourse import mybir

F32 = mybir.dt.float32
F16 = mybir.dt.float16
BF16 = mybir.dt.bfloat16
U32 = mybir.dt.uint32
ALU = mybir.AluOpType
ACT = mybir.ActivationFunctionType
AX = mybir.AxisListType.X

P = 128
T = 256
H = T // P
TAPS = 4
STATES = 16
RANK = 64
EXPERTS = 8
HEADS = 4
KEYS = 128
TOPK = 8
SLOTS = HEADS * TOPK
TABLE = 2048
BLOCKS = TABLE // P
INTER = 512
GROUPS = 32
QUADS = P // GROUPS
RING = 4
LN_EPS = 1e-5
ATTN_EPS = 1e-6
GOLDEN_CENTER = float(1.0 / np.e)
GOLDEN_LOWER = float(0.5 - np.log(4.0 / 3.0))
GOLDEN_UPPER = 0.5


VEC_REST = 147


class Signal:

    def __init__(self, sem, per=1):
        self.sem, self.per = sem, per

    def at(self, b, k=None):
        return b * self.per + (self.per if k is None else k)


class Steps:

    def __init__(self, sem, per):
        self.sem, self.per = sem, per

    def begin(self, b):
        self.b, self.n = b, 0

    def step(self):
        self.n += 1
        return 1

    def count(self):
        return self.b * self.per + self.n

    def end(self):
        assert self.n == self.per, (self.n, self.per)


def weave(steps, mixer, rest):
    if mixer is not None:
        steps["mixer_in"](mixer)
    if rest is not None:
        steps["moe_head"](rest)
    if mixer is not None:
        steps["mixer_project"](mixer)
    for e in range(EXPERTS):
        if rest is not None:
            steps["moe_expert"](rest, e)
        if mixer is not None:
            steps["mixer_scan"](mixer, e)
    if rest is not None:
        steps["moe_tail"](rest)
    if mixer is not None:
        steps["mixer_out"](mixer)
    if rest is not None:
        steps["attention"](rest)
        steps["peer"](rest)


def build(nc, d, out):
    NB = d["x"].shape[0]
    with ExitStack() as ctx:
        def sb(name, shape, dt=F32):
            return ctx.enter_context(nc.sbuf_tensor(name, [P] + shape, dt))

        def bank(name, n=1):
            return ctx.enter_context(nc.psum_tensor(name, [P, 512 * n], F32))

        def signal(name, per=1):
            return Signal(ctx.enter_context(nc.semaphore(name)), per)

        ident = sb("ident", [P])
        ones = sb("ones", [P])
        w_in = sb("w_in", [2 * P])
        w_conv = sb("w_conv", [TAPS, 2 * P])
        conv_b = sb("conv_b", [2])
        w_dt_low = sb("w_dt_low", [RANK])
        w_bc3 = sb("w_bc3", [3, 2 * STATES])
        w_dt = sb("w_dt", [P])
        inv_dt = sb("inv_dt", [1])
        inv_dt2 = sb("inv_dt2", [1])
        skip_d = sb("skip_d", [1])
        w_out = sb("w_out", [2, P])
        b_out = sb("b_out", [P])
        pick_state = sb("pick_state", [2 * STATES, P], BF16)
        moe_g = sb("moe_g", [EXPERTS, P])
        moe_u = sb("moe_u", [EXPERTS, P])
        moe_d = sb("moe_d", [EXPERTS, P])
        w_route = sb("w_route", [EXPERTS])
        temperature = sb("temperature", [1])
        neg_inv_temp = sb("neg_inv_temp", [1])
        iota8 = sb("iota8", [8])
        wq = sb("wq", [P])
        wk = sb("wk", [P])
        wv = sb("wv", [P])
        bq = sb("bq", [1])
        bk = sb("bk", [1])
        bv = sb("bv", [P])
        gamma = sb("gamma", [1])
        decay = sb("decay", [T + P])
        diagonal = sb("diagonal", [T])
        key_map = sb("key_map", [2 * HEADS, KEYS])
        w_down = sb("w_down", [TABLE])
        w_up = sb("w_up", [BLOCKS, P])
        mlp_g = sb("mlp_g", [INTER])
        mlp_u = sb("mlp_u", [INTER])
        mlp_d = sb("mlp_d", [INTER // P, P])
        expert_lo = sb("expert_lo", [P, GROUPS], F16)
        expert_hi = sb("expert_hi", [QUADS * BLOCKS, GROUPS], F16)
        quad_base = sb("quad_base", [1])
        eps_ln = sb("eps_ln", [1])

        x_in = sb("x_in", [H, P])
        x_t = sb("x_t", [T + TAPS - 1])
        xs = sb("xs", [T])
        z = sb("z", [T])
        dt_low = sb("dt_low", [T])
        bc_hi = sb("bc_hi", [T], BF16)
        bc_rest = sb("bc_rest", [T])
        bc_mid = sb("bc_mid", [T], BF16)
        bc_parts = sb("bc_parts", [T], BF16)
        dt_sum = sb("dt_sum", [T])
        dt_abs = sb("dt_abs", [T])
        dt_exp = sb("dt_exp", [T])
        dt_log = sb("dt_log", [T])
        dt_pos = sb("dt_pos", [T])
        delta = sb("delta", [T])
        du = sb("du", [T])
        dA = sb("dA", [STATES, T])
        dBu = sb("dBu", [2 * T])
        state = sb("state", [2 * T])
        state_c = sb("state_c", [RING, 2 * T])
        y_pair = sb("y_pair", [2 * T])
        y_sum = sb("y_sum", [T])
        y = sb("y", [T])

        r_m = sb("r_m", [H, P])
        st_m = sb("st_m", [H, 6])
        mv_m = sb("mv_m", [H, 2])
        ln_m = sb("ln_m", [H])
        rs_m = sb("rs_m", [H])
        r_r = sb("r_r", [H, P])
        st_r = sb("st_r", [H, 6])
        mv_r = sb("mv_r", [H, 2])
        ln_r = sb("ln_r", [H])
        rs_r = sb("rs_r", [H])

        x1 = sb("x1", [H, P])
        x2 = sb("x2", [H, P])
        x3 = sb("x3", [H, P])
        x4 = sb("x4", [H, P])
        x1_t = sb("x1_t", [T])
        x2_t = sb("x2_t", [T])
        x3_t = sb("x3_t", [T])

        r_exp = sb("r_exp", [H, 8])
        r_exp1 = sb("r_exp1", [H, 8])
        inh = sb("inh", [H, 8])
        off_center = sb("off_center", [H, 8])
        dist = sb("dist", [H, 8])
        near = sb("near", [H, 8])
        fall = sb("fall", [H, 8])
        in_zone = sb("in_zone", [H, 8])
        zone_w = sb("zone_w", [H, 8])
        zone_sum = sb("zone_sum", [H])
        none_in = sb("none_in", [H])
        fall8 = sb("fall8", [H, 8])
        fall_i = sb("fall_i", [H, 8], U32)
        fall_if = sb("fall_if", [H, 8])
        first = sb("first", [H, 8])
        two = sb("two", [H, 8])
        fb_w = sb("fb_w", [H, 8])
        fb_sum = sb("fb_sum", [H])
        fb_rec = sb("fb_rec", [H])
        fb_n = sb("fb_n", [H, 8])
        fb_d = sb("fb_d", [H, 8])
        w_all = sb("w_all", [H, 8])
        w_sum = sb("w_sum", [H])
        w_rec = sb("w_rec", [H])
        w_tok = sb("w_tok", [H, 8])
        e_silu = sb("e_silu", [2, T])
        e_h = sb("e_h", [2, T])
        e_acc = sb("e_acc", [H, P])

        q_t = sb("q_t", [T])
        k_t = sb("k_t", [T])
        v_1 = sb("v_1", [H, P + 1])
        probs = sb("probs", [T + P])
        den = sb("den", [H])
        den_r = sb("den_r", [H])

        sim = sb("sim", [H, 2 * HEADS, KEYS])
        top = sb("top", [2 * HEADS, TOPK])
        top_i = sb("top_i", [2 * HEADS, TOPK], U32)
        top_if = sb("top_if", [2 * HEADS, TOPK])
        pair = sb("pair", [HEADS, TOPK * TOPK])
        score = sb("score", [HEADS, TOPK])
        pair_i = sb("pair_i", [HEADS, TOPK], U32)
        rank_x = sb("rank_x", [SLOTS], U32)
        rank_y = sb("rank_y", [SLOTS], U32)
        rank_hot = sb("rank_hot", [SLOTS, TOPK])
        rank_val = sb("rank_val", [SLOTS, TOPK])
        slot_x = sb("slot_x", [SLOTS])
        slot_y = sb("slot_y", [SLOTS])
        slot_e = sb("slot_e", [SLOTS])
        slot_u = sb("slot_u", [SLOTS], U32)
        slot_hi = sb("slot_hi", [SLOTS], U32)
        slot_lo = sb("slot_lo", [SLOTS], U32)
        slot = sb("slot", [3, SLOTS])
        slot_t = sb("slot_t", [3, GROUPS])
        score_d = sb("score_d", [HEADS, TOPK])
        score_e = sb("score_e", [H, HEADS, TOPK])
        score_s = sb("score_s", [HEADS])
        score_r = sb("score_r", [HEADS])
        hi_16 = sb("hi_16", [GROUPS], F16)
        lo_16 = sb("lo_16", [GROUPS], F16)
        p_hi = sb("p_hi", [GROUPS], F16)
        p_lo = sb("p_lo", [GROUPS], F16)
        hot_lo = sb("hot_lo", [P, GROUPS], F16)
        hot_hi = sb("hot_hi", [QUADS * BLOCKS, GROUPS], F16)
        pick_hi = sb("pick_hi", [QUADS * BLOCKS, GROUPS], F16)
        pick_lo = sb("pick_lo", [QUADS * BLOCKS, GROUPS], F16)
        dots = sb("dots", [BLOCKS, T])
        coef = sb("coef", [BLOCKS, P])
        m_silu = sb("m_silu", [2, T])
        m_h = sb("m_h", [INTER // P, T])

        taps = state_c[:, 0:2].rearrange("p a (b n) -> p (a b) n", b=2)
        peer_q = coef[:, 0:2 * HEADS]
        peer_keys = coef[:, 2 * HEADS:4 * HEADS]
        gamma_row = m_h[:, 0]

        mix_ps = bank("mix_ps")
        b_ps = bank("b_ps")
        c_ps = bank("c_ps")
        work = [bank("work_0"), bank("work_1")]
        head_ps = bank("head_ps")
        acc = [bank("acc_0"), bank("acc_1")]

        loads = {}
        consts_pool = signal("consts_pool", 2)
        consts_vec = signal("consts_vec", 9)
        made = signal("made", 5)
        map_ps = signal("map_ps", 2)
        map_copied = signal("map_copied", 2)
        passed = signal("passed")
        x_loaded = signal("x_loaded", 16)
        x_transposed = signal("x_transposed")
        x_t_ready = signal("x_t_ready")
        conv_done = signal("conv_done")
        xz_ready = signal("xz_ready", 2)
        proj_done = signal("proj_done")
        dt_low_ready = signal("dt_low_ready")
        bc_hi_ready = signal("bc_hi_ready", 2)
        bc_rest_ready = signal("bc_rest_ready")
        bc_parts_ready = signal("bc_parts_ready", 2)
        dt_done = signal("dt_done")
        dt_sum_ready = signal("dt_sum_ready")
        dt_log_ready = signal("dt_log_ready")
        delta_ready = signal("delta_ready")
        dA_ready = signal("dA_ready", STATES)
        b_ready = signal("b_ready", STATES // 2)
        c_ready = signal("c_ready", STATES // 2)
        b_used = signal("b_used", STATES // 2)
        c_used = signal("c_used", STATES // 2)
        scanned = signal("scanned", STATES // 2)
        pair_added = signal("pair_added", STATES // 2 - 1)
        y_summed = signal("y_summed")
        y_ready = signal("y_ready")
        mix_done = signal("mix_done")
        mix_res = signal("mix_res")
        mix_var = signal("mix_var")
        mix_rstd = signal("mix_rstd")
        x1_ready = signal("x1_ready")

        x1_transposed = signal("x1_transposed")
        x1_t_ready = signal("x1_t_ready")
        logits_done = signal("logits_done")
        r_exp_ready = signal("r_exp_ready")
        dist_ready = signal("dist_ready")
        fall_ready = signal("fall_ready", 2)
        weights_ready = signal("weights_ready")
        gu_done = signal("gu_done", EXPERTS)
        e_silu_ready = signal("e_silu_ready", EXPERTS)
        e_h_ready = signal("e_h_ready", EXPERTS)
        down_done = signal("down_done", EXPERTS)
        down_used = signal("down_used", EXPERTS)
        var_ready = signal("var_ready", 3)
        rstd_ready = signal("rstd_ready", 3)
        x2_ready = signal("x2_ready")
        x2_transposed = signal("x2_transposed")
        x2_t_ready = signal("x2_t_ready")
        qkv_done = signal("qkv_done")
        qkv_ready = signal("qkv_ready", 3)
        scores_done = signal("scores_done")
        probs_ready = signal("probs_ready")
        attn_done = signal("attn_done")
        attn_read = signal("attn_read")
        x3_ready = signal("x3_ready")
        x3_transposed = signal("x3_transposed")
        x3_t_ready = signal("x3_t_ready")
        sim_done = signal("sim_done", 2 * H)
        sim_ready = signal("sim_ready", 2 * H)
        dots_done = signal("dots_done", BLOCKS // 2)
        dots_ready = signal("dots_ready", BLOCKS // 2)
        mlp_done = signal("mlp_done", INTER // P)
        m_silu_ready = signal("m_silu_ready", INTER // P)
        m_h_ready = signal("m_h_ready", INTER // P)
        score_d_ready = signal("score_d_ready", H)
        score_e_ready = signal("score_e_ready", H)
        picks_ready = signal("picks_ready", H)
        spread_done = signal("spread_done", H * QUADS)
        coef_ready = signal("coef_ready", H * QUADS)
        coef_read = signal("coef_read")
        peer_done = signal("peer_done")
        peer_read = signal("peer_read")
        x4_ready = signal("x4_ready")
        stored = signal("stored", 16)

        vec_m = Steps(ctx.enter_context(nc.semaphore("vector_mixer_steps")), 6)
        vec_r = Steps(ctx.enter_context(nc.semaphore("vector_rest_steps")), VEC_REST)
        act_m = Steps(ctx.enter_context(nc.semaphore("scalar_mixer_steps")), 3)
        act_r = Steps(ctx.enter_context(nc.semaphore("scalar_rest_steps")), 3)

        def load(eng, group, pairs):
            sem = ctx.enter_context(nc.semaphore("loaded_" + group))
            for dst, src in pairs:
                eng.dma_start(dst, src).then_inc(sem, 16)
            loads[group] = (sem, 16 * len(pairs))

        def row(v, width, start=0):
            return v[start:start + width].partition_broadcast(P)

        def column(v):
            return v.rearrange("(p a) -> p a", a=1)

        block = ctx.enter_context(nc.Block())

        @block.sync
        def _(sp):
            load(sp, "mixer", [
                (ident[:], d["ident"]), (w_in[:], d["W_in"]),
                (taps[:, :, 0:P], d["conv_x_w"].partition_broadcast(P)),
                (taps[:, :, P:2 * P], d["conv_z_w"].partition_broadcast(P)),
                (conv_b[:, 0:1], column(d["conv_x_b"])), (conv_b[:, 1:2], column(d["conv_z_b"])),
                (w_dt_low[:], d["W_xdbl"][:, 0:RANK]),
                (w_bc3[:, 0], d["W_xdbl"][:, RANK:RANK + 2 * STATES]),
                (w_bc3[:, 1], d["W_xdbl"][:, RANK:RANK + 2 * STATES]),
                (w_bc3[:, 2], d["W_xdbl"][:, RANK:RANK + 2 * STATES]),
                (w_dt[0:RANK], d["W_dt"]), (inv_dt[:], column(d["inv_dt"])),
                (skip_d[:], column(d["D"])),
                (w_out[:], d["W_out"].rearrange("(a p) n -> p a n", p=P)),
                (b_out[0:1], d["b_out"].rearrange("(a n) -> a n", a=1)),
                (pick_state[0:6 * STATES], d["pick_state"]),
            ])
            load(sp, "attention", [
                (wq[:], d["A_Wq_t"]), (wk[:], d["A_Wk_t"]), (wv[:], d["A_Wv_t"]),
                (bq[:], column(d["bq"])), (bk[:], column(d["bk"])),
                (bv[0:1], d["bv"].rearrange("(a n) -> a n", a=1)),
                (gamma[:], row(d["gamma"], 1)), (diagonal[:], d["diagonal"]),
            ])
            load(sp, "moe", [
                (moe_g[:], d["moe_Wg"].rearrange("e p i -> p e i")),
                (moe_u[:], d["moe_Wu"].rearrange("e p i -> p e i")),
                (moe_d[:], d["moe_Wd"].rearrange("e p i -> p e i")),
                (w_route[:], d["Wr"]), (temperature[:], row(d["temperature"], 1)),
                (iota8[:], d["iota8"]),
            ])

            load(sp, "peer", [
                (peer_q[0:RANK], d["Wq_p"].rearrange("c n k -> n c k")),
                (peer_keys[0:RANK], d["keys_p"].rearrange("c n k -> n c k")),
                (w_down[:], d["down_t"]),
                (w_up[:], d["up_embed"].rearrange("(a p) n -> p a n", p=P)),
                (mlp_g[:], d["M_Wg_t"]), (mlp_u[:], d["M_Wu_t"]),
                (mlp_d[:], d["M_Wd_t"].rearrange("(a p) n -> p a n", p=P)),
                (expert_lo[:], d["expert_lo"]), (expert_hi[:], d["expert_hi"]),
                (quad_base[:], d["quad_base"]),
            ])

            sp.dma_start(x_in[:], d["x"][0].rearrange("(h p) n -> p h n", p=P)).then_inc(x_loaded.sem, 16)
            with sp.Fori(1, NB) as b:
                sp.wait_ge(mix_res.sem, mix_res.at(b, 0))
                sp.dma_start(x_in[:], d["x"][b].rearrange("(h p) n -> p h n", p=P)).then_inc(x_loaded.sem, 16)

        @block.gpsimd
        def _(pool):
            pool.memset(ones[:], 1.0).then_inc(consts_pool.sem, 1)
            pool.memset(v_1[:], 1.0).then_inc(consts_pool.sem, 1)

            def mixer_scan(b, c):
                if c == 0:
                    return
                pool.wait_ge(c_used.sem, c_used.at(b, c + 1))
                if c == 1:
                    pool.wait_ge(y_summed.sem, y_summed.at(b, 0))
                    pool.tensor_tensor(y_pair[:], state_c[:, 0], state_c[:, 1], ALU.add).then_inc(pair_added.sem, 1)
                else:
                    pool.wait_ge(pair_added.sem, pair_added.at(b, c - 1))
                    pool.tensor_tensor(y_pair[:], y_pair[:], state_c[:, c % RING], ALU.add)\
                        .then_inc(pair_added.sem, 1)
                if c == STATES // 2 - 1:
                    pool.wait_ge(pair_added.sem, pair_added.at(b))
                    pool.wait_ge(y_ready.sem, y_ready.at(b, 0))
                    pool.tensor_tensor(y_sum[:], y_pair[:, 0:T], y_pair[:, T:2 * T], ALU.add).then_inc(y_summed.sem, 1)

            def peer(b):
                pool.wait_ge(x4_ready.sem, x4_ready.at(b))
                pool.dma_start(out[b].rearrange("(h p) n -> p h n", p=P), x4[:]).then_inc(stored.sem, 16)

            def nothing(*_):
                pass

            steps = {k: nothing for k in ("mixer_in", "moe_head", "mixer_project", "moe_expert", "moe_tail",
                                          "mixer_out", "attention")}
            steps.update(mixer_scan=mixer_scan, peer=peer)
            weave(steps, 0, None)
            weave(steps, 1, 0)
            with pool.Fori(1, NB - 1) as i:
                weave(steps, i + 1, i)
            weave(steps, None, NB - 1)
            pool.wait_ge(stored.sem, 16 * NB)

        @block.scalar
        def _(act):
            def copy(dst, src):
                return act.activation(dst, src, ACT.Copy)

            def rstd(own, var, ln_t, rs_t, ready):
                act.activation(ln_t[:], var, ACT.Ln, bias=eps_ln[:]).then_inc(own.sem, own.step())
                act.wait_ge(own.sem, own.count())
                act.activation(rs_t[:], ln_t[:], ACT.Exp, scale=-0.5).then_inc(ready.sem, 1)

            def mixer_in(b):
                act.wait_ge(x_transposed.sem, x_transposed.at(b))
                copy(x_t[:, 1:T + 1], mix_ps[:, 0:T]).then_inc(x_t_ready.sem, 1)
                for half, dst in ((0, xs), (1, z)):
                    act.wait_ge(conv_done.sem, conv_done.at(b))
                    act.activation(dst[:], mix_ps[:, half * T:(half + 1) * T], ACT.Silu,
                                   bias=conv_b[:, half:half + 1]).then_inc(xz_ready.sem, 1)

            def mixer_project(b):
                act_m.begin(b)
                act.wait_ge(proj_done.sem, proj_done.at(b))
                copy(dt_low[0:RANK], mix_ps[0:RANK, T:2 * T]).then_inc(dt_low_ready.sem, 1)
                copy(bc_hi[0:96], mix_ps[0:96, 0:T]).then_inc(bc_hi_ready.sem, 1)
                act.wait_ge(c_ready.sem, c_ready.at(b, 0))
                copy(bc_parts[0:32], mix_ps[0:32, 0:T]).then_inc(bc_hi_ready.sem, 1)
                act.wait_ge(dt_done.sem, dt_done.at(b))
                act.activation(dt_sum[:], mix_ps[:, 0:T], ACT.Identity, bias=inv_dt2[:]).then_inc(dt_sum_ready.sem, 1)
                act.wait_ge(dt_sum_ready.sem, dt_sum_ready.at(b))
                act.activation(dt_abs[:], dt_sum[:], ACT.Abs).then_inc(act_m.sem, act_m.step())
                act.wait_ge(act_m.sem, act_m.count())
                act.activation(dt_exp[:], dt_abs[:], ACT.Exp, scale=-1.0).then_inc(act_m.sem, act_m.step())
                act.wait_ge(act_m.sem, act_m.count())
                act.activation(dt_log[:], dt_exp[:], ACT.Ln, bias=1.0).then_inc(dt_log_ready.sem, 1)
                act.wait_ge(delta_ready.sem, delta_ready.at(b))
                act.wait_ge(scanned.sem, scanned.at(b, 0))
                for n in range(STATES):
                    act.activation(dA[:, n, 1:T], delta[:, 1:T], ACT.Exp, scale=-float(n + 1)).then_inc(dA_ready.sem, 1)

            def mixer_out(b):
                act.wait_ge(mix_var.sem, mix_var.at(b))
                rstd(act_m, mv_m[:, :, 1], ln_m, rs_m, mix_rstd)
                act_m.end()

            def moe_head(b):
                act_r.begin(b)
                act.wait_ge(x1_transposed.sem, x1_transposed.at(b))
                copy(x1_t[:], head_ps[:, 0:T]).then_inc(x1_t_ready.sem, 1)
                act.wait_ge(logits_done.sem, logits_done.at(b))
                act.activation(r_exp[:].rearrange("p h e -> p (h e)"), head_ps[:, T:T + 8 * H], ACT.Exp,
                               scale=neg_inv_temp[:]).then_inc(r_exp_ready.sem, 1)
                act.wait_ge(dist_ready.sem, dist_ready.at(b))
                act.activation(near[:], dist[:], ACT.Exp, scale=-1.0 / 0.1).then_inc(fall_ready.sem, 1)
                act.activation(fall[:], dist[:], ACT.Exp, scale=-1.0 / 0.3).then_inc(fall_ready.sem, 1)

            def moe_expert(b, e):
                act.wait_ge(gu_done.sem, gu_done.at(b, e + 1))
                act.wait_ge(e_h_ready.sem, e_h_ready.at(b, max(e - 1, 0)))
                act.activation(e_silu[:, e % 2], work[e % 2][:, 0:T], ACT.Silu).then_inc(e_silu_ready.sem, 1)

            def moe_tail(b):
                act.wait_ge(var_ready.sem, var_ready.at(b, 1))
                rstd(act_r, mv_r[:, :, 1], ln_r, rs_r, rstd_ready)

            def attention(b):
                act.wait_ge(x2_transposed.sem, x2_transposed.at(b))
                copy(x2_t[:], head_ps[:, 0:T]).then_inc(x2_t_ready.sem, 1)
                act.wait_ge(qkv_done.sem, qkv_done.at(b))
                act.activation(q_t[:], work[0][:, 0:T], ACT.Relu, bias=bq[:]).then_inc(qkv_ready.sem, 1)
                act.activation(k_t[:], work[0][:, T:2 * T], ACT.Relu, bias=bk[:]).then_inc(qkv_ready.sem, 1)
                copy(v_1[:, :, 0:P], work[1][:, 0:T].rearrange("p (h n) -> p h n", h=H)).then_inc(qkv_ready.sem, 1)
                act.wait_ge(var_ready.sem, var_ready.at(b, 2))
                rstd(act_r, mv_r[:, :, 1], ln_r, rs_r, rstd_ready)

            def peer(b):
                act.wait_ge(x3_transposed.sem, x3_transposed.at(b))
                copy(x3_t[:], head_ps[:, 0:T]).then_inc(x3_t_ready.sem, 1)
                for h in range(H):
                    for half in range(2):
                        act.wait_ge(sim_done.sem, sim_done.at(b, 2 * h + half + 1))
                        copy(sim[:, h, HEADS * half:HEADS * (half + 1)],
                             work[half][:].rearrange("p (c k) -> p c k", c=HEADS)).then_inc(sim_ready.sem, 1)
                for c in range(BLOCKS // 2):
                    act.wait_ge(dots_done.sem, dots_done.at(b, c + 1))
                    if c == 0:
                        act.wait_ge(coef_ready.sem, coef_ready.at(b, 0))
                    act.activation(dots[:, 2 * c:2 * c + 2], work[c % 2][:].rearrange("p (a t) -> p a t", a=2),
                                   ACT.Silu).then_inc(dots_ready.sem, 1)
                for j in range(INTER // P):
                    act.wait_ge(mlp_done.sem, mlp_done.at(b, j + 1))
                    act.wait_ge(m_h_ready.sem, m_h_ready.at(b, max(j - 1, 0)))
                    act.activation(m_silu[:, j % 2], work[j % 2][:, 0:T], ACT.Silu).then_inc(m_silu_ready.sem, 1)
                for h in range(H):
                    act.wait_ge(score_d_ready.sem, score_d_ready.at(b, h + 1))
                    act.activation(score_e[:, h], score_d[:], ACT.Exp).then_inc(score_e_ready.sem, 1)
                act.wait_ge(var_ready.sem, var_ready.at(b, 3))
                rstd(act_r, mv_r[:, :, 1], ln_r, rs_r, rstd_ready)
                act_r.end()

            def nothing(*_):
                pass

            act.wait_ge(*loads["mixer"])
            act.wait_ge(consts_vec.sem, consts_vec.at(0))
            steps = dict(mixer_in=mixer_in, moe_head=moe_head, mixer_project=mixer_project, moe_expert=moe_expert,
                         mixer_scan=nothing, moe_tail=moe_tail, mixer_out=mixer_out, attention=attention, peer=peer)
            weave(steps, 0, None)
            act.wait_ge(*loads["attention"])
            act.wait_ge(map_ps.sem, map_ps.at(0))
            copy(key_map[:, 0:HEADS], acc[0][:].rearrange("p (c k) -> p c k", c=HEADS)).then_inc(map_copied.sem, 1)
            copy(key_map[:, HEADS:2 * HEADS], acc[1][:].rearrange("p (c k) -> p c k", c=HEADS))\
                .then_inc(map_copied.sem, 1)
            act.wait_ge(made.sem, made.at(0))
            act.wait_ge(*loads["moe"])
            weave(steps, 1, 0)
            with act.Fori(1, NB - 1) as i:
                weave(steps, i + 1, i)
            weave(steps, None, NB - 1)

        @block.tensor
        def _(pe):
            def mm(dst, lhs, rhs, start=True, stop=True):
                return pe.matmul(dst, lhs, rhs, start=start, stop=stop)

            def to_columns(dst, x):
                for h in range(H):
                    last = pe.transpose(dst[:, h * P:(h + 1) * P], x[:, h], ident[:])
                return last

            def mixer_in(b):
                pe.wait_ge(x_loaded.sem, x_loaded.at(b))
                pe.wait_ge(mix_res.sem, mix_res.at(b, 0))
                to_columns(mix_ps, x_in).then_inc(x_transposed.sem, 1)
                pe.wait_ge(x_t_ready.sem, x_t_ready.at(b))
                for half in range(2):
                    for k in range(TAPS):
                        last = mm(mix_ps[:, half * T:(half + 1) * T], w_conv[:, k, half * P:(half + 1) * P],
                                  x_t[:, k:k + T], start=k == 0, stop=k == TAPS - 1)
                last.then_inc(conv_done.sem, 1)

            def mixer_project(b):
                pe.wait_ge(xz_ready.sem, xz_ready.at(b))
                mm(mix_ps[0:96, 0:T], w_bc3[:].rearrange("p a n -> p (a n)"), xs[:])
                mm(mix_ps[0:RANK, T:2 * T], w_dt_low[:], xs[:]).then_inc(proj_done.sem, 1)
                pe.wait_ge(dt_low_ready.sem, dt_low_ready.at(b))
                pe.wait_ge(bc_hi_ready.sem, bc_hi_ready.at(b))
                pe.wait_ge(bc_rest_ready.sem, bc_rest_ready.at(b))
                mm(mix_ps[:, 0:T], w_dt[0:RANK], dt_low[0:RANK]).then_inc(dt_done.sem, 1)

            def mixer_scan(b, c):
                if c == 0:
                    pe.wait_ge(bc_parts_ready.sem, bc_parts_ready.at(b))
                pe.wait_ge(b_used.sem, b_used.at(b, c))
                for n in range(2):
                    last = mm(b_ps[:, n * T:(n + 1) * T], pick_state[0:96, 2 * c + n], bc_parts[0:96])
                last.then_inc(b_ready.sem, 1)
                pe.wait_ge(c_used.sem, c_used.at(b, c))
                for n in range(2):
                    last = mm(c_ps[:, n * T:(n + 1) * T], pick_state[0:96, STATES + 2 * c + n], bc_parts[0:96])
                last.then_inc(c_ready.sem, 1)

            def mixer_out(b):
                pe.wait_ge(y_ready.sem, y_ready.at(b))
                for h in range(H):
                    at = mix_ps[:, h * P:(h + 1) * P]
                    mm(at, y[:, h * P:(h + 1) * P], w_out[:, 0], stop=False)
                    mm(at, z[:, h * P:(h + 1) * P], w_out[:, 1], start=False, stop=False)
                    last = mm(at, ones[0:1], b_out[0:1], start=False)
                last.then_inc(mix_done.sem, 1)

            def moe_head(b):
                pe.wait_ge(x1_ready.sem, x1_ready.at(b))
                pe.wait_ge(peer_read.sem, peer_read.at(b, 0))
                to_columns(head_ps, x1).then_inc(x1_transposed.sem, 1)
                pe.wait_ge(x1_t_ready.sem, x1_t_ready.at(b))
                for h in range(H):
                    last = mm(head_ps[:, T + 8 * h:T + 8 * h + 8], x1_t[:, h * P:(h + 1) * P], w_route[:])
                last.then_inc(logits_done.sem, 1)

            def expert_down(b, e):
                pe.wait_ge(e_h_ready.sem, e_h_ready.at(b, e + 1))
                if e < 2:
                    pe.wait_ge(coef_ready.sem, coef_ready.at(b, 0))
                else:
                    pe.wait_ge(down_used.sem, down_used.at(b, e - 1))
                for h in range(H):
                    last = mm(acc[e % 2][:, h * P:(h + 1) * P], e_h[:, e % 2, h * P:(h + 1) * P], moe_d[:, e])
                last.then_inc(down_done.sem, 1)

            def moe_expert(b, e):
                if e < 2:
                    pe.wait_ge(m_h_ready.sem, m_h_ready.at(b, 0))
                else:
                    pe.wait_ge(e_h_ready.sem, e_h_ready.at(b, e - 1))
                mm(work[e % 2][:, 0:T], moe_g[:, e], x1_t[:])
                mm(work[e % 2][:, T:2 * T], moe_u[:, e], x1_t[:]).then_inc(gu_done.sem, 1)
                if e:
                    expert_down(b, e - 1)

            def moe_tail(b):
                expert_down(b, EXPERTS - 1)

            def attention(b):
                pe.wait_ge(x2_ready.sem, x2_ready.at(b))
                to_columns(head_ps, x2).then_inc(x2_transposed.sem, 1)
                pe.wait_ge(x2_t_ready.sem, x2_t_ready.at(b))
                mm(work[0][:, 0:T], wq[:], x2_t[:])
                mm(work[0][:, T:2 * T], wk[:], x2_t[:])
                for h in range(H):
                    at = work[1][:, h * P:(h + 1) * P]
                    mm(at, x2_t[:, h * P:(h + 1) * P], wv[:], stop=False)
                    last = mm(at, ones[0:1], bv[0:1], start=False)
                last.then_inc(qkv_done.sem, 1)
                pe.wait_ge(qkv_ready.sem, qkv_ready.at(b))
                mm(acc[0][:, 0:T], k_t[:, 0:P], q_t[:])
                mm(acc[0][:, T:T + P], k_t[:, P:T], q_t[:, P:T]).then_inc(scores_done.sem, 1)
                pe.wait_ge(probs_ready.sem, probs_ready.at(b))
                mm(head_ps[:, 0:P + 1], probs[:, 0:P], v_1[:, 0])
                mm(head_ps[:, T:T + P + 1], probs[:, P:T], v_1[:, 0], stop=False)
                mm(head_ps[:, T:T + P + 1], probs[:, T:T + P], v_1[:, 1], start=False).then_inc(attn_done.sem, 1)

            def spread(b, h):
                pe.wait_ge(picks_ready.sem, picks_ready.at(b, h + 1))
                for q in range(QUADS):
                    n = h * QUADS + q
                    if n >= 2:
                        pe.wait_ge(coef_ready.sem, coef_ready.at(b, n - 1))
                    for g in range(GROUPS // QUADS):
                        at = acc[n % 2][:, g * 64:(g + 1) * 64]
                        token = q * (GROUPS // QUADS) + g
                        mm(at, hot_lo[:, :, token], pick_hi[:, :, token], stop=False)
                        last = mm(at, hot_lo[:, :, token], pick_lo[:, :, token], start=False)
                    last.then_inc(spread_done.sem, 1)

            def peer_sum(b, h):
                at = head_ps[:, h * P:(h + 1) * P]
                for j in range(INTER // P):
                    mm(at, m_h[:, j, h * P:(h + 1) * P], mlp_d[:, j], start=j == 0, stop=False)
                pe.wait_ge(coef_ready.sem, coef_ready.at(b, (h + 1) * QUADS))
                for a in range(BLOCKS):
                    last = mm(at, coef[:, a], w_up[:, a], start=False, stop=a == BLOCKS - 1)
                return last

            def peer(b):
                pe.wait_ge(x3_ready.sem, x3_ready.at(b))
                to_columns(head_ps, x3).then_inc(x3_transposed.sem, 1)
                pe.wait_ge(x3_t_ready.sem, x3_t_ready.at(b))
                for h in range(H):
                    for half in range(2):
                        n = 2 * h + half
                        if n >= 2:
                            pe.wait_ge(sim_ready.sem, sim_ready.at(b, n - 1))
                        mm(work[half][:], x3_t[:, h * P:(h + 1) * P],
                           key_map[:, HEADS * half:HEADS * (half + 1)].rearrange("p c k -> p (c k)"))\
                            .then_inc(sim_done.sem, 1)
                for c in range(BLOCKS // 2):
                    if c < 2:
                        pe.wait_ge(sim_ready.sem, sim_ready.at(b, c + 3))
                    else:
                        pe.wait_ge(dots_ready.sem, dots_ready.at(b, c - 1))
                    for a in (2 * c, 2 * c + 1):
                        last = mm(work[c % 2][:, (a % 2) * T:(a % 2 + 1) * T], w_down[:, a * P:(a + 1) * P], x3_t[:])
                    last.then_inc(dots_done.sem, 1)
                for j in range(INTER // P):
                    if j < 2:
                        pe.wait_ge(dots_ready.sem, dots_ready.at(b, BLOCKS // 2 - 1 + j))
                    else:
                        pe.wait_ge(m_h_ready.sem, m_h_ready.at(b, j - 1))
                    mm(work[j % 2][:, 0:T], mlp_g[:, j * P:(j + 1) * P], x3_t[:])
                    mm(work[j % 2][:, T:2 * T], mlp_u[:, j * P:(j + 1) * P], x3_t[:]).then_inc(mlp_done.sem, 1)
                spread(b, 0)
                pe.wait_ge(m_h_ready.sem, m_h_ready.at(b))
                peer_sum(b, 0).then_inc(coef_read.sem, 1)
                spread(b, 1)
                peer_sum(b, 1).then_inc(peer_done.sem, 1)

            pe.wait_ge(*loads["mixer"])
            pe.wait_ge(consts_vec.sem, consts_vec.at(0))
            pe.wait_ge(consts_pool.sem, consts_pool.at(0))
            steps = dict(mixer_in=mixer_in, moe_head=moe_head, mixer_project=mixer_project, moe_expert=moe_expert,
                         mixer_scan=mixer_scan, moe_tail=moe_tail, mixer_out=mixer_out, attention=attention,
                         peer=peer)
            weave(steps, 0, None)
            pe.wait_ge(*loads["moe"])
            pe.wait_ge(*loads["attention"])
            pe.wait_ge(*loads["peer"])
            for part in range(2):
                for c in range(HEADS):
                    n = part * HEADS + c
                    last = mm(acc[part][:, c * KEYS:(c + 1) * KEYS], peer_q[0:RANK, n], peer_keys[0:RANK, n])
                last.then_inc(map_ps.sem, 1)
            pe.wait_ge(map_copied.sem, map_copied.at(0))
            weave(steps, 1, 0)
            with pe.Fori(1, NB - 1) as i:
                weave(steps, i + 1, i)
            weave(steps, None, NB - 1)

        @block.vector
        def _(vec):
            def wide(x, n):
                return x.unsqueeze(len(x.shape)).broadcast_to(list(x.shape) + [n])

            def normalize_in(own, r, st, mv, ready):
                for h in range(H):
                    vec.bn_stats(st[:, h], r[:, h]).then_inc(own.sem, own.step())
                vec.wait_ge(own.sem, own.count())
                vec.sem_inc(passed.sem, 1)
                vec.bn_aggr(mv[:, 0], st[:, 0]).then_inc(own.sem, own.step())
                vec.bn_aggr(mv[:, 1], st[:, 1]).then_inc(ready.sem, 1)

            def normalize_out(r, mv, rs, x, ready):
                for h in range(H):
                    last = vec.tensor_scalar(x[:, h], r[:, h], mv[:, h, 0:1], rs[:, h:h + 1],
                                             ALU.subtract, ALU.mult)
                last.then_inc(ready.sem, 1)

            def mixer_project(b):
                own = vec_m
                own.begin(b)
                vec.wait_ge(bc_hi_ready.sem, bc_hi_ready.at(b))
                vec.tensor_tensor(bc_rest[0:96], mix_ps[0:96, 0:T], bc_hi[0:96], ALU.subtract).then_inc(bc_rest_ready.sem, 1)
                vec.wait_ge(bc_rest_ready.sem, bc_rest_ready.at(b))
                vec.tensor_copy(bc_mid[0:96], bc_rest[0:96]).then_inc(own.sem, own.step())
                vec.wait_ge(c_ready.sem, c_ready.at(b, 0))
                vec.tensor_copy(bc_parts[32:64], bc_rest[32:64]).then_inc(bc_parts_ready.sem, 1)
                vec.wait_ge(own.sem, own.count())
                vec.tensor_tensor(bc_parts[64:96], bc_rest[64:96], bc_mid[64:96], ALU.subtract).then_inc(bc_parts_ready.sem, 1)
                vec.wait_ge(dt_sum_ready.sem, dt_sum_ready.at(b))
                vec.tensor_scalar(dt_pos[:], dt_sum[:], 0.0, None, ALU.max).then_inc(own.sem, own.step())
                vec.wait_ge(own.sem, own.count())
                vec.wait_ge(dt_log_ready.sem, dt_log_ready.at(b))
                vec.tensor_tensor(delta[:], dt_pos[:], dt_log[:], ALU.add).then_inc(delta_ready.sem, 1)
                vec.wait_ge(delta_ready.sem, delta_ready.at(b))
                vec.tensor_tensor(du[:], delta[:], xs[:], ALU.mult).then_inc(own.sem, own.step())

            def mixer_scan(b, c):
                own = vec_m
                vec.wait_ge(b_ready.sem, b_ready.at(b, c + 1))
                if c == 0:
                    vec.wait_ge(own.sem, own.count())
                vec.tensor_tensor(dBu[:].rearrange("p (n t) -> p n t", n=2), b_ps[:].rearrange("p (n t) -> p n t", n=2),
                                  du[:].unsqueeze(1).broadcast_to([P, 2, T]), ALU.mult).then_inc(b_used.sem, 1)
                vec.wait_ge(dA_ready.sem, dA_ready.at(b, 2 * c + 2))
                vec.wait_ge(b_used.sem, b_used.at(b, c + 1))
                vec.tensor_tensor_scan(state[:], dA[:, 2 * c:2 * c + 2].rearrange("p n t -> p (n t)"), dBu[:], 0.0,
                                       ALU.mult, ALU.add).then_inc(scanned.sem, 1)
                vec.wait_ge(c_ready.sem, c_ready.at(b, c + 1))
                if c == 0:
                    vec.wait_ge(y_summed.sem, y_summed.at(b, 0))
                if c >= RING:
                    vec.wait_ge(pair_added.sem, pair_added.at(b, max(c - RING, 1)))
                vec.wait_ge(scanned.sem, scanned.at(b, c + 1))
                vec.tensor_tensor(state_c[:, c % RING], state[:], c_ps[:], ALU.mult).then_inc(c_used.sem, 1)

            def mixer_out(b):
                own = vec_m
                vec.wait_ge(y_summed.sem, y_summed.at(b))
                vec.scalar_tensor_tensor(y[:], xs[:], skip_d[:], y_sum[:], ALU.mult, ALU.add).then_inc(y_ready.sem, 1)
                vec.wait_ge(mix_done.sem, mix_done.at(b))
                vec.tensor_tensor(r_m[:].rearrange("p h n -> p (h n)"), mix_ps[:, 0:T],
                                  x_in[:].rearrange("p h n -> p (h n)"), ALU.add).then_inc(mix_res.sem, 1)
                vec.wait_ge(mix_res.sem, mix_res.at(b))
                normalize_in(own, r_m, st_m, mv_m, mix_var)
                vec.wait_ge(mix_rstd.sem, mix_rstd.at(b))
                normalize_out(r_m, mv_m, rs_m, x1, x1_ready)
                own.end()

            def moe_head(b):
                own = vec_r
                own.begin(b)

                vec.wait_ge(r_exp_ready.sem, r_exp_ready.at(b))
                vec.tensor_scalar(r_exp1[:], r_exp[:], 1.0, None, ALU.add).then_inc(own.sem, own.step())
                vec.wait_ge(own.sem, own.count())
                vec.reciprocal(inh[:], r_exp1[:]).then_inc(own.sem, own.step())
                vec.wait_ge(own.sem, own.count())
                vec.tensor_scalar(off_center[:], inh[:], GOLDEN_CENTER, None, ALU.subtract).then_inc(own.sem, own.step())
                vec.wait_ge(own.sem, own.count())
                vec.scalar_tensor_tensor(dist[:], off_center[:], -1.0, off_center[:], ALU.mult, ALU.max)\
                    .then_inc(dist_ready.sem, 1)
                vec.tensor_scalar(in_zone[:], inh[:], GOLDEN_LOWER, None, ALU.is_ge).then_inc(own.sem, own.step())
                vec.wait_ge(fall_ready.sem, fall_ready.at(b))
                vec.scalar_tensor_tensor(zone_w[:], inh[:], GOLDEN_UPPER, near[:], ALU.is_le, ALU.mult).then_inc(own.sem, own.step())
                vec.wait_ge(own.sem, own.count())
                vec.tensor_tensor(zone_w[:], zone_w[:], in_zone[:], ALU.mult).then_inc(own.sem, own.step())
                vec.wait_ge(own.sem, own.count())
                vec.tensor_reduce(zone_sum[:], zone_w[:], AX, ALU.add).then_inc(own.sem, own.step())
                for h in range(H):
                    vec.max(fall8[:, h], fall[:, h]).then_inc(own.sem, own.step())
                vec.wait_ge(own.sem, own.count())
                vec.sem_inc(passed.sem, 1)
                for h in range(H):
                    vec.max_index(fall_i[:, h], fall8[:, h], fall[:, h]).then_inc(own.sem, own.step())
                vec.wait_ge(own.sem, own.count())
                vec.tensor_copy(fall_if[:], fall_i[:]).then_inc(own.sem, own.step())
                vec.wait_ge(own.sem, own.count())
                numbers = iota8[:].unsqueeze(1).broadcast_to([P, H, 8])
                vec.tensor_tensor(first[:], numbers, fall_if[:, :, 0:1].broadcast_to([P, H, 8]), ALU.is_equal).then_inc(own.sem, own.step())
                vec.tensor_tensor(two[:], numbers, fall_if[:, :, 1:2].broadcast_to([P, H, 8]), ALU.is_equal).then_inc(own.sem, own.step())
                vec.wait_ge(own.sem, own.count())
                vec.tensor_tensor(two[:], two[:], first[:], ALU.add).then_inc(own.sem, own.step())
                vec.wait_ge(own.sem, own.count())
                vec.tensor_tensor(fb_w[:], fall[:], two[:], ALU.mult).then_inc(own.sem, own.step())
                vec.wait_ge(own.sem, own.count())
                vec.tensor_reduce(fb_sum[:], fb_w[:], AX, ALU.add).then_inc(own.sem, own.step())
                vec.wait_ge(own.sem, own.count())
                vec.tensor_scalar(fb_sum[:], fb_sum[:], 1e-8, None, ALU.max).then_inc(own.sem, own.step())
                vec.wait_ge(own.sem, own.count())
                vec.reciprocal(fb_rec[:], fb_sum[:]).then_inc(own.sem, own.step())
                vec.wait_ge(own.sem, own.count())
                vec.tensor_scalar(none_in[:], zone_sum[:], 1e-8, None, ALU.is_lt).then_inc(own.sem, own.step())
                vec.tensor_tensor(fb_n[:], fb_w[:], wide(fb_rec[:], 8), ALU.mult).then_inc(own.sem, own.step())
                vec.wait_ge(own.sem, own.count())
                vec.tensor_tensor(fb_d[:], fb_n[:], zone_w[:], ALU.subtract).then_inc(own.sem, own.step())
                vec.wait_ge(own.sem, own.count())
                vec.tensor_tensor(fb_d[:], fb_d[:], wide(none_in[:], 8), ALU.mult).then_inc(own.sem, own.step())
                vec.wait_ge(own.sem, own.count())
                vec.tensor_tensor(w_all[:], fb_d[:], zone_w[:], ALU.add).then_inc(own.sem, own.step())
                vec.wait_ge(own.sem, own.count())
                vec.tensor_reduce(w_sum[:], w_all[:], AX, ALU.add).then_inc(own.sem, own.step())
                vec.wait_ge(own.sem, own.count())
                vec.tensor_scalar(w_sum[:], w_sum[:], 1e-8, None, ALU.max).then_inc(own.sem, own.step())
                vec.wait_ge(own.sem, own.count())
                vec.reciprocal(w_rec[:], w_sum[:]).then_inc(own.sem, own.step())
                vec.wait_ge(own.sem, own.count())
                vec.tensor_tensor(w_tok[:], w_all[:], wide(w_rec[:], 8), ALU.mult).then_inc(own.sem, own.step())
                vec.wait_ge(own.sem, own.count())

            def expert_add(b, e):
                vec.wait_ge(down_done.sem, down_done.at(b, e + 1))
                if e:
                    vec.wait_ge(down_used.sem, down_used.at(b, e))
                for h in range(H):
                    before = x1 if e == 0 else e_acc
                    last = vec.scalar_tensor_tensor(e_acc[:, h], acc[e % 2][:, h * P:(h + 1) * P],
                                                    w_tok[:, h, e:e + 1], before[:, h], ALU.mult, ALU.add)
                last.then_inc(down_used.sem, 1)

            def moe_expert(b, e):
                vec.wait_ge(e_silu_ready.sem, e_silu_ready.at(b, e + 1))
                vec.wait_ge(down_done.sem, down_done.at(b, max(e - 1, 0)))
                vec.tensor_tensor(e_h[:, e % 2], e_silu[:, e % 2], work[e % 2][:, T:2 * T], ALU.mult)\
                    .then_inc(e_h_ready.sem, 1)
                if e:
                    expert_add(b, e - 1)

            def moe_tail(b):
                expert_add(b, EXPERTS - 1)
                vec.wait_ge(down_used.sem, down_used.at(b))
                normalize_in(vec_r, e_acc, st_r, mv_r, var_ready)
                vec.wait_ge(rstd_ready.sem, rstd_ready.at(b, 1))
                normalize_out(e_acc, mv_r, rs_r, x2, x2_ready)

            def attention(b):
                own = vec_r
                vec.wait_ge(scores_done.sem, scores_done.at(b))
                vec.tensor_tensor(probs[:], acc[0][:, 0:T + P], decay[:], ALU.mult).then_inc(probs_ready.sem, 1)
                vec.wait_ge(attn_done.sem, attn_done.at(b))
                vec.wait_ge(x2_ready.sem, x2_ready.at(b))
                sums = head_ps[:].rearrange("p (h n) -> p h n", h=H)
                vec.tensor_scalar(den[:], sums[:, :, P], ATTN_EPS, None, ALU.add).then_inc(own.sem, own.step())
                vec.wait_ge(own.sem, own.count())
                vec.reciprocal(den_r[:], den[:]).then_inc(own.sem, own.step())
                vec.wait_ge(own.sem, own.count())
                for h in range(H):
                    last = vec.scalar_tensor_tensor(r_r[:, h], sums[:, h, 0:P], den_r[:, h:h + 1], x2[:, h],
                                                    ALU.mult, ALU.add)
                last.then_inc(attn_read.sem, 1)
                vec.wait_ge(attn_read.sem, attn_read.at(b))
                normalize_in(own, r_r, st_r, mv_r, var_ready)
                vec.wait_ge(rstd_ready.sem, rstd_ready.at(b, 2))
                normalize_out(r_r, mv_r, rs_r, x3, x3_ready)

            def find(b, h):
                own = vec_r

                vec.wait_ge(sim_ready.sem, sim_ready.at(b, 2 * h + 2))
                vec.sem_inc(passed.sem, 1)
                for c in range(2 * HEADS):
                    vec.max(top[:, c], sim[:, h, c]).then_inc(own.sem, own.step())
                vec.wait_ge(own.sem, own.count())
                vec.sem_inc(passed.sem, 1)
                for c in range(2 * HEADS):
                    vec.max_index(top_i[:, c], top[:, c], sim[:, h, c]).then_inc(own.sem, own.step())
                for c in range(HEADS):
                    vec.tensor_tensor(pair[:, c].rearrange("p (i j) -> p i j", i=TOPK), wide(top[:, c], TOPK),
                                              top[:, HEADS + c].unsqueeze(1).broadcast_to([P, TOPK, TOPK]), ALU.add).then_inc(own.sem, own.step())
                vec.wait_ge(own.sem, own.count())
                vec.tensor_copy(top_if[:], top_i[:]).then_inc(own.sem, own.step())
                for c in range(HEADS):
                    vec.max(score[:, c], pair[:, c]).then_inc(own.sem, own.step())
                vec.wait_ge(own.sem, own.count())
                vec.sem_inc(passed.sem, 1)
                for c in range(HEADS):
                    vec.max_index(pair_i[:, c], score[:, c], pair[:, c]).then_inc(own.sem, own.step())
                vec.tensor_tensor(score_d[:], score[:], score[:, :, 0:1].broadcast_to([P, HEADS, TOPK]),
                                  ALU.subtract).then_inc(score_d_ready.sem, 1)
                vec.wait_ge(own.sem, own.count())
                flat = pair_i[:].rearrange("p c k -> p (c k)")
                vec.tensor_scalar(rank_x[:], flat, 3, None, ALU.logical_shift_right).then_inc(own.sem, own.step())
                vec.tensor_scalar(rank_y[:], flat, 7, None, ALU.bitwise_and).then_inc(own.sem, own.step())
                vec.wait_ge(own.sem, own.count())
                numbers = iota8[:].unsqueeze(1).broadcast_to([P, SLOTS, TOPK])
                for part, (rank, out_) in enumerate(((rank_x, slot_x), (rank_y, slot_y))):
                    vec.tensor_tensor(rank_hot[:], numbers, wide(rank[:], TOPK), ALU.is_equal).then_inc(own.sem, own.step())
                    vec.wait_ge(own.sem, own.count())
                    index = top_if[:, part * HEADS:(part + 1) * HEADS].unsqueeze(2)\
                        .broadcast_to([P, HEADS, TOPK, TOPK])
                    vec.tensor_tensor(rank_val[:].rearrange("p (c k) i -> p c k i", c=HEADS),
                                           rank_hot[:].rearrange("p (c k) i -> p c k i", c=HEADS), index, ALU.mult).then_inc(own.sem, own.step())
                    vec.wait_ge(own.sem, own.count())
                    vec.tensor_reduce(out_[:], rank_val[:], AX, ALU.add).then_inc(own.sem, own.step())
                    vec.wait_ge(own.sem, own.count())
                vec.scalar_tensor_tensor(slot_e[:], slot_x[:], float(KEYS), slot_y[:], ALU.mult, ALU.add).then_inc(own.sem, own.step())
                vec.wait_ge(own.sem, own.count())
                vec.tensor_scalar(slot_u[:], slot_e[:], float(TABLE - 1), None, ALU.min).then_inc(own.sem, own.step())
                vec.wait_ge(own.sem, own.count())
                vec.tensor_scalar(slot_hi[:], slot_u[:], 7, None, ALU.logical_shift_right).then_inc(own.sem, own.step())
                vec.tensor_scalar(slot_lo[:], slot_u[:], P - 1, None, ALU.bitwise_and).then_inc(own.sem, own.step())
                vec.wait_ge(own.sem, own.count())
                vec.tensor_copy(slot[:, 0], slot_hi[:]).then_inc(own.sem, own.step())
                vec.tensor_copy(slot[:, 1], slot_lo[:]).then_inc(own.sem, own.step())
                vec.wait_ge(own.sem, own.count())

            def lay_out(b, h):
                own = vec_r

                vec.wait_ge(score_e_ready.sem, score_e_ready.at(b, h + 1))
                vec.tensor_reduce(score_s[:], score_e[:, h], AX, ALU.add).then_inc(own.sem, own.step())
                vec.wait_ge(own.sem, own.count())
                vec.reciprocal(score_r[:], score_s[:]).then_inc(own.sem, own.step())
                vec.wait_ge(own.sem, own.count())
                vec.tensor_tensor(slot[:, 2].rearrange("p (c k) -> p c k", c=HEADS), score_e[:, h],
                                       wide(score_r[:], TOPK), ALU.mult).then_inc(own.sem, own.step())
                vec.wait_ge(own.sem, own.count())
                vec.transpose(slot_t[:].rearrange("p a g -> p (a g)"), slot[:].rearrange("p a g -> p (a g)")).then_inc(own.sem, own.step())
                vec.wait_ge(own.sem, own.count())
                vec.tensor_scalar(hi_16[:], slot_t[:, 0], quad_base[:], None, ALU.add).then_inc(own.sem, own.step())
                vec.tensor_copy(lo_16[:], slot_t[:, 1]).then_inc(own.sem, own.step())
                vec.tensor_copy(p_hi[:], slot_t[:, 2]).then_inc(own.sem, own.step())
                vec.wait_ge(own.sem, own.count())
                vec.tensor_tensor(p_lo[:], slot_t[:, 2], p_hi[:], ALU.subtract).then_inc(own.sem, own.step())
                vec.wait_ge(own.sem, own.count())
                vec.wait_ge(spread_done.sem, spread_done.at(b, h * QUADS))
                vec.tensor_tensor(hot_lo[:], expert_lo[:], lo_16[:].unsqueeze(1).broadcast_to([P, P, GROUPS]),
                                          ALU.is_equal).then_inc(own.sem, own.step())
                many = [P, QUADS * BLOCKS, GROUPS]
                vec.tensor_tensor(hot_hi[:], expert_hi[:], hi_16[:].unsqueeze(1).broadcast_to(many), ALU.is_equal).then_inc(own.sem, own.step())
                vec.wait_ge(own.sem, own.count())
                vec.tensor_tensor(pick_hi[:], hot_hi[:], p_hi[:].unsqueeze(1).broadcast_to(many), ALU.mult).then_inc(own.sem, own.step())
                vec.tensor_tensor(pick_lo[:], hot_hi[:], p_lo[:].unsqueeze(1).broadcast_to(many), ALU.mult)\
                    .then_inc(picks_ready.sem, 1)

            def coefficients(b, h):
                vec.wait_ge(dots_ready.sem, dots_ready.at(b))
                if h:
                    vec.wait_ge(coef_read.sem, coef_read.at(b))
                for q in range(QUADS):
                    n = h * QUADS + q
                    vec.wait_ge(spread_done.sem, spread_done.at(b, n + 1))
                    few = GROUPS // QUADS
                    at = slice(q * few, (q + 1) * few)
                    for s in range(QUADS):
                        last = vec.tensor_tensor(
                            coef[:].rearrange("p a (s g) -> p g s a", s=QUADS)[:, at, s],
                            acc[n % 2][:].rearrange("p (g s a) -> p g s a", g=few, s=QUADS)[:, :, s],
                            dots[:, :, h * P:(h + 1) * P].rearrange("p a (s g) -> p g s a", s=QUADS)[:, at, s],
                            ALU.mult)
                    last.then_inc(coef_ready.sem, 1)

            def peer(b):
                own = vec_r
                find(b, 0)
                for j in range(INTER // P):
                    vec.wait_ge(m_silu_ready.sem, m_silu_ready.at(b, j + 1))
                    vec.tensor_tensor(m_h[:, j], m_silu[:, j % 2], work[j % 2][:, T:2 * T], ALU.mult)\
                        .then_inc(m_h_ready.sem, 1)
                lay_out(b, 0)
                find(b, 1)
                coefficients(b, 0)
                lay_out(b, 1)
                coefficients(b, 1)
                vec.wait_ge(peer_done.sem, peer_done.at(b))
                vec.wait_ge(x3_ready.sem, x3_ready.at(b))
                vec.tensor_tensor(r_r[:].rearrange("p h n -> p (h n)"), head_ps[:, 0:T],
                                  x3[:].rearrange("p h n -> p (h n)"), ALU.add).then_inc(peer_read.sem, 1)
                vec.wait_ge(peer_read.sem, peer_read.at(b))
                normalize_in(own, r_r, st_r, mv_r, var_ready)
                vec.wait_ge(rstd_ready.sem, rstd_ready.at(b, 3))
                vec.wait_ge(stored.sem, stored.at(b, 0))
                normalize_out(r_r, mv_r, rs_r, x4, x4_ready)
                own.end()

            def nothing(*_):
                pass

            vec.memset(mv_m[:], 0.0).then_inc(consts_vec.sem, 1)
            vec.memset(x_t[:], 0.0).then_inc(consts_vec.sem, 1)
            vec.memset(dA[:], 0.0).then_inc(consts_vec.sem, 1)
            vec.memset(eps_ln[:], LN_EPS).then_inc(consts_vec.sem, 1)
            vec.wait_ge(*loads["mixer"])
            for k in range(TAPS):
                vec.tensor_tensor(w_conv[:, k], w_in[:], taps[:, k], ALU.mult).then_inc(consts_vec.sem, 1)
            vec.tensor_scalar(inv_dt2[:], inv_dt[:], 2.0, None, ALU.mult).then_inc(consts_vec.sem, 1)
            vec.wait_ge(consts_vec.sem, consts_vec.at(0))
            steps = dict(mixer_in=nothing, moe_head=moe_head, mixer_project=mixer_project, moe_expert=moe_expert,
                         mixer_scan=mixer_scan, moe_tail=moe_tail, mixer_out=mixer_out, attention=attention,
                         peer=peer)
            weave(steps, 0, None)
            vec.wait_ge(*loads["attention"])
            vec.tensor_copy(gamma_row, gamma[:].broadcast_to([P, T])).then_inc(made.sem, 1)
            vec.wait_ge(made.sem, made.at(0, 1))
            vec.tensor_tensor_scan(decay[:, 0:T], gamma_row, diagonal[:], 0.0, ALU.mult, ALU.add).then_inc(made.sem, 1)
            vec.wait_ge(made.sem, made.at(0, 2))
            vec.tensor_copy(decay[:, T:T + P], decay[:, 0:P]).then_inc(made.sem, 1)
            vec.wait_ge(*loads["moe"])
            vec.wait_ge(*loads["peer"])
            vec.reciprocal(neg_inv_temp[:], temperature[:]).then_inc(made.sem, 1)
            vec.wait_ge(made.sem, made.at(0, 4))
            vec.tensor_scalar(neg_inv_temp[:], neg_inv_temp[:], -1.0, None, ALU.mult).then_inc(made.sem, 1)
            vec.wait_ge(made.sem, made.at(0, 5))
            weave(steps, 1, 0)
            with vec.Fori(1, NB - 1) as i:
                weave(steps, i + 1, i)
            weave(steps, None, NB - 1)


def kernel(**inputs):
    import concourse.bacc as bacc
    from concourse.bass_utils import run_bass_kernel_spmd

    A, M, C, D = "L0_attn_", "L0_ffn_", "L1_attn_", "L1_ffn_"
    i = {k: np.asarray(v) for k, v in inputs.items()}

    def flip(a):
        return np.ascontiguousarray(np.swapaxes(a, -1, -2))

    rows = np.arange(P)
    pick = (np.arange(6 * STATES)[:, None] % (2 * STATES) == np.arange(2 * STATES)[None, :])
    arrays = {
        "x": i[A + "x"], "W_in": i[A + "W_in"], "conv_x_w": i[A + "conv_x_w"][:, 0], "conv_z_w": i[A + "conv_z_w"][:, 0],
        "conv_x_b": i[A + "conv_x_b"], "conv_z_b": i[A + "conv_z_b"], "W_xdbl": i[A + "W_xdbl"],
        "W_dt": i[A + "W_dt"], "inv_dt": i[A + "inv_dt"], "D": i[A + "D"], "W_out": i[A + "W_out"],
        "b_out": i[A + "b_out"],
        "moe_Wg": i[M + "Wg"], "moe_Wu": i[M + "Wu"], "moe_Wd": i[M + "Wd"], "Wr": i[M + "Wr"],
        "temperature": i[M + "temperature"],
        "A_Wq_t": flip(i[C + "Wq"]), "A_Wk_t": flip(i[C + "Wk"]), "A_Wv_t": flip(i[C + "Wv"]),
        "bq": i[C + "bq"], "bk": i[C + "bk"], "bv": i[C + "bv"], "gamma": i[C + "gamma"].reshape(1),
        "Wq_p": i[D + "Wq"].reshape(2 * HEADS, RANK, P),
        "keys_p": i[D + "keys"].transpose(2, 0, 3, 1).reshape(2 * HEADS, RANK, KEYS),
        "down_t": flip(i[D + "down_embed"]), "up_embed": i[D + "up_embed"],
        "M_Wg_t": flip(i[D + "Wg"]), "M_Wu_t": flip(i[D + "Wu"]), "M_Wd_t": flip(i[D + "Wd"]),
        "ident": np.eye(P, dtype=np.float32),
        "diagonal": np.eye(P, T, dtype=np.float32),
        "iota8": np.tile(np.arange(8, dtype=np.float32), (P, 1)),
        "pick_state": np.repeat(pick[:, :, None], P, axis=2).astype(mybir.dt.np(BF16)),
        "expert_lo": np.tile(np.arange(P, dtype=np.float16)[None, :, None], (P, 1, GROUPS)),
        "expert_hi": np.tile(np.arange(QUADS * BLOCKS, dtype=np.float16)[None, :, None], (P, 1, GROUPS)),
        "quad_base": (rows // GROUPS * BLOCKS).astype(np.float32)[:, None],
    }
    nc = bacc.Bacc("TRN2", target_bir_lowering=False, num_devices=1)
    given, aps = {}, {}
    for name, a in arrays.items():
        a = np.ascontiguousarray(a)
        given["in_" + name] = a
        aps[name] = nc.dram_tensor("in_" + name, a.shape, mybir.dt.from_np(a.dtype), kind="ExternalInput").ap()
    shape = arrays["x"].shape
    out = nc.dram_tensor("out", shape, F32, kind="ExternalOutput").ap()
    build(nc, aps, out)
    r = run_bass_kernel_spmd(nc, [given], core_ids=[0])
    return r.results[0]["out"]
```

```python
from contextlib import ExitStack

import numpy as np

import concourse.bass as bass
from concourse import mybir

F32 = mybir.dt.float32
F16 = mybir.dt.float16
BF16 = mybir.dt.bfloat16
U32 = mybir.dt.uint32
ALU = mybir.AluOpType
ACT = mybir.ActivationFunctionType
AX = mybir.AxisListType.X

P = 128
T = 256
H = T // P
TAPS = 4
STATES = 16
RANK = 64
EXPERTS = 8
HEADS = 4
KEYS = 128
TOPK = 8
SLOTS = HEADS * TOPK
TABLE = 2048
BLOCKS = TABLE // P
INTER = 512
GROUPS = 32
QUADS = P // GROUPS

SLOTS_TIME = 24
SPREAD_STATES = dict(zip((7, 8, 10, 13, 14, 15, 16, 17), range(8)))
SCAN = dict(zip((8, 9, 11, 14, 15, 16, 17, 18), range(8)))
EXPERT_IN = dict(zip((1, 2, 4, 5, 7, 8, 10, 11), range(8)))
EXPERT_MUL = dict(zip((2, 3, 5, 6, 8, 9, 11, 12), range(8)))
EXPERT_OUT = dict(zip((4, 5, 6, 7, 9, 10, 12, 13), range(8)))
EXPERT_ADD = dict(zip((5, 6, 7, 8, 10, 11, 13, 14), range(8)))
DOTS = {3: (0, 1), 4: (2, 3), 5: (4, 5), 6: (6, 7)}
MLP_IN = dict(zip((12, 13, 14, 15), range(4)))
MLP_MUL = dict(zip((13, 14, 15, 16), range(4)))
TOP_KEYS = {2: 0, 8: 1}
KEY_NAMES = {3: 0, 9: 1}
PAIRS = {4: 0, 10: 1}
EXPERT_NAMES = {5: 0, 11: 1}
TO_SLOTS = {6: 0, 12: 1}
ONE_HOT = {7: 0, 13: 1}
SPREAD = dict(zip((8, 9, 10, 11, 16, 17, 18, 19), range(8)))
COEF = dict(zip((9, 10, 11, 12, 17, 18, 19, 20), range(8)))
SUM_0 = {13: 0, 14: 4, 15: 8, 16: 12}

E_RING = 4
RING = 4
LN_EPS = 1e-5
ATTN_EPS = 1e-6
GOLDEN_CENTER = float(1.0 / np.e)
GOLDEN_LOWER = float(0.5 - np.log(4.0 / 3.0))
GOLDEN_UPPER = 0.5


VEC_MIDDLE = 36
VEC_PICKS = 105


class Signal:

    def __init__(self, sem, per=1):
        self.sem, self.per = sem, per

    def at(self, b, k=None):
        return b * self.per + (self.per if k is None else k)


class Steps:

    def __init__(self, sem, per):
        self.sem, self.per = sem, per

    def begin(self, b):
        self.b, self.n = b, 0

    def step(self):
        self.n += 1
        return 1

    def count(self):
        return self.b * self.per + self.n

    def end(self):
        assert self.n == self.per, (self.n, self.per)


def weave(steps, mixer=None, middle=None, picks=None):
    for slot in range(SLOTS_TIME):
        if picks is not None:
            steps["picks"](picks, slot)
        if mixer is not None:
            steps["mixer"](mixer, slot)
        if middle is not None:
            steps["middle"](middle, slot)


def later_sequences(engine, steps, NB):
    weave(steps, mixer=1, middle=0)
    weave(steps, mixer=2, middle=1, picks=0)
    with engine.Fori(1, NB - 2) as i:
        weave(steps, mixer=i + 2, middle=i + 1, picks=i)
    weave(steps, middle=NB - 1, picks=NB - 2)
    weave(steps, picks=NB - 1)


def build(nc, d, out):
    NB = d["x"].shape[0]
    with ExitStack() as ctx:
        def sb(name, shape, dt=F32):
            return ctx.enter_context(nc.sbuf_tensor(name, [P] + shape, dt))

        def bank(name, n=1):
            return ctx.enter_context(nc.psum_tensor(name, [P, 512 * n], F32))

        def signal(name, per=1):
            return Signal(ctx.enter_context(nc.semaphore(name)), per)

        ident = sb("ident", [P])
        ones = sb("ones", [P])
        w_in = sb("w_in", [2 * P])
        w_conv = sb("w_conv", [TAPS, 2 * P])
        conv_b = sb("conv_b", [2])
        w_dt_low = sb("w_dt_low", [RANK])
        w_bc3 = sb("w_bc3", [3, 2 * STATES])
        w_dt = sb("w_dt", [P])
        inv_dt = sb("inv_dt", [1])
        inv_dt2 = sb("inv_dt2", [1])
        skip_d = sb("skip_d", [1])
        w_out = sb("w_out", [2, P])
        b_out = sb("b_out", [P])
        pick_state = sb("pick_state", [2 * STATES, P], BF16)
        moe_g = sb("moe_g", [EXPERTS, P])
        moe_u = sb("moe_u", [EXPERTS, P])
        moe_d = sb("moe_d", [EXPERTS, P])
        w_route = sb("w_route", [EXPERTS])
        temperature = sb("temperature", [1])
        neg_inv_temp = sb("neg_inv_temp", [1])
        iota8 = sb("iota8", [8])
        wq = sb("wq", [P])
        wk = sb("wk", [P])
        wv = sb("wv", [P])
        bq = sb("bq", [1])
        bk = sb("bk", [1])
        bv = sb("bv", [P])
        gamma = sb("gamma", [1])
        decay = sb("decay", [T + P])
        diagonal = sb("diagonal", [T])
        key_map = sb("key_map", [2 * HEADS, KEYS])
        w_down = sb("w_down", [TABLE])
        w_up = sb("w_up", [BLOCKS, P])
        mlp_g = sb("mlp_g", [INTER])
        mlp_u = sb("mlp_u", [INTER])
        mlp_d = sb("mlp_d", [INTER // P, P])
        expert_lo = sb("expert_lo", [P, GROUPS], F16)
        expert_hi = sb("expert_hi", [QUADS * BLOCKS, GROUPS], F16)
        quad_base = sb("quad_base", [1])
        eps_ln = sb("eps_ln", [H])
        minus_half = sb("minus_half", [H])

        x_in = sb("x_in", [H, P])
        x_t = sb("x_t", [T + TAPS - 1])
        xs = sb("xs", [T])
        z = sb("z", [T])
        dt_low = sb("dt_low", [T])
        bc_hi = sb("bc_hi", [T], BF16)
        bc_rest = sb("bc_rest", [T])
        bc_mid = sb("bc_mid", [T], BF16)
        bc_parts = sb("bc_parts", [T], BF16)
        dt_sum = sb("dt_sum", [T])
        dt_abs = sb("dt_abs", [T])
        dt_exp = sb("dt_exp", [T])
        dt_log = sb("dt_log", [T])
        dt_pos = sb("dt_pos", [T])
        delta = sb("delta", [T])
        du = sb("du", [T])
        dA = sb("dA", [STATES, T])
        dBu = sb("dBu", [2 * T])
        state = sb("state", [2 * T])
        state_c = sb("state_c", [RING, 2 * T])
        y_pair = sb("y_pair", [2 * T])
        y_sum = sb("y_sum", [T])
        y = sb("y", [T])

        def norm_buffers(stage):
            return (sb("sum_" + stage, [H, P]), sb("stats_" + stage, [H, 6]), sb("mean_var_" + stage, [H, 2]),
                    sb("var_eps_" + stage, [H]), sb("rstd_" + stage, [H]))

        norm_a, norm_b, norm_c = norm_buffers("mixer"), norm_buffers("middle"), norm_buffers("picks")

        x1 = sb("x1", [H, P])
        x2 = sb("x2", [H, P])
        x3 = sb("x3", [H, P])
        x4 = sb("x4", [H, P])
        x1_t = sb("x1_t", [T])
        x2_t = sb("x2_t", [T])
        x3_t = sb("x3_t", [T])

        r_exp = sb("r_exp", [H, 8])
        r_exp1 = sb("r_exp1", [H, 8])
        inh = sb("inh", [H, 8])
        off_center = sb("off_center", [H, 8])
        dist = sb("dist", [H, 8])
        near = sb("near", [H, 8])
        fall = sb("fall", [H, 8])
        in_zone = sb("in_zone", [H, 8])
        zone_w = sb("zone_w", [H, 8])
        zone_sum = sb("zone_sum", [H])
        none_in = sb("none_in", [H])
        fall8 = sb("fall8", [H, 8])
        fall_i = sb("fall_i", [H, 8], U32)
        fall_if = sb("fall_if", [H, 8])
        first = sb("first", [H, 8])
        two = sb("two", [H, 8])
        fb_w = sb("fb_w", [H, 8])
        fb_sum = sb("fb_sum", [H])
        fb_rec = sb("fb_rec", [H])
        fb_n = sb("fb_n", [H, 8])
        fb_d = sb("fb_d", [H, 8])
        w_all = sb("w_all", [H, 8])
        w_sum = sb("w_sum", [H])
        w_rec = sb("w_rec", [H])
        w_tok = sb("w_tok", [H, 8])
        e_silu = sb("e_silu", [2, T])
        e_h = sb("e_h", [E_RING, T])

        q_t = sb("q_t", [T])
        k_t = sb("k_t", [T])
        v_1 = sb("v_1", [H, P + 1])
        probs = sb("probs", [T + P])
        den = sb("den", [H])
        den_r = sb("den_r", [H])

        sim = sb("sim", [H, 2 * HEADS, KEYS])
        top = sb("top", [2 * HEADS, TOPK])
        top_i = sb("top_i", [2 * HEADS, TOPK], U32)
        top_if = sb("top_if", [2 * HEADS, TOPK])
        pair = sb("pair", [HEADS, TOPK * TOPK])
        score = sb("score", [HEADS, TOPK])
        pair_i = sb("pair_i", [HEADS, TOPK], U32)
        rank = sb("rank", [2, SLOTS], U32)
        rank_hot = sb("rank_hot", [2 * SLOTS, TOPK])
        rank_val = sb("rank_val", [2 * SLOTS, TOPK])
        slot_xy = sb("slot_xy", [2 * SLOTS])
        slot_e = sb("slot_e", [SLOTS])
        slot_u = sb("slot_u", [SLOTS], U32)
        slot_hi = sb("slot_hi", [SLOTS], U32)
        slot_lo = sb("slot_lo", [SLOTS], U32)
        slot = sb("slot", [3, SLOTS])
        slot_t = sb("slot_t", [3, GROUPS])
        score_d = sb("score_d", [HEADS, TOPK])
        score_e = sb("score_e", [H, HEADS, TOPK])
        score_s = sb("score_s", [HEADS])
        score_r = sb("score_r", [HEADS])
        hi_16 = sb("hi_16", [GROUPS], F16)
        lo_16 = sb("lo_16", [GROUPS], F16)
        p_hi = sb("p_hi", [GROUPS], F16)
        p_lo = sb("p_lo", [GROUPS], F16)
        hot_lo = sb("hot_lo", [P, GROUPS], F16)
        hot_hi = sb("hot_hi", [QUADS * BLOCKS, GROUPS], F16)
        pick_hi = sb("pick_hi", [QUADS * BLOCKS, GROUPS], F16)
        pick_lo = sb("pick_lo", [QUADS * BLOCKS, GROUPS], F16)
        dots = sb("dots", [BLOCKS, T])
        coef = sb("coef", [BLOCKS, P])
        m_silu = sb("m_silu", [2, T])
        m_h = sb("m_h", [INTER // P, T])

        taps = state_c[:, 0:2].rearrange("p a (b n) -> p (a b) n", b=2)
        peer_q = coef[:, 0:2 * HEADS]
        peer_keys = coef[:, 2 * HEADS:4 * HEADS]
        gamma_row = m_h[:, 0]

        b_ps = bank("b_ps")
        c_ps = bank("c_ps")
        mid = [bank("mid_0"), bank("mid_1")]
        mid_acc = bank("mid_acc")
        pick_ps = [bank("pick_0"), bank("pick_1")]
        pick_sum = bank("pick_sum")

        loads = {}
        consts_pool = signal("consts_pool", 4)
        consts_vec = signal("consts_vec", 8)
        made = signal("made", 5)
        map_ps = signal("map_ps", 2)
        map_copied = signal("map_copied", 2)
        passed = signal("passed")
        x_loaded = signal("x_loaded", 16)
        x_transposed = signal("x_transposed")
        x_t_ready = signal("x_t_ready")
        conv_done = signal("conv_done")
        xz_ready = signal("xz_ready", 2)
        proj_done = signal("proj_done")
        dt_low_ready = signal("dt_low_ready")
        bc_hi_ready = signal("bc_hi_ready", 2)
        bc_rest_ready = signal("bc_rest_ready")
        bc_parts_ready = signal("bc_parts_ready", 2)
        dt_done = signal("dt_done")
        dt_sum_ready = signal("dt_sum_ready")
        dt_log_ready = signal("dt_log_ready")
        delta_ready = signal("delta_ready")
        dA_ready = signal("dA_ready", STATES)
        b_ready = signal("b_ready", STATES // 2)
        c_ready = signal("c_ready", STATES // 2)
        b_used = signal("b_used", STATES // 2)
        c_used = signal("c_used", STATES // 2)
        du_ready = signal("du_ready")
        scanned = signal("scanned", STATES // 2)
        pair_added = signal("pair_added", STATES // 2 - 1)
        y_summed = signal("y_summed")
        y_ready = signal("y_ready")
        mix_done = signal("mix_done")
        mix_res = signal("mix_res")
        mix_var = signal("mix_var")
        mix_eps = signal("mix_eps")
        mix_rstd = signal("mix_rstd")
        x1_ready = signal("x1_ready")

        x1_transposed = signal("x1_transposed")
        x1_t_ready = signal("x1_t_ready")
        logits_done = signal("logits_done")
        r_exp_ready = signal("r_exp_ready")
        dist_ready = signal("dist_ready")
        fall_ready = signal("fall_ready", 2)
        weights_ready = signal("weights_ready")
        gu_done = signal("gu_done", EXPERTS)
        e_silu_ready = signal("e_silu_ready", EXPERTS)
        e_h_ready = signal("e_h_ready", EXPERTS)
        down_done = signal("down_done", EXPERTS)
        down_used = signal("down_used", EXPERTS)
        mid_var = signal("mid_var", 2)
        mid_eps = signal("mid_eps", 2)
        mid_rstd = signal("mid_rstd", 2)
        pick_var = signal("pick_var")
        pick_eps = signal("pick_eps")
        pick_rstd = signal("pick_rstd")
        x2_ready = signal("x2_ready")
        x2_transposed = signal("x2_transposed")
        x2_t_ready = signal("x2_t_ready")
        qkv_done = signal("qkv_done")
        qkv_ready = signal("qkv_ready", 3)
        scores_done = signal("scores_done")
        probs_ready = signal("probs_ready")
        attn_done = signal("attn_done")
        attn_read = signal("attn_read")
        x3_ready = signal("x3_ready")
        x3_transposed = signal("x3_transposed")
        x3_t_ready = signal("x3_t_ready")
        sim_done = signal("sim_done", 2 * H)
        sim_ready = signal("sim_ready", 2 * H)
        dots_done = signal("dots_done", BLOCKS // 2)
        dots_ready = signal("dots_ready", BLOCKS // 2)
        mlp_done = signal("mlp_done", INTER // P)
        m_silu_ready = signal("m_silu_ready", INTER // P)
        m_h_ready = signal("m_h_ready", INTER // P)
        score_d_ready = signal("score_d_ready", H)
        score_e_ready = signal("score_e_ready", H)
        picks_ready = signal("picks_ready", H)
        spread_done = signal("spread_done", H * QUADS)
        coef_ready = signal("coef_ready", H * QUADS)
        coef_read = signal("coef_read")
        peer_done = signal("peer_done")
        peer_read = signal("peer_read")
        x4_ready = signal("x4_ready")
        stored = signal("stored", 16)

        vec_a = Steps(ctx.enter_context(nc.semaphore("vector_mixer_steps")), 5)
        vec_b = Steps(ctx.enter_context(nc.semaphore("vector_middle_steps")), VEC_MIDDLE)
        vec_c = Steps(ctx.enter_context(nc.semaphore("vector_picks_steps")), VEC_PICKS)
        act_a = Steps(ctx.enter_context(nc.semaphore("scalar_mixer_steps")), 2)

        def load(eng, group, pairs):
            sem = ctx.enter_context(nc.semaphore("loaded_" + group))
            for dst, src in pairs:
                eng.dma_start(dst, src).then_inc(sem, 16)
            loads[group] = (sem, 16 * len(pairs))

        def row(v, width, start=0):
            return v[start:start + width].partition_broadcast(P)

        def column(v):
            return v.rearrange("(p a) -> p a", a=1)

        block = ctx.enter_context(nc.Block())

        @block.sync
        def _(sp):
            load(sp, "mixer", [
                (ident[:], d["ident"]), (w_in[:], d["W_in"]),
                (taps[:, :, 0:P], d["conv_x_w"].partition_broadcast(P)),
                (taps[:, :, P:2 * P], d["conv_z_w"].partition_broadcast(P)),
                (conv_b[:, 0:1], column(d["conv_x_b"])), (conv_b[:, 1:2], column(d["conv_z_b"])),
                (w_dt_low[:], d["W_xdbl"][:, 0:RANK]),
                (w_bc3[:, 0], d["W_xdbl"][:, RANK:RANK + 2 * STATES]),
                (w_bc3[:, 1], d["W_xdbl"][:, RANK:RANK + 2 * STATES]),
                (w_bc3[:, 2], d["W_xdbl"][:, RANK:RANK + 2 * STATES]),
                (w_dt[0:RANK], d["W_dt"]), (inv_dt[:], column(d["inv_dt"])),
                (skip_d[:], column(d["D"])),
                (w_out[:], d["W_out"].rearrange("(a p) n -> p a n", p=P)),
                (b_out[0:1], d["b_out"].rearrange("(a n) -> a n", a=1)),
                (pick_state[0:6 * STATES], d["pick_state"]),
            ])
            load(sp, "attention", [
                (wq[:], d["A_Wq_t"]), (wk[:], d["A_Wk_t"]), (wv[:], d["A_Wv_t"]),
                (bq[:], column(d["bq"])), (bk[:], column(d["bk"])),
                (bv[0:1], d["bv"].rearrange("(a n) -> a n", a=1)),
                (gamma[:], row(d["gamma"], 1)), (diagonal[:], d["diagonal"]),
            ])
            load(sp, "moe", [
                (moe_g[:], d["moe_Wg"].rearrange("e p i -> p e i")),
                (moe_u[:], d["moe_Wu"].rearrange("e p i -> p e i")),
                (moe_d[:], d["moe_Wd"].rearrange("e p i -> p e i")),
                (w_route[:], d["Wr"]), (temperature[:], row(d["temperature"], 1)),
                (iota8[:], d["iota8"]),
            ])

            load(sp, "peer", [
                (peer_q[0:RANK], d["Wq_p"].rearrange("c n k -> n c k")),
                (peer_keys[0:RANK], d["keys_p"].rearrange("c n k -> n c k")),
                (w_down[:], d["down_t"]),
                (w_up[:], d["up_embed"].rearrange("(a p) n -> p a n", p=P)),
                (mlp_g[:], d["M_Wg_t"]), (mlp_u[:], d["M_Wu_t"]),
                (mlp_d[:], d["M_Wd_t"].rearrange("(a p) n -> p a n", p=P)),
                (expert_lo[:], d["expert_lo"]), (expert_hi[:], d["expert_hi"]),
                (quad_base[:], d["quad_base"]),
            ])

            def fetch(b):
                sp.wait_ge(mix_res.sem, mix_res.at(b, 0))
                sp.dma_start(x_in[:], d["x"][b].rearrange("(h p) n -> p h n", p=P)).then_inc(x_loaded.sem, 16)

            def store(b):
                sp.wait_ge(x4_ready.sem, x4_ready.at(b))
                sp.dma_start(out[b].rearrange("(h p) n -> p h n", p=P), x4[:]).then_inc(stored.sem, 16)

            sp.dma_start(x_in[:], d["x"][0].rearrange("(h p) n -> p h n", p=P)).then_inc(x_loaded.sem, 16)
            for b in range(1, 4):
                fetch(b)
            store(0)
            with sp.Fori(1, NB - 3) as i:
                fetch(i + 3)
                store(i)
            for b in range(NB - 3, NB):
                store(b)
            sp.wait_ge(stored.sem, stored.at(NB - 1))

        @block.gpsimd
        def _(pool):
            pool.memset(ones[:], 1.0).then_inc(consts_pool.sem, 1)
            pool.memset(v_1[:], 1.0).then_inc(consts_pool.sem, 1)
            pool.memset(eps_ln[:], LN_EPS).then_inc(consts_pool.sem, 1)
            pool.memset(minus_half[:], -0.5).then_inc(consts_pool.sem, 1)
            pool.wait_ge(consts_pool.sem, consts_pool.at(0))

            def mixer(b, slot):
                c = SCAN.get(slot, -1)
                if c >= 1:
                    pool.wait_ge(c_used.sem, c_used.at(b, c + 1))
                    if c == 1:
                        pool.wait_ge(y_summed.sem, y_summed.at(b, 0))
                        pool.tensor_tensor(y_pair[:], state_c[:, 0], state_c[:, 1], ALU.add).then_inc(pair_added.sem, 1)
                    else:
                        pool.wait_ge(pair_added.sem, pair_added.at(b, c - 1))
                        pool.tensor_tensor(y_pair[:], y_pair[:], state_c[:, c % RING], ALU.add)\
                            .then_inc(pair_added.sem, 1)
                if c == STATES // 2 - 1:
                    pool.wait_ge(pair_added.sem, pair_added.at(b))
                    pool.wait_ge(y_ready.sem, y_ready.at(b, 0))
                    pool.tensor_tensor(y_sum[:], y_pair[:, 0:T], y_pair[:, T:2 * T], ALU.add)\
                        .then_inc(y_summed.sem, 1)
                if slot == 22:
                    _, _, mean_var, var_eps, rstd = norm_a
                    pool.wait_ge(mix_var.sem, mix_var.at(b))
                    pool.tensor_tensor(var_eps[:], mean_var[:, :, 1], eps_ln[:], ALU.add).then_inc(mix_eps.sem, 1)
                    pool.wait_ge(mix_eps.sem, mix_eps.at(b))
                    pool.tensor_tensor(rstd[:], var_eps[:], minus_half[:], ALU.pow).then_inc(mix_rstd.sem, 1)

            def middle(b, slot):
                if slot in (14, 21):
                    k = 1 if slot == 14 else 2
                    _, _, mean_var, var_eps, rstd = norm_b
                    pool.wait_ge(mid_var.sem, mid_var.at(b, k))
                    pool.tensor_tensor(var_eps[:], mean_var[:, :, 1], eps_ln[:], ALU.add).then_inc(mid_eps.sem, 1)
                    pool.wait_ge(mid_eps.sem, mid_eps.at(b, k))
                    pool.tensor_tensor(rstd[:], var_eps[:], minus_half[:], ALU.pow).then_inc(mid_rstd.sem, 1)

            def picks(b, slot):
                if slot == 22:
                    _, _, mean_var, var_eps, rstd = norm_c
                    pool.wait_ge(pick_var.sem, pick_var.at(b))
                    pool.tensor_tensor(var_eps[:], mean_var[:, :, 1], eps_ln[:], ALU.add).then_inc(pick_eps.sem, 1)
                    pool.wait_ge(pick_eps.sem, pick_eps.at(b))
                    pool.tensor_tensor(rstd[:], var_eps[:], minus_half[:], ALU.pow).then_inc(pick_rstd.sem, 1)

            steps = dict(mixer=mixer, middle=middle, picks=picks)
            weave(steps, mixer=0)
            later_sequences(pool, steps, NB)

        @block.scalar
        def _(act):
            def copy(dst, src):
                return act.activation(dst, src, ACT.Copy)

            def mixer(b, slot):
                if slot == 0:
                    act.wait_ge(x_transposed.sem, x_transposed.at(b))
                    copy(x_t[:, 1:T + 1], b_ps[:, 0:T]).then_inc(x_t_ready.sem, 1)
                if slot == 1:
                    act.wait_ge(conv_done.sem, conv_done.at(b))
                    for half, dst in ((0, xs), (1, z)):
                        act.activation(dst[:], c_ps[:, half * T:(half + 1) * T], ACT.Silu,
                                       bias=conv_b[:, half:half + 1]).then_inc(xz_ready.sem, 1)
                if slot == 2:
                    act.wait_ge(proj_done.sem, proj_done.at(b))
                    copy(dt_low[0:RANK], b_ps[0:RANK, T:2 * T]).then_inc(dt_low_ready.sem, 1)
                    copy(bc_hi[0:96], b_ps[0:96, 0:T]).then_inc(bc_hi_ready.sem, 1)
                    act.wait_ge(c_ready.sem, c_ready.at(b, 0))
                    copy(bc_parts[0:32], b_ps[0:32, 0:T]).then_inc(bc_hi_ready.sem, 1)
                if slot == 3:
                    act.wait_ge(dt_done.sem, dt_done.at(b))
                    act.activation(dt_sum[:], c_ps[:, 0:T], ACT.Identity, bias=inv_dt2[:]).then_inc(dt_sum_ready.sem, 1)
                    act.wait_ge(dt_sum_ready.sem, dt_sum_ready.at(b))
                    act_a.begin(b)
                    act.activation(dt_abs[:], dt_sum[:], ACT.Abs).then_inc(act_a.sem, act_a.step())
                    act.wait_ge(act_a.sem, act_a.count())
                    act.activation(dt_exp[:], dt_abs[:], ACT.Exp, scale=-1.0).then_inc(act_a.sem, act_a.step())
                    act.wait_ge(act_a.sem, act_a.count())
                    act.activation(dt_log[:], dt_exp[:], ACT.Ln, bias=1.0).then_inc(dt_log_ready.sem, 1)
                    act_a.end()
                if slot == 5:
                    act.wait_ge(delta_ready.sem, delta_ready.at(b))
                    act.wait_ge(scanned.sem, scanned.at(b, 0))
                    for n in range(STATES):
                        act.activation(dA[:, n, 1:T], delta[:, 1:T], ACT.Exp, scale=-float(n + 1))\
                            .then_inc(dA_ready.sem, 1)

            def middle(b, slot):
                if slot == 0:
                    act.wait_ge(x1_transposed.sem, x1_transposed.at(b))
                    copy(x1_t[:], mid_acc[:, 0:T]).then_inc(x1_t_ready.sem, 1)
                if slot == 1:
                    act.wait_ge(logits_done.sem, logits_done.at(b))
                    act.activation(r_exp[:].rearrange("p h e -> p (h e)"), mid_acc[:, 0:8 * H], ACT.Exp,
                                   scale=neg_inv_temp[:]).then_inc(r_exp_ready.sem, 1)
                if slot == 3:
                    act.wait_ge(dist_ready.sem, dist_ready.at(b))
                    act.activation(near[:], dist[:], ACT.Exp, scale=-1.0 / 0.1).then_inc(fall_ready.sem, 1)
                    act.activation(fall[:], dist[:], ACT.Exp, scale=-1.0 / 0.3).then_inc(fall_ready.sem, 1)
                if slot in EXPERT_IN:
                    e = EXPERT_IN[slot]
                    act.wait_ge(gu_done.sem, gu_done.at(b, e + 1))
                    act.wait_ge(e_h_ready.sem, e_h_ready.at(b, max(e - 1, 0)))
                    act.activation(e_silu[:, e % 2], mid[e % 2][:, 0:T], ACT.Silu).then_inc(e_silu_ready.sem, 1)
                if slot == 16:
                    act.wait_ge(x2_transposed.sem, x2_transposed.at(b))
                    copy(x2_t[:], mid[0][:, 0:T]).then_inc(x2_t_ready.sem, 1)
                if slot == 17:
                    act.wait_ge(qkv_done.sem, qkv_done.at(b))
                    act.activation(q_t[:], mid[1][:, 0:T], ACT.Relu, bias=bq[:]).then_inc(qkv_ready.sem, 1)
                    act.activation(k_t[:], mid[1][:, T:2 * T], ACT.Relu, bias=bk[:]).then_inc(qkv_ready.sem, 1)
                    copy(v_1[:, :, 0:P], mid[0][:, 0:T].rearrange("p (h n) -> p h n", h=H)).then_inc(qkv_ready.sem, 1)

            def picks(b, slot):
                if slot == 0:
                    act.wait_ge(x3_transposed.sem, x3_transposed.at(b))
                    copy(x3_t[:], pick_ps[1][:, 0:T]).then_inc(x3_t_ready.sem, 1)
                if slot in (1, 2):
                    for n in range(2 * slot - 2, 2 * slot):
                        h, half = divmod(n, 2)
                        act.wait_ge(sim_done.sem, sim_done.at(b, 2 * h + half + 1))
                        copy(sim[:, h, HEADS * half:HEADS * (half + 1)],
                             pick_ps[half][:].rearrange("p (c k) -> p c k", c=HEADS)).then_inc(sim_ready.sem, 1)
                if slot in DOTS:
                    for c in DOTS[slot]:
                        act.wait_ge(dots_done.sem, dots_done.at(b, c + 1))
                        if c == 0:
                            act.wait_ge(coef_ready.sem, coef_ready.at(b, 0))
                        act.activation(dots[:, 2 * c:2 * c + 2], pick_ps[c % 2][:].rearrange("p (a t) -> p a t", a=2),
                                       ACT.Silu).then_inc(dots_ready.sem, 1)
                if slot in MLP_IN:
                    j = MLP_IN[slot]
                    act.wait_ge(mlp_done.sem, mlp_done.at(b, j + 1))
                    act.activation(m_silu[:, j % 2], pick_ps[j % 2][:, 0:T], ACT.Silu).then_inc(m_silu_ready.sem, 1)
                if slot in EXPERT_NAMES:
                    h = EXPERT_NAMES[slot]
                    act.wait_ge(score_d_ready.sem, score_d_ready.at(b, h + 1))
                    act.activation(score_e[:, h], score_d[:], ACT.Exp).then_inc(score_e_ready.sem, 1)

            act.wait_ge(*loads["mixer"])
            act.wait_ge(consts_vec.sem, consts_vec.at(0))
            steps = dict(mixer=mixer, middle=middle, picks=picks)
            weave(steps, mixer=0)
            act.wait_ge(map_ps.sem, map_ps.at(0))
            copy(key_map[:, 0:HEADS], pick_ps[0][:].rearrange("p (c k) -> p c k", c=HEADS)).then_inc(map_copied.sem, 1)
            copy(key_map[:, HEADS:2 * HEADS], pick_ps[1][:].rearrange("p (c k) -> p c k", c=HEADS))\
                .then_inc(map_copied.sem, 1)
            act.wait_ge(made.sem, made.at(0))
            later_sequences(act, steps, NB)

        @block.tensor
        def _(pe):
            def mm(dst, lhs, rhs, start=True, stop=True):
                return pe.matmul(dst, lhs, rhs, start=start, stop=stop)

            def to_columns(dst, x):
                for h in range(H):
                    last = pe.transpose(dst[:, h * P:(h + 1) * P], x[:, h], ident[:])
                return last

            def mixer(b, slot):
                if slot == 0:
                    pe.wait_ge(x_loaded.sem, x_loaded.at(b))
                    pe.wait_ge(mix_res.sem, mix_res.at(b, 0))
                    to_columns(b_ps, x_in).then_inc(x_transposed.sem, 1)
                if slot == 1:
                    pe.wait_ge(x_t_ready.sem, x_t_ready.at(b))
                    pe.wait_ge(c_used.sem, c_used.at(b, 0))
                    for half in range(2):
                        for k in range(TAPS):
                            last = mm(c_ps[:, half * T:(half + 1) * T], w_conv[:, k, half * P:(half + 1) * P],
                                      x_t[:, k:k + T], start=k == 0, stop=k == TAPS - 1)
                    last.then_inc(conv_done.sem, 1)
                if slot == 2:
                    pe.wait_ge(xz_ready.sem, xz_ready.at(b))
                    mm(b_ps[0:96, 0:T], w_bc3[:].rearrange("p a n -> p (a n)"), xs[:])
                    mm(b_ps[0:RANK, T:2 * T], w_dt_low[:], xs[:]).then_inc(proj_done.sem, 1)
                if slot == 3:
                    pe.wait_ge(dt_low_ready.sem, dt_low_ready.at(b))
                    mm(c_ps[:, 0:T], w_dt[0:RANK], dt_low[0:RANK]).then_inc(dt_done.sem, 1)
                if slot in SPREAD_STATES:
                    c = SPREAD_STATES[slot]
                    if c == 0:
                        pe.wait_ge(bc_parts_ready.sem, bc_parts_ready.at(b))
                        pe.wait_ge(dt_sum_ready.sem, dt_sum_ready.at(b))
                    pe.wait_ge(b_used.sem, b_used.at(b, c))
                    for n in range(2):
                        last = mm(b_ps[:, n * T:(n + 1) * T], pick_state[0:96, 2 * c + n], bc_parts[0:96])
                    last.then_inc(b_ready.sem, 1)
                    pe.wait_ge(c_used.sem, c_used.at(b, c))
                    for n in range(2):
                        last = mm(c_ps[:, n * T:(n + 1) * T], pick_state[0:96, STATES + 2 * c + n], bc_parts[0:96])
                    last.then_inc(c_ready.sem, 1)
                if slot == 21:
                    pe.wait_ge(y_ready.sem, y_ready.at(b))
                    for h in range(H):
                        at = b_ps[:, h * P:(h + 1) * P]
                        mm(at, y[:, h * P:(h + 1) * P], w_out[:, 0], stop=False)
                        mm(at, z[:, h * P:(h + 1) * P], w_out[:, 1], start=False, stop=False)
                        last = mm(at, ones[0:1], b_out[0:1], start=False)
                    last.then_inc(mix_done.sem, 1)

            def middle(b, slot):
                if slot == 0:
                    pe.wait_ge(x1_ready.sem, x1_ready.at(b))
                    pe.wait_ge(probs_ready.sem, probs_ready.at(b, 0))
                    to_columns(mid_acc, x1).then_inc(x1_transposed.sem, 1)
                if slot == 1:
                    pe.wait_ge(x1_t_ready.sem, x1_t_ready.at(b))
                    for h in range(H):
                        last = mm(mid_acc[:, 8 * h:8 * h + 8], x1_t[:, h * P:(h + 1) * P], w_route[:])
                    last.then_inc(logits_done.sem, 1)
                if slot in EXPERT_IN:
                    e = EXPERT_IN[slot]
                    if e < 2:
                        pe.wait_ge(attn_read.sem, attn_read.at(b, 0))
                    else:
                        pe.wait_ge(e_h_ready.sem, e_h_ready.at(b, e - 1))
                    mm(mid[e % 2][:, 0:T], moe_g[:, e], x1_t[:])
                    mm(mid[e % 2][:, T:2 * T], moe_u[:, e], x1_t[:]).then_inc(gu_done.sem, 1)
                if slot in EXPERT_OUT:
                    e = EXPERT_OUT[slot]
                    pe.wait_ge(e_h_ready.sem, e_h_ready.at(b, e + 1))
                    if e == 0:
                        pe.wait_ge(r_exp_ready.sem, r_exp_ready.at(b))
                    pe.wait_ge(down_used.sem, down_used.at(b, e))
                    for h in range(H):
                        last = mm(mid_acc[:, h * P:(h + 1) * P], e_h[:, e % E_RING, h * P:(h + 1) * P], moe_d[:, e])
                    last.then_inc(down_done.sem, 1)
                if slot == 16:
                    pe.wait_ge(x2_ready.sem, x2_ready.at(b))
                    to_columns(mid[0], x2).then_inc(x2_transposed.sem, 1)
                if slot == 17:
                    pe.wait_ge(x2_t_ready.sem, x2_t_ready.at(b))
                    mm(mid[1][:, 0:T], wq[:], x2_t[:])
                    mm(mid[1][:, T:2 * T], wk[:], x2_t[:])
                    for h in range(H):
                        at = mid[0][:, h * P:(h + 1) * P]
                        mm(at, x2_t[:, h * P:(h + 1) * P], wv[:], stop=False)
                        last = mm(at, ones[0:1], bv[0:1], start=False)
                    last.then_inc(qkv_done.sem, 1)
                if slot == 18:
                    pe.wait_ge(qkv_ready.sem, qkv_ready.at(b))
                    mm(mid_acc[:, 0:T], k_t[:, 0:P], q_t[:])
                    mm(mid_acc[:, T:T + P], k_t[:, P:T], q_t[:, P:T]).then_inc(scores_done.sem, 1)
                if slot == 20:
                    pe.wait_ge(probs_ready.sem, probs_ready.at(b))
                    mm(mid[0][:, 0:P + 1], probs[:, 0:P], v_1[:, 0])
                    mm(mid[0][:, T:T + P + 1], probs[:, P:T], v_1[:, 0], stop=False)
                    mm(mid[0][:, T:T + P + 1], probs[:, T:T + P], v_1[:, 1], start=False).then_inc(attn_done.sem, 1)

            def spread(b, n):
                h, q = divmod(n, QUADS)
                if n % QUADS == 0:
                    pe.wait_ge(picks_ready.sem, picks_ready.at(b, h + 1))
                if n == 0:
                    pe.wait_ge(dots_ready.sem, dots_ready.at(b))
                elif n in (4, 5):
                    pe.wait_ge(m_h_ready.sem, m_h_ready.at(b, n - 1))
                elif n >= 2:
                    pe.wait_ge(coef_ready.sem, coef_ready.at(b, n - 1))
                for g in range(GROUPS // QUADS):
                    at = pick_ps[n % 2][:, g * 64:(g + 1) * 64]
                    token = q * (GROUPS // QUADS) + g
                    mm(at, hot_lo[:, :, token], pick_hi[:, :, token], stop=False)
                    last = mm(at, hot_lo[:, :, token], pick_lo[:, :, token], start=False)
                last.then_inc(spread_done.sem, 1)

            def sum_experts(h, blocks, first):
                for a in blocks:
                    last = mm(pick_sum[:, h * P:(h + 1) * P], coef[:, a], w_up[:, a], start=first and a == 0,
                              stop=not first and a == BLOCKS - 1)
                return last

            def sum_mlp(h, first):
                for j in range(INTER // P):
                    mm(pick_sum[:, h * P:(h + 1) * P], m_h[:, j, h * P:(h + 1) * P], mlp_d[:, j],
                       start=first and j == 0, stop=not first and j == INTER // P - 1)

            def picks(b, slot):
                if slot == 0:
                    pe.wait_ge(x3_ready.sem, x3_ready.at(b))
                    pe.wait_ge(coef_ready.sem, coef_ready.at(b, 0))
                    to_columns(pick_ps[1], x3).then_inc(x3_transposed.sem, 1)
                if slot in (1, 2):
                    if slot == 1:
                        pe.wait_ge(x3_t_ready.sem, x3_t_ready.at(b))
                    for n in range(2 * slot - 2, 2 * slot):
                        h, half = divmod(n, 2)
                        if n >= 2:
                            pe.wait_ge(sim_ready.sem, sim_ready.at(b, n - 1))
                        mm(pick_ps[half][:], x3_t[:, h * P:(h + 1) * P],
                           key_map[:, HEADS * half:HEADS * (half + 1)].rearrange("p c k -> p (c k)"))\
                            .then_inc(sim_done.sem, 1)
                if slot in DOTS:
                    for c in DOTS[slot]:
                        if c < 2:
                            pe.wait_ge(sim_ready.sem, sim_ready.at(b, c + 3))
                        else:
                            pe.wait_ge(dots_ready.sem, dots_ready.at(b, c - 1))
                        for a in (2 * c, 2 * c + 1):
                            last = mm(pick_ps[c % 2][:, (a % 2) * T:(a % 2 + 1) * T], w_down[:, a * P:(a + 1) * P],
                                      x3_t[:])
                        last.then_inc(dots_done.sem, 1)
                if slot in SPREAD:
                    spread(b, SPREAD[slot])
                if slot in MLP_IN:
                    j = MLP_IN[slot]
                    if j < 2:
                        pe.wait_ge(coef_ready.sem, coef_ready.at(b, 3 + j))
                    else:
                        pe.wait_ge(m_h_ready.sem, m_h_ready.at(b, j - 1))
                    mm(pick_ps[j % 2][:, 0:T], mlp_g[:, j * P:(j + 1) * P], x3_t[:])
                    mm(pick_ps[j % 2][:, T:2 * T], mlp_u[:, j * P:(j + 1) * P], x3_t[:]).then_inc(mlp_done.sem, 1)
                if slot in SUM_0:
                    a = SUM_0[slot]
                    if a == 0:
                        pe.wait_ge(coef_ready.sem, coef_ready.at(b, QUADS))
                        pe.wait_ge(peer_read.sem, peer_read.at(b, 0))
                    last = sum_experts(0, range(a, a + 4), first=True)
                    if a + 4 == BLOCKS:
                        last.then_inc(coef_read.sem, 1)
                if slot == 17:
                    pe.wait_ge(m_h_ready.sem, m_h_ready.at(b))
                    sum_mlp(0, first=False)
                if slot == 18:
                    sum_mlp(1, first=True)
                if slot == 21:
                    pe.wait_ge(coef_ready.sem, coef_ready.at(b))
                    sum_experts(1, range(BLOCKS), first=False).then_inc(peer_done.sem, 1)

            pe.wait_ge(*loads["mixer"])
            pe.wait_ge(consts_vec.sem, consts_vec.at(0))
            pe.wait_ge(consts_pool.sem, consts_pool.at(0))
            steps = dict(mixer=mixer, middle=middle, picks=picks)
            weave(steps, mixer=0)
            pe.wait_ge(*loads["peer"])
            for part in range(2):
                for c in range(HEADS):
                    n = part * HEADS + c
                    last = mm(pick_ps[part][:, c * KEYS:(c + 1) * KEYS], peer_q[0:RANK, n], peer_keys[0:RANK, n])
                last.then_inc(map_ps.sem, 1)
            pe.wait_ge(map_copied.sem, map_copied.at(0))
            pe.wait_ge(*loads["moe"])
            pe.wait_ge(*loads["attention"])
            later_sequences(pe, steps, NB)

        @block.vector
        def _(vec):
            def wide(x, n):
                return x.unsqueeze(len(x.shape)).broadcast_to(list(x.shape) + [n])

            def normalize_in(own, norm, ready):
                r, st, mv = norm[:3]
                for h in range(H):
                    vec.bn_stats(st[:, h], r[:, h]).then_inc(own.sem, own.step())
                vec.wait_ge(own.sem, own.count())
                vec.sem_inc(passed.sem, 1)
                vec.bn_aggr(mv[:, 0], st[:, 0]).then_inc(own.sem, own.step())
                vec.bn_aggr(mv[:, 1], st[:, 1]).then_inc(ready.sem, 1)

            def normalize_out(norm, x, ready):
                r, _, mv, _, rs = norm
                for h in range(H):
                    last = vec.tensor_scalar(x[:, h], r[:, h], mv[:, h, 0:1], rs[:, h:h + 1],
                                             ALU.subtract, ALU.mult)
                last.then_inc(ready.sem, 1)

            def mixer(b, slot):
                own = vec_a
                if slot == 3:
                    own.begin(b)
                    vec.wait_ge(bc_hi_ready.sem, bc_hi_ready.at(b))
                    vec.tensor_tensor(bc_rest[0:96], b_ps[0:96, 0:T], bc_hi[0:96], ALU.subtract)\
                        .then_inc(bc_rest_ready.sem, 1)
                    vec.wait_ge(bc_rest_ready.sem, bc_rest_ready.at(b))
                    vec.tensor_copy(bc_mid[0:96], bc_rest[0:96]).then_inc(own.sem, own.step())
                    vec.wait_ge(c_ready.sem, c_ready.at(b, 0))
                    vec.tensor_copy(bc_parts[32:64], bc_rest[32:64]).then_inc(bc_parts_ready.sem, 1)
                    vec.wait_ge(own.sem, own.count())
                    vec.tensor_tensor(bc_parts[64:96], bc_rest[64:96], bc_mid[64:96], ALU.subtract)\
                        .then_inc(bc_parts_ready.sem, 1)
                if slot == 4:
                    vec.wait_ge(dt_sum_ready.sem, dt_sum_ready.at(b))
                    vec.tensor_scalar(dt_pos[:], dt_sum[:], 0.0, None, ALU.max).then_inc(own.sem, own.step())
                    vec.wait_ge(own.sem, own.count())
                    vec.wait_ge(dt_log_ready.sem, dt_log_ready.at(b))
                    vec.tensor_tensor(delta[:], dt_pos[:], dt_log[:], ALU.add).then_inc(delta_ready.sem, 1)
                    vec.wait_ge(delta_ready.sem, delta_ready.at(b))
                    vec.tensor_tensor(du[:], delta[:], xs[:], ALU.mult).then_inc(du_ready.sem, 1)
                if slot in SCAN:
                    c = SCAN[slot]
                    vec.wait_ge(b_ready.sem, b_ready.at(b, c + 1))
                    vec.wait_ge(du_ready.sem, du_ready.at(b))
                    vec.tensor_tensor(dBu[:].rearrange("p (n t) -> p n t", n=2),
                                      b_ps[:].rearrange("p (n t) -> p n t", n=2),
                                      du[:].unsqueeze(1).broadcast_to([P, 2, T]), ALU.mult).then_inc(b_used.sem, 1)
                    vec.wait_ge(dA_ready.sem, dA_ready.at(b, 2 * c + 2))
                    vec.wait_ge(b_used.sem, b_used.at(b, c + 1))
                    vec.tensor_tensor_scan(state[:], dA[:, 2 * c:2 * c + 2].rearrange("p n t -> p (n t)"), dBu[:], 0.0,
                                           ALU.mult, ALU.add).then_inc(scanned.sem, 1)
                    vec.wait_ge(c_ready.sem, c_ready.at(b, c + 1))
                    if c == 0:
                        vec.wait_ge(y_summed.sem, y_summed.at(b, 0))
                    if c >= RING:
                        vec.wait_ge(pair_added.sem, pair_added.at(b, max(c - RING, 1)))
                    vec.wait_ge(scanned.sem, scanned.at(b, c + 1))
                    vec.tensor_tensor(state_c[:, c % RING], state[:], c_ps[:], ALU.mult).then_inc(c_used.sem, 1)
                if slot == 20:
                    vec.wait_ge(y_summed.sem, y_summed.at(b))
                    vec.scalar_tensor_tensor(y[:], xs[:], skip_d[:], y_sum[:], ALU.mult, ALU.add)\
                        .then_inc(y_ready.sem, 1)
                if slot == 22:
                    vec.wait_ge(mix_done.sem, mix_done.at(b))
                    vec.tensor_tensor(norm_a[0][:].rearrange("p h n -> p (h n)"), b_ps[:, 0:T],
                                      x_in[:].rearrange("p h n -> p (h n)"), ALU.add).then_inc(mix_res.sem, 1)
                    vec.wait_ge(mix_res.sem, mix_res.at(b))
                    normalize_in(own, norm_a, mix_var)
                if slot == 23:
                    vec.wait_ge(mix_rstd.sem, mix_rstd.at(b))
                    normalize_out(norm_a, x1, x1_ready)
                    own.end()

            def middle(b, slot):
                own = vec_b
                if slot == 2:
                    own.begin(b)
                    vec.wait_ge(r_exp_ready.sem, r_exp_ready.at(b))
                    vec.tensor_scalar(r_exp1[:], r_exp[:], 1.0, None, ALU.add).then_inc(own.sem, own.step())
                    vec.wait_ge(own.sem, own.count())
                    vec.reciprocal(inh[:], r_exp1[:]).then_inc(own.sem, own.step())
                    vec.wait_ge(own.sem, own.count())
                    vec.tensor_scalar(off_center[:], inh[:], GOLDEN_CENTER, None, ALU.subtract).then_inc(own.sem, own.step())
                    vec.wait_ge(own.sem, own.count())
                    vec.scalar_tensor_tensor(dist[:], off_center[:], -1.0, off_center[:], ALU.mult, ALU.max)\
                        .then_inc(dist_ready.sem, 1)
                    vec.tensor_scalar(in_zone[:], inh[:], GOLDEN_LOWER, None, ALU.is_ge).then_inc(own.sem, own.step())
                if slot == 4:
                    vec.wait_ge(fall_ready.sem, fall_ready.at(b))
                    vec.scalar_tensor_tensor(zone_w[:], inh[:], GOLDEN_UPPER, near[:], ALU.is_le, ALU.mult).then_inc(own.sem, own.step())
                    vec.wait_ge(own.sem, own.count())
                    vec.tensor_tensor(zone_w[:], zone_w[:], in_zone[:], ALU.mult).then_inc(own.sem, own.step())
                    vec.wait_ge(own.sem, own.count())
                    vec.tensor_reduce(zone_sum[:], zone_w[:], AX, ALU.add).then_inc(own.sem, own.step())
                    for h in range(H):
                        vec.max(fall8[:, h], fall[:, h]).then_inc(own.sem, own.step())
                    vec.wait_ge(own.sem, own.count())
                    vec.sem_inc(passed.sem, 1)
                    for h in range(H):
                        vec.max_index(fall_i[:, h], fall8[:, h], fall[:, h]).then_inc(own.sem, own.step())
                    vec.wait_ge(own.sem, own.count())
                    vec.tensor_copy(fall_if[:], fall_i[:]).then_inc(own.sem, own.step())
                    vec.wait_ge(own.sem, own.count())
                    numbers = iota8[:].unsqueeze(1).broadcast_to([P, H, 8])
                    vec.tensor_tensor(first[:], numbers, fall_if[:, :, 0:1].broadcast_to([P, H, 8]), ALU.is_equal).then_inc(own.sem, own.step())
                    vec.tensor_tensor(two[:], numbers, fall_if[:, :, 1:2].broadcast_to([P, H, 8]), ALU.is_equal).then_inc(own.sem, own.step())
                    vec.wait_ge(own.sem, own.count())
                    vec.tensor_tensor(two[:], two[:], first[:], ALU.add).then_inc(own.sem, own.step())
                    vec.wait_ge(own.sem, own.count())
                    vec.tensor_tensor(fb_w[:], fall[:], two[:], ALU.mult).then_inc(own.sem, own.step())
                    vec.wait_ge(own.sem, own.count())
                    vec.tensor_reduce(fb_sum[:], fb_w[:], AX, ALU.add).then_inc(own.sem, own.step())
                    vec.wait_ge(own.sem, own.count())
                    vec.tensor_scalar(fb_sum[:], fb_sum[:], 1e-8, None, ALU.max).then_inc(own.sem, own.step())
                    vec.wait_ge(own.sem, own.count())
                    vec.reciprocal(fb_rec[:], fb_sum[:]).then_inc(own.sem, own.step())
                    vec.wait_ge(own.sem, own.count())
                    vec.tensor_scalar(none_in[:], zone_sum[:], 1e-8, None, ALU.is_lt).then_inc(own.sem, own.step())
                    vec.tensor_tensor(fb_n[:], fb_w[:], wide(fb_rec[:], 8), ALU.mult).then_inc(own.sem, own.step())
                    vec.wait_ge(own.sem, own.count())
                    vec.tensor_tensor(fb_d[:], fb_n[:], zone_w[:], ALU.subtract).then_inc(own.sem, own.step())
                    vec.wait_ge(own.sem, own.count())
                    vec.tensor_tensor(fb_d[:], fb_d[:], wide(none_in[:], 8), ALU.mult).then_inc(own.sem, own.step())
                    vec.wait_ge(own.sem, own.count())
                    vec.tensor_tensor(w_all[:], fb_d[:], zone_w[:], ALU.add).then_inc(own.sem, own.step())
                    vec.wait_ge(own.sem, own.count())
                    vec.tensor_reduce(w_sum[:], w_all[:], AX, ALU.add).then_inc(own.sem, own.step())
                    vec.wait_ge(own.sem, own.count())
                    vec.tensor_scalar(w_sum[:], w_sum[:], 1e-8, None, ALU.max).then_inc(own.sem, own.step())
                    vec.wait_ge(own.sem, own.count())
                    vec.reciprocal(w_rec[:], w_sum[:]).then_inc(own.sem, own.step())
                    vec.wait_ge(own.sem, own.count())
                    vec.tensor_tensor(w_tok[:], w_all[:], wide(w_rec[:], 8), ALU.mult).then_inc(own.sem, own.step())
                    vec.wait_ge(own.sem, own.count())
                if slot in EXPERT_MUL:
                    e = EXPERT_MUL[slot]
                    vec.wait_ge(e_silu_ready.sem, e_silu_ready.at(b, e + 1))
                    if e >= E_RING:
                        vec.wait_ge(down_done.sem, down_done.at(b, e - E_RING + 1))
                    vec.tensor_tensor(e_h[:, e % E_RING], e_silu[:, e % 2], mid[e % 2][:, T:2 * T], ALU.mult)\
                        .then_inc(e_h_ready.sem, 1)
                if slot in EXPERT_ADD:
                    e = EXPERT_ADD[slot]
                    vec.wait_ge(down_done.sem, down_done.at(b, e + 1))
                    total = norm_b[0]
                    if e:
                        vec.wait_ge(down_used.sem, down_used.at(b, e))
                    for h in range(H):
                        before = x1 if e == 0 else total
                        last = vec.scalar_tensor_tensor(total[:, h], mid_acc[:, h * P:(h + 1) * P],
                                                        w_tok[:, h, e:e + 1], before[:, h], ALU.mult, ALU.add)
                    last.then_inc(down_used.sem, 1)
                if slot == 14:
                    vec.wait_ge(down_used.sem, down_used.at(b))
                    normalize_in(own, norm_b, mid_var)
                if slot == 15:
                    vec.wait_ge(mid_rstd.sem, mid_rstd.at(b, 1))
                    normalize_out(norm_b, x2, x2_ready)
                if slot == 19:
                    vec.wait_ge(scores_done.sem, scores_done.at(b))
                    vec.tensor_tensor(probs[:], mid_acc[:, 0:T + P], decay[:], ALU.mult).then_inc(probs_ready.sem, 1)
                if slot == 21:
                    vec.wait_ge(attn_done.sem, attn_done.at(b))
                    vec.wait_ge(x2_ready.sem, x2_ready.at(b))
                    sums = mid[0][:].rearrange("p (h n) -> p h n", h=H)
                    vec.tensor_scalar(den[:], sums[:, :, P], ATTN_EPS, None, ALU.add).then_inc(own.sem, own.step())
                    vec.wait_ge(own.sem, own.count())
                    vec.reciprocal(den_r[:], den[:]).then_inc(own.sem, own.step())
                    vec.wait_ge(own.sem, own.count())
                    for h in range(H):
                        last = vec.scalar_tensor_tensor(norm_b[0][:, h], sums[:, h, 0:P], den_r[:, h:h + 1], x2[:, h],
                                                        ALU.mult, ALU.add)
                    last.then_inc(attn_read.sem, 1)
                    vec.wait_ge(attn_read.sem, attn_read.at(b))
                    normalize_in(own, norm_b, mid_var)
                if slot == 22:
                    vec.wait_ge(mid_rstd.sem, mid_rstd.at(b, 2))
                    normalize_out(norm_b, x3, x3_ready)
                    own.end()

            def find_keys(b, h):
                own = vec_c
                vec.wait_ge(sim_ready.sem, sim_ready.at(b, 2 * h + 2))
                vec.sem_inc(passed.sem, 1)
                for c in range(2 * HEADS):
                    vec.max(top[:, c], sim[:, h, c]).then_inc(own.sem, own.step())

            def name_keys(b, h):
                own = vec_c
                vec.wait_ge(own.sem, own.count())
                vec.sem_inc(passed.sem, 1)
                for c in range(2 * HEADS):
                    vec.max_index(top_i[:, c], top[:, c], sim[:, h, c]).then_inc(own.sem, own.step())

            def find_pairs(b, h):
                own = vec_c
                for c in range(HEADS):
                    vec.tensor_tensor(pair[:, c].rearrange("p (i j) -> p i j", i=TOPK), wide(top[:, c], TOPK),
                                              top[:, HEADS + c].unsqueeze(1).broadcast_to([P, TOPK, TOPK]), ALU.add).then_inc(own.sem, own.step())
                vec.wait_ge(own.sem, own.count())
                vec.tensor_copy(top_if[:], top_i[:]).then_inc(own.sem, own.step())
                for c in range(HEADS):
                    vec.max(score[:, c], pair[:, c]).then_inc(own.sem, own.step())
                vec.wait_ge(own.sem, own.count())
                vec.sem_inc(passed.sem, 1)
                for c in range(HEADS):
                    vec.max_index(pair_i[:, c], score[:, c], pair[:, c]).then_inc(own.sem, own.step())
                vec.tensor_tensor(score_d[:], score[:], score[:, :, 0:1].broadcast_to([P, HEADS, TOPK]),
                                  ALU.subtract).then_inc(score_d_ready.sem, 1)

            def name_experts(b, h):
                own = vec_c
                vec.wait_ge(own.sem, own.count())
                flat = pair_i[:].rearrange("p c k -> p (c k)")
                vec.tensor_scalar(rank[:, 0], flat, 3, None, ALU.logical_shift_right).then_inc(own.sem, own.step())
                vec.tensor_scalar(rank[:, 1], flat, 7, None, ALU.bitwise_and).then_inc(own.sem, own.step())
                vec.wait_ge(own.sem, own.count())
                numbers = iota8[:].unsqueeze(1).broadcast_to([P, 2 * SLOTS, TOPK])
                vec.tensor_tensor(rank_hot[:], numbers, wide(rank[:].rearrange("p a s -> p (a s)"), TOPK), ALU.is_equal)\
                    .then_inc(own.sem, own.step())
                vec.wait_ge(own.sem, own.count())
                index = top_if[:].unsqueeze(2).broadcast_to([P, 2 * HEADS, TOPK, TOPK])
                vec.tensor_tensor(rank_val[:].rearrange("p (c k) i -> p c k i", k=TOPK),
                                  rank_hot[:].rearrange("p (c k) i -> p c k i", k=TOPK), index, ALU.mult)\
                    .then_inc(own.sem, own.step())
                vec.wait_ge(own.sem, own.count())
                vec.tensor_reduce(slot_xy[:], rank_val[:], AX, ALU.add).then_inc(own.sem, own.step())
                vec.wait_ge(own.sem, own.count())
                vec.scalar_tensor_tensor(slot_e[:], slot_xy[:, 0:SLOTS], float(KEYS), slot_xy[:, SLOTS:2 * SLOTS], ALU.mult, ALU.add).then_inc(own.sem, own.step())
                vec.wait_ge(own.sem, own.count())
                vec.tensor_scalar(slot_u[:], slot_e[:], float(TABLE - 1), None, ALU.min).then_inc(own.sem, own.step())
                vec.wait_ge(own.sem, own.count())
                vec.tensor_scalar(slot_hi[:], slot_u[:], 7, None, ALU.logical_shift_right).then_inc(own.sem, own.step())
                vec.tensor_scalar(slot_lo[:], slot_u[:], P - 1, None, ALU.bitwise_and).then_inc(own.sem, own.step())
                vec.wait_ge(own.sem, own.count())
                vec.tensor_copy(slot[:, 0], slot_hi[:]).then_inc(own.sem, own.step())
                vec.tensor_copy(slot[:, 1], slot_lo[:]).then_inc(own.sem, own.step())
                vec.wait_ge(own.sem, own.count())

            def lay_out(b, h):
                own = vec_c
                vec.wait_ge(score_e_ready.sem, score_e_ready.at(b, h + 1))
                vec.tensor_reduce(score_s[:], score_e[:, h], AX, ALU.add).then_inc(own.sem, own.step())
                vec.wait_ge(own.sem, own.count())
                vec.reciprocal(score_r[:], score_s[:]).then_inc(own.sem, own.step())
                vec.wait_ge(own.sem, own.count())
                vec.tensor_tensor(slot[:, 2].rearrange("p (c k) -> p c k", c=HEADS), score_e[:, h],
                                       wide(score_r[:], TOPK), ALU.mult).then_inc(own.sem, own.step())
                vec.wait_ge(own.sem, own.count())
                vec.transpose(slot_t[:].rearrange("p a g -> p (a g)"), slot[:].rearrange("p a g -> p (a g)")).then_inc(own.sem, own.step())
                vec.wait_ge(own.sem, own.count())
                vec.tensor_scalar(hi_16[:], slot_t[:, 0], quad_base[:], None, ALU.add).then_inc(own.sem, own.step())
                vec.tensor_copy(lo_16[:], slot_t[:, 1]).then_inc(own.sem, own.step())
                vec.tensor_copy(p_hi[:], slot_t[:, 2]).then_inc(own.sem, own.step())
                vec.wait_ge(own.sem, own.count())
                vec.tensor_tensor(p_lo[:], slot_t[:, 2], p_hi[:], ALU.subtract).then_inc(own.sem, own.step())
                vec.wait_ge(own.sem, own.count())

            def one_hot(b, h):
                own = vec_c
                vec.wait_ge(own.sem, own.count())
                vec.wait_ge(spread_done.sem, spread_done.at(b, h * QUADS))
                vec.tensor_tensor(hot_lo[:], expert_lo[:], lo_16[:].unsqueeze(1).broadcast_to([P, P, GROUPS]),
                                          ALU.is_equal).then_inc(own.sem, own.step())
                many = [P, QUADS * BLOCKS, GROUPS]
                vec.tensor_tensor(hot_hi[:], expert_hi[:], hi_16[:].unsqueeze(1).broadcast_to(many), ALU.is_equal).then_inc(own.sem, own.step())
                vec.wait_ge(own.sem, own.count())
                vec.tensor_tensor(pick_hi[:], hot_hi[:], p_hi[:].unsqueeze(1).broadcast_to(many), ALU.mult).then_inc(own.sem, own.step())
                vec.tensor_tensor(pick_lo[:], hot_hi[:], p_lo[:].unsqueeze(1).broadcast_to(many), ALU.mult)\
                    .then_inc(picks_ready.sem, 1)

            def coefficients(b, n):
                h, q = divmod(n, QUADS)
                if n == 0:
                    vec.wait_ge(dots_ready.sem, dots_ready.at(b))
                if n == QUADS:
                    vec.wait_ge(coef_read.sem, coef_read.at(b))
                vec.wait_ge(spread_done.sem, spread_done.at(b, n + 1))
                few = GROUPS // QUADS
                at = slice(q * few, (q + 1) * few)
                vec.tensor_tensor(
                    coef[:].rearrange("p a (s g) -> p g s a", s=QUADS)[:, at],
                    pick_ps[n % 2][:].rearrange("p (g s a) -> p g s a", g=few, s=QUADS),
                    dots[:, :, h * P:(h + 1) * P].rearrange("p a (s g) -> p g s a", s=QUADS)[:, at],
                    ALU.mult).then_inc(coef_ready.sem, 1)

            def picks(b, slot):
                own = vec_c
                if slot in TOP_KEYS:
                    if TOP_KEYS[slot] == 0:
                        own.begin(b)
                    find_keys(b, TOP_KEYS[slot])
                if slot in KEY_NAMES:
                    name_keys(b, KEY_NAMES[slot])
                if slot in PAIRS:
                    find_pairs(b, PAIRS[slot])
                if slot in EXPERT_NAMES:
                    name_experts(b, EXPERT_NAMES[slot])
                if slot in TO_SLOTS:
                    lay_out(b, TO_SLOTS[slot])
                if slot in ONE_HOT:
                    one_hot(b, ONE_HOT[slot])
                if slot in MLP_MUL:
                    j = MLP_MUL[slot]
                    vec.wait_ge(m_silu_ready.sem, m_silu_ready.at(b, j + 1))
                    vec.tensor_tensor(m_h[:, j], m_silu[:, j % 2], pick_ps[j % 2][:, T:2 * T], ALU.mult)\
                        .then_inc(m_h_ready.sem, 1)
                if slot in COEF:
                    coefficients(b, COEF[slot])
                if slot == 22:
                    vec.wait_ge(peer_done.sem, peer_done.at(b))
                    vec.wait_ge(x3_ready.sem, x3_ready.at(b))
                    vec.tensor_tensor(norm_c[0][:].rearrange("p h n -> p (h n)"), pick_sum[:, 0:T],
                                      x3[:].rearrange("p h n -> p (h n)"), ALU.add).then_inc(peer_read.sem, 1)
                    vec.wait_ge(peer_read.sem, peer_read.at(b))
                    normalize_in(own, norm_c, pick_var)
                if slot == 23:
                    vec.wait_ge(pick_rstd.sem, pick_rstd.at(b))
                    vec.wait_ge(stored.sem, stored.at(b, 0))
                    normalize_out(norm_c, x4, x4_ready)
                    own.end()

            vec.memset(x_t[:], 0.0).then_inc(consts_vec.sem, 1)
            vec.memset(dA[:], 0.0).then_inc(consts_vec.sem, 1)
            vec.memset(norm_a[2][:], 0.0).then_inc(consts_vec.sem, 1)
            vec.wait_ge(*loads["mixer"])
            for k in range(TAPS):
                vec.tensor_tensor(w_conv[:, k], w_in[:], taps[:, k], ALU.mult).then_inc(consts_vec.sem, 1)
            vec.tensor_scalar(inv_dt2[:], inv_dt[:], 2.0, None, ALU.mult).then_inc(consts_vec.sem, 1)
            vec.wait_ge(consts_vec.sem, consts_vec.at(0))
            steps = dict(mixer=mixer, middle=middle, picks=picks)
            weave(steps, mixer=0)
            vec.wait_ge(*loads["attention"])
            vec.tensor_copy(gamma_row, gamma[:].broadcast_to([P, T])).then_inc(made.sem, 1)
            vec.wait_ge(made.sem, made.at(0, 1))
            vec.tensor_tensor_scan(decay[:, 0:T], gamma_row, diagonal[:], 0.0, ALU.mult, ALU.add).then_inc(made.sem, 1)
            vec.wait_ge(made.sem, made.at(0, 2))
            vec.tensor_copy(decay[:, T:T + P], decay[:, 0:P]).then_inc(made.sem, 1)
            vec.wait_ge(*loads["moe"])
            vec.wait_ge(*loads["peer"])
            vec.reciprocal(neg_inv_temp[:], temperature[:]).then_inc(made.sem, 1)
            vec.wait_ge(made.sem, made.at(0, 4))
            vec.tensor_scalar(neg_inv_temp[:], neg_inv_temp[:], -1.0, None, ALU.mult).then_inc(made.sem, 1)
            vec.wait_ge(made.sem, made.at(0, 5))
            later_sequences(vec, steps, NB)


def kernel(**inputs):
    import concourse.bacc as bacc
    from concourse.bass_utils import run_bass_kernel_spmd

    A, M, C, D = "L0_attn_", "L0_ffn_", "L1_attn_", "L1_ffn_"
    i = {k: np.asarray(v) for k, v in inputs.items()}

    def flip(a):
        return np.ascontiguousarray(np.swapaxes(a, -1, -2))

    rows = np.arange(P)
    pick = (np.arange(6 * STATES)[:, None] % (2 * STATES) == np.arange(2 * STATES)[None, :])
    arrays = {
        "x": i[A + "x"], "W_in": i[A + "W_in"], "conv_x_w": i[A + "conv_x_w"][:, 0], "conv_z_w": i[A + "conv_z_w"][:, 0],
        "conv_x_b": i[A + "conv_x_b"], "conv_z_b": i[A + "conv_z_b"], "W_xdbl": i[A + "W_xdbl"],
        "W_dt": i[A + "W_dt"], "inv_dt": i[A + "inv_dt"], "D": i[A + "D"], "W_out": i[A + "W_out"],
        "b_out": i[A + "b_out"],
        "moe_Wg": i[M + "Wg"], "moe_Wu": i[M + "Wu"], "moe_Wd": i[M + "Wd"], "Wr": i[M + "Wr"],
        "temperature": i[M + "temperature"],
        "A_Wq_t": flip(i[C + "Wq"]), "A_Wk_t": flip(i[C + "Wk"]), "A_Wv_t": flip(i[C + "Wv"]),
        "bq": i[C + "bq"], "bk": i[C + "bk"], "bv": i[C + "bv"], "gamma": i[C + "gamma"].reshape(1),
        "Wq_p": i[D + "Wq"].reshape(2 * HEADS, RANK, P),
        "keys_p": i[D + "keys"].transpose(2, 0, 3, 1).reshape(2 * HEADS, RANK, KEYS),
        "down_t": flip(i[D + "down_embed"]), "up_embed": i[D + "up_embed"],
        "M_Wg_t": flip(i[D + "Wg"]), "M_Wu_t": flip(i[D + "Wu"]), "M_Wd_t": flip(i[D + "Wd"]),
        "ident": np.eye(P, dtype=np.float32),
        "diagonal": np.eye(P, T, dtype=np.float32),
        "iota8": np.tile(np.arange(8, dtype=np.float32), (P, 1)),
        "pick_state": np.repeat(pick[:, :, None], P, axis=2).astype(mybir.dt.np(BF16)),
        "expert_lo": np.tile(np.arange(P, dtype=np.float16)[None, :, None], (P, 1, GROUPS)),
        "expert_hi": np.tile(np.arange(QUADS * BLOCKS, dtype=np.float16)[None, :, None], (P, 1, GROUPS)),
        "quad_base": (rows // GROUPS * BLOCKS).astype(np.float32)[:, None],
    }
    nc = bacc.Bacc("TRN2", target_bir_lowering=False, num_devices=1)
    given, aps = {}, {}
    for name, a in arrays.items():
        a = np.ascontiguousarray(a)
        given["in_" + name] = a
        aps[name] = nc.dram_tensor("in_" + name, a.shape, mybir.dt.from_np(a.dtype), kind="ExternalInput").ap()
    shape = arrays["x"].shape
    out = nc.dram_tensor("out", shape, F32, kind="ExternalOutput").ap()
    build(nc, aps, out)
    r = run_bass_kernel_spmd(nc, [given], core_ids=[0])
    return r.results[0]["out"]
```

```python
from contextlib import ExitStack

import numpy as np

import concourse.bass as bass
from concourse import mybir

F32 = mybir.dt.float32
F16 = mybir.dt.float16
BF16 = mybir.dt.bfloat16
U32 = mybir.dt.uint32
ALU = mybir.AluOpType
ACT = mybir.ActivationFunctionType
AX = mybir.AxisListType.X

P = 128
T = 256
H = T // P
TAPS = 4
STATES = 16
RANK = 64
EXPERTS = 8
HEADS = 4
KEYS = 128
TOPK = 8
SLOTS = HEADS * TOPK
TABLE = 2048
BLOCKS = TABLE // P
INTER = 512
GROUPS = 32
QUADS = P // GROUPS

ROUND = 48
LEAD = dict(picks=0, middle=65, mixer=128)
FIRST_ROUND = (LEAD["mixer"] + ROUND - 1) // ROUND
PE_ORDER = ("mixer", "picks", "middle")
ACT_ORDER = ("picks", "mixer", "middle")
DVE_ORDER = ("middle", "picks", "mixer")
CONV = 0
PROJ = 6
DT = 7
DELTA = 11
DECAYS = 12
SCAN = (16, 19, 22, 26, 32, 34, 36, 37)
MIX_OUT = 40
MIX_VAR = 41
MIX_NORM = 44
LOGITS = 0
DISTANCES = 3
FALLOFF = 2
WEIGHTS = 4
EXPERT_IN = (0, 4, 7, 10, 14, 16, 20, 24)
EXPERT_ACT = (5, 6, 7, 14, 15, 17, 20, 24)
EXPERT_MUL = (5, 5, 11, 15, 18, 21, 23, 27)
EXPERT_TURN = (6, 8, 9, 14, 18, 20, 27, 27)
EXPERT_OUT = (8, 12, 17, 21, 23, 24, 30, 31)
MOE_VAR = 31
MOE_NORM = 33
X2_TURN = 34
QKV = 39
SCORES = 42
PROBS = 43
ATTEND = 46
ATTN_VAR = 46
ATTN_NORM = 46
SIM = (1, 2, 3, 3)
KEYS_TOP = (5, 5)
KEYS_NAME = (5, 7)
PAIRS = 7
NAME_EXPERTS = 9
TO_SLOTS = 10
DOTS = (5, 5, 5, 6, 7, 7, 9, 10)
MLP_IN = (10, 13, 15, 15)
MLP_MUL = (11, 14, 16, 18)
HOT = (14, 22)
PICKED = (14, 22)
SPREAD = (17, 17, 17, 19, 26, 27, 29, 29)
COEF = (19, 19, 22, 22, 23, 27, 28, 30)
SUM_START = (25, 34)
SUM_EXPERTS = (27, 29, 30, 32, 34, 34, 35, 35)
PICKS_VAR = 38
PICKS_NORM = 46

UNROLL = 4
E_RING = 4
RING = 4
LN_EPS = 1e-5
ATTN_EPS = 1e-6
GOLDEN_CENTER = float(1.0 / np.e)
GOLDEN_LOWER = float(0.5 - np.log(4.0 / 3.0))
GOLDEN_UPPER = 0.5


VEC_MIDDLE = 35
VEC_PICKS = 81


def due(places, slot):
    return [k for k, place in enumerate(places) if place == slot]


class Signal:

    def __init__(self, sem, per=1):
        self.sem, self.per = sem, per

    def at(self, b, k=None):
        return b * self.per + (self.per if k is None else k)


class Steps:

    def __init__(self, sem, per):
        self.sem, self.per = sem, per

    def at(self, b):
        self.b = b

    def begin(self):
        self.n = 0

    def step(self):
        self.n += 1
        return 1

    def count(self):
        return self.b * self.per + self.n

    def end(self):
        assert self.n == self.per, (self.n, self.per)


def weave(steps, i, NB=None):
    for slot in range(ROUND):
        begun = []
        for stage in steps:
            ahead, place = divmod(slot + LEAD[stage], ROUND)
            if NB is None or 0 <= i + ahead < NB:
                begun.append(steps[stage](i + ahead, place))
        begun = [step for step in begun if step is not None]
        while begun:
            begun = [step for step in begun if next(step, "ended") != "ended"]


def fill(steps, NB):
    for i in range(1 - FIRST_ROUND, 1):
        weave(steps, i, NB)


def run_and_drain(engine, steps, NB):
    times = (NB - FIRST_ROUND - 1) // UNROLL
    with engine.Fori(1, 1 + times * UNROLL, step=UNROLL) as i:
        for n in range(UNROLL):
            weave(steps, i + n)
    for i in range(1 + times * UNROLL, NB):
        weave(steps, i, NB)


def build(nc, d, out):
    NB = d["x"].shape[0]
    with ExitStack() as ctx:
        def sb(name, shape, dt=F32):
            return ctx.enter_context(nc.sbuf_tensor(name, [P] + shape, dt))

        def bank(name, n=1):
            return ctx.enter_context(nc.psum_tensor(name, [P, 512 * n], F32))

        def signal(name, per=1):
            return Signal(ctx.enter_context(nc.semaphore(name)), per)

        ident = sb("ident", [P])
        ones = sb("ones", [P])
        w_in = sb("w_in", [2 * P])
        w_conv = sb("w_conv", [TAPS, 2 * P])
        conv_b = sb("conv_b", [2])
        w_dt_low = sb("w_dt_low", [RANK])
        w_bc3 = sb("w_bc3", [3, 2 * STATES])
        w_dt = sb("w_dt", [P])
        inv_dt = sb("inv_dt", [1])
        inv_dt2 = sb("inv_dt2", [1])
        skip_d = sb("skip_d", [1])
        w_out = sb("w_out", [2, P])
        w_skip = sb("w_skip", [P])
        b_out = sb("b_out", [P])
        pick_state = sb("pick_state", [2 * STATES, P], BF16)
        moe_gu = sb("moe_gu", [EXPERTS, 2, P])
        zero_row = sb("zero_row", [T], BF16)
        moe_d = sb("moe_d", [EXPERTS, P])
        w_route = sb("w_route", [EXPERTS])
        temperature = sb("temperature", [1])
        neg_inv_temp = sb("neg_inv_temp", [1])
        iota8 = sb("iota8", [8])
        wq = sb("wq", [P])
        wk = sb("wk", [P])
        wv = sb("wv", [P])
        bq = sb("bq", [1])
        bk = sb("bk", [1])
        bv = sb("bv", [P])
        gamma = sb("gamma", [1])
        decay = sb("decay", [T + P])
        diagonal = sb("diagonal", [T])
        key_map = sb("key_map", [2 * HEADS, KEYS])
        w_down = sb("w_down", [TABLE])
        w_up = sb("w_up", [BLOCKS, P])
        mlp_g = sb("mlp_g", [INTER])
        mlp_u = sb("mlp_u", [INTER])
        mlp_d = sb("mlp_d", [INTER // P, P])
        expert_lo = sb("expert_lo", [P, GROUPS], F16)
        expert_hi = sb("expert_hi", [QUADS * BLOCKS, GROUPS], F16)
        quad_base = sb("quad_base", [1])
        iota_16 = sb("iota_16", [TOPK, H * 2 * SLOTS], F16)
        eps_ln = sb("eps_ln", [H])
        minus_half = sb("minus_half", [H])
        zero = sb("zero", [H])

        x_in = sb("x_in", [H, P])
        x_t = sb("x_t", [T + TAPS - 1])
        xs = sb("xs", [T])
        z = sb("z", [T])
        dt_low = sb("dt_low", [T])
        bc_hi = sb("bc_hi", [T], BF16)
        bc_rest = sb("bc_rest", [T])
        bc_mid = sb("bc_mid", [T], BF16)
        bc_parts = sb("bc_parts", [T], BF16)
        dt_sum = sb("dt_sum", [T])
        dt_soft = sb("dt_soft", [T])
        dt_pos = sb("dt_pos", [T])
        delta = sb("delta", [T])
        du = sb("du", [T])
        dA = sb("dA", [STATES, T])
        dBu = sb("dBu", [2, 2 * T])
        state = sb("state", [2 * T])
        state_c = sb("state_c", [RING, 2 * T])
        y_pair = sb("y_pair", [2 * T])
        y_sum = sb("y_sum", [T])

        def norm_buffers(stage):
            return (sb("stats_" + stage, [H, 6]), sb("mean_var_" + stage, [H, 2]), sb("var_eps_" + stage, [H]),
                    sb("minus_mean_" + stage, [H]), sb("rstd_" + stage, [H]), sb("shift_" + stage, [H]))

        norm_a, norm_b, norm_c = norm_buffers("mixer"), norm_buffers("middle"), norm_buffers("picks")
        mid_sum = sb("mid_sum", [H, P])

        x1 = sb("x1", [H, P])
        x2 = sb("x2", [H, P])
        x3 = sb("x3", [H, P])
        x4 = sb("x4", [H, P])
        x1_t = sb("x1_t", [T])
        x2_t = sb("x2_t", [T])
        x3_t = sb("x3_t", [T])

        r_exp = sb("r_exp", [H, 8])
        r_exp1 = sb("r_exp1", [H, 8])
        inh = sb("inh", [H, 8])
        off_center = sb("off_center", [H, 8])
        dist = sb("dist", [H, 8])
        near = sb("near", [H, 8])
        fall = sb("fall", [H, 8])
        in_zone = sb("in_zone", [H, 8])
        zone_w = sb("zone_w", [H, 8])
        zone_sum = sb("zone_sum", [H])
        none_in = sb("none_in", [H])
        fall8 = sb("fall8", [H, 8])
        fall_i = sb("fall_i", [H, 8], U32)
        fall_if = sb("fall_if", [H, 8])
        first = sb("first", [H, 8])
        two = sb("two", [H, 8])
        fb_w = sb("fb_w", [H, 8])
        fb_sum = sb("fb_sum", [H])
        fb_rec = sb("fb_rec", [H])
        fb_n = sb("fb_n", [H, 8])
        fb_d = sb("fb_d", [H, 8])
        w_all = sb("w_all", [H, 8])
        w_sum = sb("w_sum", [H])
        w_rec = sb("w_rec", [H])
        w_tok = sb("w_tok", [H, 8])
        e_silu = sb("e_silu", [2, H, P])
        e_w = sb("e_w", [2, H, P])
        e_h = sb("e_h", [E_RING, T])

        q_t = sb("q_t", [T])
        k_t = sb("k_t", [T])
        v_1 = sb("v_1", [H, P + 1])
        probs = sb("probs", [T + P])
        den = sb("den", [H])
        den_r = sb("den_r", [H])

        sim = sb("sim", [H, 2 * HEADS, KEYS])
        top = sb("top", [H, 2 * HEADS, TOPK])
        top_i = sb("top_i", [H, 2 * HEADS, TOPK], U32)
        key_16 = sb("key_16", [TOPK, H * 2 * HEADS], F16)
        pair = sb("pair", [H, HEADS, TOPK * TOPK])
        score = sb("score", [H, HEADS, TOPK])
        pair_i = sb("pair_i", [H, HEADS, TOPK], U32)
        rank = sb("rank", [TOPK, H, 2, HEADS], U32)
        rank_16 = sb("rank_16", [H * 2 * SLOTS], F16)
        rank_hot = sb("rank_hot", [TOPK, H * 2 * SLOTS], F16)
        key_sum4 = sb("key_sum4", [4, H * 2 * SLOTS], F16)
        key_sum2 = sb("key_sum2", [2, H * 2 * SLOTS], F16)
        slot_xy = sb("slot_xy", [TOPK * H, 2, HEADS], F16)
        slot_e = sb("slot_e", [TOPK * H, HEADS])
        slot_u = sb("slot_u", [TOPK * H, HEADS], U32)
        slot_n = sb("slot_n", [H, 2, SLOTS], U32)
        slot_nt = sb("slot_nt", [H, 2, GROUPS], U32)
        slot_p = sb("slot_p", [H, TOPK, HEADS])
        slot_pt = sb("slot_pt", [H, GROUPS])
        score_d = sb("score_d", [H * HEADS, TOPK])
        score_e = sb("score_e", [H * HEADS, TOPK])
        score_s = sb("score_s", [H * HEADS])
        score_r = sb("score_r", [H * HEADS])
        hi_16 = sb("hi_16", [H, GROUPS], F16)
        lo_16 = sb("lo_16", [H, GROUPS], F16)
        p_hi = sb("p_hi", [H, GROUPS], F16)
        p_lo = sb("p_lo", [H, GROUPS], F16)
        hot_lo = sb("hot_lo", [P, GROUPS], F16)
        hot_hi = sb("hot_hi", [QUADS * BLOCKS, GROUPS], F16)
        pick_hi = sb("pick_hi", [QUADS * BLOCKS, GROUPS], F16)
        pick_lo = sb("pick_lo", [QUADS * BLOCKS, GROUPS], F16)
        dots = sb("dots", [BLOCKS, T])
        m_silu = sb("m_silu", [2, T])
        m_h = sb("m_h", [INTER // P, T])

        taps = state_c[:, 0:2].rearrange("p a (b n) -> p (a b) n", b=2)
        peer_q = dots[:, 0:HEADS].rearrange("p a (b n) -> p (a b) n", b=2)
        peer_keys = dots[:, HEADS:2 * HEADS].rearrange("p a (b n) -> p (a b) n", b=2)
        gamma_row = m_h[:, 0]

        b_ps = bank("b_ps")
        b_tiles = b_ps[:, 0:T].rearrange("p (h n) -> p h n", h=H)
        c_ps = bank("c_ps")
        mid = [bank("mid_0"), bank("mid_1")]
        mid_tiles = [m[:].rearrange("p (h a n) -> p h a n", h=H, a=2) for m in mid]
        mid_acc = bank("mid_acc")
        mid_acc_tiles = mid_acc[:, 0:T].rearrange("p (h n) -> p h n", h=H)
        pick_ps = [bank("pick_0"), bank("pick_1")]
        pick_sum = bank("pick_sum")
        pick_tiles = pick_sum[:, 0:T].rearrange("p (h n) -> p h n", h=H)

        loads = {}
        consts_pool = signal("consts_pool", 6)
        consts_vec = signal("consts_vec", 9)
        made = signal("made", 5)
        map_ps = signal("map_ps", 2)
        map_copied = signal("map_copied", 2)
        passed = signal("passed")
        x_loaded = signal("x_loaded", 16)
        x_transposed = signal("x_transposed")
        x_t_ready = signal("x_t_ready")
        conv_done = signal("conv_done")
        xz_ready = signal("xz_ready", 2)
        proj_done = signal("proj_done")
        dt_low_ready = signal("dt_low_ready")
        bc_hi_ready = signal("bc_hi_ready", 2)
        bc_rest_ready = signal("bc_rest_ready")
        bc_mid_ready = signal("bc_mid_ready", 2)
        bc_parts_ready = signal("bc_parts_ready")
        dt_done = signal("dt_done")
        dt_sum_ready = signal("dt_sum_ready")
        dt_log_ready = signal("dt_log_ready", 2)
        delta_ready = signal("delta_ready")
        dA_ready = signal("dA_ready", STATES)
        b_ready = signal("b_ready", STATES // 2)
        c_ready = signal("c_ready", STATES // 2)
        b_used = signal("b_used", STATES // 2)
        c_used = signal("c_used", STATES // 2)
        du_ready = signal("du_ready")
        scanned = signal("scanned", STATES // 2)
        pair_added = signal("pair_added", STATES // 2 - 1)
        y_summed = signal("y_summed")
        mix_done = signal("mix_done")
        mix_var = signal("mix_var")
        mix_eps = signal("mix_eps", 2)
        mix_rstd = signal("mix_rstd", 2)
        x1_ready = signal("x1_ready")

        x1_transposed = signal("x1_transposed")
        x1_t_ready = signal("x1_t_ready")
        logits_done = signal("logits_done")
        r_exp_ready = signal("r_exp_ready")
        dist_ready = signal("dist_ready")
        fall_ready = signal("fall_ready", 2)
        weights_ready = signal("weights_ready")
        gu_done = signal("gu_done", EXPERTS)
        e_silu_ready = signal("e_silu_ready", EXPERTS)
        e_w_ready = signal("e_w_ready", EXPERTS)
        e_turned = signal("e_turned", EXPERTS)
        e_h_ready = signal("e_h_ready", EXPERTS)
        expert_out = signal("expert_out", EXPERTS)
        mid_var = signal("mid_var", 2)
        mid_eps = signal("mid_eps", 4)
        mid_rstd = signal("mid_rstd", 4)
        pick_var = signal("pick_var")
        pick_eps = signal("pick_eps", 2)
        pick_rstd = signal("pick_rstd", 2)
        x2_ready = signal("x2_ready")
        x2_transposed = signal("x2_transposed")
        x2_t_ready = signal("x2_t_ready")
        qkv_done = signal("qkv_done")
        qkv_ready = signal("qkv_ready", 3)
        scores_done = signal("scores_done")
        probs_ready = signal("probs_ready")
        attn_done = signal("attn_done")
        attn_read = signal("attn_read")
        x3_ready = signal("x3_ready")
        x3_transposed = signal("x3_transposed")
        x3_t_ready = signal("x3_t_ready")
        sim_done = signal("sim_done", 2 * H)
        sim_ready = signal("sim_ready", 2 * H)
        dots_done = signal("dots_done", BLOCKS // 2)
        dots_ready = signal("dots_ready", BLOCKS // 2)
        mlp_done = signal("mlp_done", INTER // P)
        m_silu_ready = signal("m_silu_ready", INTER // P)
        m_h_ready = signal("m_h_ready", INTER // P)
        score_d_ready = signal("score_d_ready")
        score_e_ready = signal("score_e_ready")
        picks_ready = signal("picks_ready", H)
        spread_done = signal("spread_done", H * QUADS)
        coef_ready = signal("coef_ready", H * QUADS)
        peer_done = signal("peer_done")
        x4_ready = signal("x4_ready")
        stored = signal("stored", 16)

        vec_a = Steps(ctx.enter_context(nc.semaphore("vector_mixer_steps")), 3)
        vec_b = Steps(ctx.enter_context(nc.semaphore("vector_middle_steps")), VEC_MIDDLE)
        vec_c = Steps(ctx.enter_context(nc.semaphore("vector_picks_steps")), VEC_PICKS)
        act_a = Steps(ctx.enter_context(nc.semaphore("scalar_mixer_steps")), 2)

        def load(eng, group, pairs):
            sem = ctx.enter_context(nc.semaphore("loaded_" + group))
            for dst, src in pairs:
                eng.dma_start(dst, src).then_inc(sem, 16)
            loads[group] = (sem, 16 * len(pairs))

        def row(v, width, start=0):
            return v[start:start + width].partition_broadcast(P)

        def column(v):
            return v.rearrange("(p a) -> p a", a=1)

        block = ctx.enter_context(nc.Block())

        @block.sync
        def _(sp):
            sp.dma_start(x_in[:], d["x"][0].rearrange("(h p) n -> p h n", p=P)).then_inc(x_loaded.sem, 16)
            load(sp, "conv", [
                (ident[:], d["ident"]), (w_in[:], d["W_in"]),
                (taps[:, :, 0:P], d["conv_x_w"].partition_broadcast(P)),
                (taps[:, :, P:2 * P], d["conv_z_w"].partition_broadcast(P)),
                (conv_b[:, 0:1], column(d["conv_x_b"])), (conv_b[:, 1:2], column(d["conv_z_b"])),
            ])
            load(sp, "attention", [
                (wq[:], d["A_Wq_t"]), (wk[:], d["A_Wk_t"]), (wv[:], d["A_Wv_t"]),
                (bq[:], column(d["bq"])), (bk[:], column(d["bk"])),
                (bv[0:1], d["bv"].rearrange("(a n) -> a n", a=1)),
                (gamma[:], row(d["gamma"], 1)), (diagonal[:], d["diagonal"]),
            ])
            load(sp, "moe", [
                (moe_gu[:, :, 0], d["moe_Wg"].rearrange("e p i -> p e i")),
                (moe_gu[:, :, 1], d["moe_Wu"].rearrange("e p i -> p e i")),
                (moe_d[:], d["moe_Wd"].rearrange("e p i -> p e i")),
                (w_route[:], d["Wr"]), (temperature[:], row(d["temperature"], 1)),
                (iota8[:], d["iota8"]),
            ])

            load(sp, "peer", [
                (peer_q[0:RANK], d["Wq_p"].rearrange("c n k -> n c k")),
                (peer_keys[0:RANK], d["keys_p"].rearrange("c n k -> n c k")),
                (w_down[:], d["down_t"]),
                (w_up[:], d["up_embed"].rearrange("(a p) n -> p a n", p=P)),
                (mlp_g[:], d["M_Wg_t"]), (mlp_u[:], d["M_Wu_t"]),
                (mlp_d[:], d["M_Wd_t"].rearrange("(a p) n -> p a n", p=P)),
                (expert_lo[:], d["expert_lo"]), (expert_hi[:], d["expert_hi"]),
                (quad_base[:], d["quad_base"]), (iota_16[:], d["iota_16"]),
            ])

            def fetch(b):
                sp.wait_ge(x_transposed.sem, x_transposed.at(b, 0))
                sp.dma_start(x_in[:], d["x"][b].rearrange("(h p) n -> p h n", p=P)).then_inc(x_loaded.sem, 16)

            def store(b):
                sp.wait_ge(x4_ready.sem, x4_ready.at(b))
                sp.dma_start(out[b].rearrange("(h p) n -> p h n", p=P), x4[:]).then_inc(stored.sem, 16)

            for b in range(1, 4):
                fetch(b)
            store(0)
            with sp.Fori(1, NB - 3) as i:
                fetch(i + 3)
                store(i)
            for b in range(NB - 3, NB):
                store(b)
            sp.wait_ge(stored.sem, stored.at(NB - 1))

        @block.gpsimd
        def _(pool):
            pool.memset(ones[:], 1.0).then_inc(consts_pool.sem, 1)
            pool.memset(zero_row[:], 0.0).then_inc(consts_pool.sem, 1)
            pool.memset(zero[:], 0.0).then_inc(consts_pool.sem, 1)
            pool.memset(v_1[:], 1.0).then_inc(consts_pool.sem, 1)
            pool.memset(eps_ln[:], LN_EPS).then_inc(consts_pool.sem, 1)
            pool.memset(minus_half[:], -0.5).then_inc(consts_pool.sem, 1)
            pool.wait_ge(consts_pool.sem, consts_pool.at(0))

            def mixer(b, slot):
                for c in due(SCAN, slot):
                    if c == 0:
                        continue
                    pool.wait_ge(c_used.sem, c_used.at(b, c + 1))
                    if c == 1:
                        pool.wait_ge(y_summed.sem, y_summed.at(b, 0))
                        pool.tensor_tensor(y_pair[:], state_c[:, 0], state_c[:, 1], ALU.add).then_inc(pair_added.sem, 1)
                    else:
                        pool.wait_ge(pair_added.sem, pair_added.at(b, c - 1))
                        pool.tensor_tensor(y_pair[:], y_pair[:], state_c[:, c % RING], ALU.add)\
                            .then_inc(pair_added.sem, 1)
                if slot == SCAN[-1]:
                    pool.wait_ge(pair_added.sem, pair_added.at(b))
                    pool.wait_ge(mix_done.sem, mix_done.at(b, 0))
                    pool.tensor_tensor(y_sum[:], y_pair[:, 0:T], y_pair[:, T:2 * T], ALU.add)\
                        .then_inc(y_summed.sem, 1)
                if slot == MIX_VAR:
                    _, mean_var, var_eps, minus_mean, rstd, shift = norm_a
                    pool.wait_ge(mix_var.sem, mix_var.at(b))
                    pool.tensor_tensor(minus_mean[:], zero[:], mean_var[:, :, 0], ALU.subtract).then_inc(mix_eps.sem, 1)
                    pool.tensor_tensor(var_eps[:], mean_var[:, :, 1], eps_ln[:], ALU.add).then_inc(mix_eps.sem, 1)
                    pool.wait_ge(mix_eps.sem, mix_eps.at(b))
                    pool.tensor_tensor(rstd[:], var_eps[:], minus_half[:], ALU.pow).then_inc(mix_rstd.sem, 1)
                    pool.wait_ge(mix_rstd.sem, mix_rstd.at(b, 1))
                    pool.tensor_tensor(shift[:], minus_mean[:], rstd[:], ALU.mult).then_inc(mix_rstd.sem, 1)

            def middle(b, slot):
                if slot in (MOE_VAR, ATTN_VAR):
                    k = 1 if slot == MOE_VAR else 2
                    _, mean_var, var_eps, minus_mean, rstd, shift = norm_b
                    pool.wait_ge(mid_var.sem, mid_var.at(b, k))
                    pool.tensor_tensor(minus_mean[:], zero[:], mean_var[:, :, 0], ALU.subtract).then_inc(mid_eps.sem, 1)
                    pool.tensor_tensor(var_eps[:], mean_var[:, :, 1], eps_ln[:], ALU.add).then_inc(mid_eps.sem, 1)
                    pool.wait_ge(mid_eps.sem, mid_eps.at(b, 2 * k))
                    pool.tensor_tensor(rstd[:], var_eps[:], minus_half[:], ALU.pow).then_inc(mid_rstd.sem, 1)
                    pool.wait_ge(mid_rstd.sem, mid_rstd.at(b, 2 * k - 1))
                    pool.tensor_tensor(shift[:], minus_mean[:], rstd[:], ALU.mult).then_inc(mid_rstd.sem, 1)

            def picks(b, slot):
                if slot == PICKS_VAR:
                    _, mean_var, var_eps, minus_mean, rstd, shift = norm_c
                    pool.wait_ge(pick_var.sem, pick_var.at(b))
                    pool.tensor_tensor(minus_mean[:], zero[:], mean_var[:, :, 0], ALU.subtract).then_inc(pick_eps.sem, 1)
                    pool.tensor_tensor(var_eps[:], mean_var[:, :, 1], eps_ln[:], ALU.add).then_inc(pick_eps.sem, 1)
                    pool.wait_ge(pick_eps.sem, pick_eps.at(b))
                    pool.tensor_tensor(rstd[:], var_eps[:], minus_half[:], ALU.pow).then_inc(pick_rstd.sem, 1)
                    pool.wait_ge(pick_rstd.sem, pick_rstd.at(b, 1))
                    pool.tensor_tensor(shift[:], minus_mean[:], rstd[:], ALU.mult).then_inc(pick_rstd.sem, 1)

            steps = {stage: dict(mixer=mixer, middle=middle, picks=picks)[stage] for stage in DVE_ORDER}
            weave(steps, -FIRST_ROUND, NB)
            fill(steps, NB)
            run_and_drain(pool, steps, NB)

        @block.scalar
        def _(act):
            def copy(dst, src):
                return act.activation(dst, src, ACT.Copy)

            def normalize(x, r, norm, ready):
                rstd, shift = norm[4:]
                for h in range(H):
                    last = act.activation(x[:, h], r[:, h], ACT.Identity, bias=shift[:, h:h + 1], scale=rstd[:, h:h + 1])
                last.then_inc(ready.sem, 1)

            def mixer(b, slot):
                act_a.at(b)
                if slot == 0:
                    act.wait_ge(x_transposed.sem, x_transposed.at(b))
                    copy(x_t[:, 1:T + 1], b_ps[:, 0:T]).then_inc(x_t_ready.sem, 1)
                if slot == CONV:
                    act.wait_ge(conv_done.sem, conv_done.at(b))
                    for half, dst in ((0, xs), (1, z)):
                        act.activation(dst[:], c_ps[:, half * T:(half + 1) * T], ACT.Silu,
                                       bias=conv_b[:, half:half + 1]).then_inc(xz_ready.sem, 1)
                if slot == PROJ:
                    act.wait_ge(proj_done.sem, proj_done.at(b))
                    copy(dt_low[0:RANK], b_ps[0:RANK, T:2 * T]).then_inc(dt_low_ready.sem, 1)
                    copy(bc_hi[0:96], b_ps[0:96, 0:T]).then_inc(bc_hi_ready.sem, 1)
                    act.wait_ge(c_ready.sem, c_ready.at(b, 0))
                    copy(bc_parts[0:32], b_ps[0:32, 0:T]).then_inc(bc_hi_ready.sem, 1)
                if slot == DT:
                    act.wait_ge(dt_done.sem, dt_done.at(b))
                    act.activation(dt_sum[:], c_ps[:, 0:T], ACT.Identity, bias=inv_dt2[:]).then_inc(dt_sum_ready.sem, 1)
                    act.wait_ge(dt_sum_ready.sem, dt_sum_ready.at(b))
                    act_a.begin()
                    act.activation(dt_pos[:], dt_sum[:], ACT.Relu).then_inc(dt_log_ready.sem, 1)
                    act.activation(dt_soft[:], dt_sum[:], ACT.Abs).then_inc(act_a.sem, act_a.step())
                    act.wait_ge(act_a.sem, act_a.count())
                    act.activation(dt_soft[:], dt_soft[:], ACT.Exp, scale=-1.0).then_inc(act_a.sem, act_a.step())
                    act.wait_ge(act_a.sem, act_a.count())
                    act.activation(dt_soft[:], dt_soft[:], ACT.Ln, bias=1.0).then_inc(dt_log_ready.sem, 1)
                    act_a.end()
                if slot == PROJ + 1:
                    act.wait_ge(bc_rest_ready.sem, bc_rest_ready.at(b))
                    copy(bc_mid[64:96], bc_rest[64:96]).then_inc(bc_mid_ready.sem, 1)
                    copy(bc_parts[32:64], bc_rest[32:64]).then_inc(bc_mid_ready.sem, 1)
                if slot == DECAYS:
                    act.wait_ge(delta_ready.sem, delta_ready.at(b))
                    act.wait_ge(scanned.sem, scanned.at(b, 0))
                    for n in range(STATES):
                        act.activation(dA[:, n, 1:T], delta[:, 1:T], ACT.Exp, scale=-float(n + 1))\
                            .then_inc(dA_ready.sem, 1)

                if slot == MIX_NORM:
                    act.wait_ge(mix_rstd.sem, mix_rstd.at(b))
                    act.wait_ge(x1_transposed.sem, x1_transposed.at(b, 0))
                    normalize(x1, b_tiles, norm_a, x1_ready)

            def middle(b, slot):
                if slot == 0:
                    act.wait_ge(x1_transposed.sem, x1_transposed.at(b))
                    copy(x1_t[:], mid_acc[:, 0:T]).then_inc(x1_t_ready.sem, 1)
                if slot == LOGITS:
                    act.wait_ge(logits_done.sem, logits_done.at(b))
                    act.activation(r_exp[:].rearrange("p h e -> p (h e)"), mid_acc[:, 0:8 * H], ACT.Exp,
                                   scale=neg_inv_temp[:]).then_inc(r_exp_ready.sem, 1)
                if slot == FALLOFF:
                    act.wait_ge(dist_ready.sem, dist_ready.at(b))
                    act.activation(near[:], dist[:], ACT.Exp, scale=-1.0 / 0.1).then_inc(fall_ready.sem, 1)
                    act.activation(fall[:], dist[:], ACT.Exp, scale=-1.0 / 0.3).then_inc(fall_ready.sem, 1)
                for e in due(EXPERT_ACT, slot):
                    act.wait_ge(gu_done.sem, gu_done.at(b, e + 1))
                    act.wait_ge(e_w_ready.sem, e_w_ready.at(b, max(e - 1, 0)))
                    act.activation(e_silu[:, e % 2], mid_tiles[e % 2][:, :, 0], ACT.Silu).then_inc(e_silu_ready.sem, 1)
                for e in due(EXPERT_TURN, slot):
                    act.wait_ge(e_turned.sem, e_turned.at(b, e + 1))
                    act.wait_ge(expert_out.sem, expert_out.at(b, max(e - E_RING + 1, 0)))
                    copy(e_h[:, e % E_RING], mid[e % 2][:, 0:T]).then_inc(e_h_ready.sem, 1)
                if slot == MOE_NORM:
                    act.wait_ge(mid_rstd.sem, mid_rstd.at(b, 2))
                    act.wait_ge(attn_read.sem, attn_read.at(b, 0))
                    normalize(x2, mid_acc_tiles, norm_b, x2_ready)
                if slot == X2_TURN:
                    act.wait_ge(x2_transposed.sem, x2_transposed.at(b))
                    copy(x2_t[:], mid[0][:, 0:T]).then_inc(x2_t_ready.sem, 1)
                if slot == QKV:
                    act.wait_ge(qkv_done.sem, qkv_done.at(b))
                    act.activation(q_t[:], mid[1][:, 0:T], ACT.Relu, bias=bq[:]).then_inc(qkv_ready.sem, 1)
                    act.activation(k_t[:], mid[1][:, T:2 * T], ACT.Relu, bias=bk[:]).then_inc(qkv_ready.sem, 1)
                    copy(v_1[:, :, 0:P], mid[0][:, 0:T].rearrange("p (h n) -> p h n", h=H)).then_inc(qkv_ready.sem, 1)

                if slot == ATTN_NORM:
                    act.wait_ge(mid_rstd.sem, mid_rstd.at(b, 4))
                    act.wait_ge(x3_transposed.sem, x3_transposed.at(b, 0))
                    normalize(x3, mid_sum, norm_b, x3_ready)

            def picks(b, slot):
                if slot == 0:
                    act.wait_ge(x3_transposed.sem, x3_transposed.at(b))
                    copy(x3_t[:], pick_ps[1][:, 0:T]).then_inc(x3_t_ready.sem, 1)
                for n in due(SIM, slot):
                    h, half = divmod(n, 2)
                    act.wait_ge(sim_done.sem, sim_done.at(b, 2 * h + half + 1))
                    copy(sim[:, h, HEADS * half:HEADS * (half + 1)],
                         pick_ps[half][:].rearrange("p (c k) -> p c k", c=HEADS)).then_inc(sim_ready.sem, 1)
                for c in due(DOTS, slot):
                    act.wait_ge(dots_done.sem, dots_done.at(b, c + 1))
                    if c == 0:
                        act.wait_ge(peer_done.sem, peer_done.at(b, 0))
                    act.activation(dots[:, 2 * c:2 * c + 2], pick_ps[c % 2][:].rearrange("p (a t) -> p a t", a=2),
                                   ACT.Silu).then_inc(dots_ready.sem, 1)
                for j in due(MLP_IN, slot):
                    act.wait_ge(mlp_done.sem, mlp_done.at(b, j + 1))
                    act.activation(m_silu[:, j % 2], pick_ps[j % 2][:, 0:T], ACT.Silu).then_inc(m_silu_ready.sem, 1)
                if slot == NAME_EXPERTS:
                    act.wait_ge(score_d_ready.sem, score_d_ready.at(b))
                    act.activation(score_e[:], score_d[:], ACT.Exp).then_inc(score_e_ready.sem, 1)

                if slot == PICKS_NORM:
                    act.wait_ge(pick_rstd.sem, pick_rstd.at(b))
                    act.wait_ge(stored.sem, stored.at(b, 0))
                    normalize(x4, pick_tiles, norm_c, x4_ready)

            load(act, "mixer", [
                (w_dt_low[:], d["W_xdbl"][:, 0:RANK]),
                (w_bc3[:, 0], d["W_xdbl"][:, RANK:RANK + 2 * STATES]),
                (w_bc3[:, 1], d["W_xdbl"][:, RANK:RANK + 2 * STATES]),
                (w_bc3[:, 2], d["W_xdbl"][:, RANK:RANK + 2 * STATES]),
                (w_dt[0:RANK], d["W_dt"]), (inv_dt[:], column(d["inv_dt"])),
                (skip_d[:], column(d["D"])),
                (w_out[:], d["W_out"].rearrange("(a p) n -> p a n", p=P)),
                (b_out[0:1], d["b_out"].rearrange("(a n) -> a n", a=1)),
                (pick_state[0:6 * STATES], d["pick_state"]),
            ])
            act.wait_ge(*loads["conv"])
            act.wait_ge(consts_vec.sem, consts_vec.at(0))
            steps = {stage: dict(mixer=mixer, middle=middle, picks=picks)[stage] for stage in ACT_ORDER}
            weave(steps, -FIRST_ROUND, NB)
            act.wait_ge(map_ps.sem, map_ps.at(0))
            copy(key_map[:, 0:HEADS], pick_ps[0][:].rearrange("p (c k) -> p c k", c=HEADS)).then_inc(map_copied.sem, 1)
            copy(key_map[:, HEADS:2 * HEADS], pick_ps[1][:].rearrange("p (c k) -> p c k", c=HEADS))\
                .then_inc(map_copied.sem, 1)
            act.wait_ge(made.sem, made.at(0))
            fill(steps, NB)
            run_and_drain(act, steps, NB)

        @block.tensor
        def _(pe):
            def mm(dst, lhs, rhs, start=True, stop=True):
                return pe.matmul(dst, lhs, rhs, start=start, stop=stop)

            def to_columns(dst, x):
                for h in range(H):
                    last = pe.transpose(dst[:, h * P:(h + 1) * P], x[:, h], ident[:])
                return last

            def spread_b(c):
                for n in range(2):
                    last = mm(b_ps[:, n * T:(n + 1) * T], pick_state[0:96, 2 * c + n], bc_parts[0:96])
                return last

            def mixer(b, slot):
                if slot == 0:
                    pe.wait_ge(x_loaded.sem, x_loaded.at(b))
                    pe.wait_ge(x1_ready.sem, x1_ready.at(b, 0))
                    to_columns(b_ps, x_in).then_inc(x_transposed.sem, 1)
                if slot == CONV:
                    pe.wait_ge(x_t_ready.sem, x_t_ready.at(b))
                    pe.wait_ge(c_used.sem, c_used.at(b, 0))
                    for half in range(2):
                        for k in range(TAPS):
                            last = mm(c_ps[:, half * T:(half + 1) * T], w_conv[:, k, half * P:(half + 1) * P],
                                      x_t[:, k:k + T], start=k == 0, stop=k == TAPS - 1)
                    last.then_inc(conv_done.sem, 1)
                if slot == PROJ:
                    pe.wait_ge(xz_ready.sem, xz_ready.at(b))
                    mm(b_ps[0:96, 0:T], w_bc3[:].rearrange("p a n -> p (a n)"), xs[:])
                    mm(b_ps[0:RANK, T:2 * T], w_dt_low[:], xs[:]).then_inc(proj_done.sem, 1)
                if slot == DT:
                    pe.wait_ge(dt_low_ready.sem, dt_low_ready.at(b))
                    mm(c_ps[:, 0:T], w_dt[0:RANK], dt_low[0:RANK]).then_inc(dt_done.sem, 1)
                for c in due(SCAN, slot + 1):
                    if c == 0:
                        pe.wait_ge(dt_sum_ready.sem, dt_sum_ready.at(b))
                        pe.wait_ge(bc_parts_ready.sem, bc_parts_ready.at(b))
                        spread_b(0).then_inc(b_ready.sem, 1)
                    pe.wait_ge(c_used.sem, c_used.at(b, c))
                    for n in range(2):
                        last = mm(c_ps[:, n * T:(n + 1) * T], pick_state[0:96, STATES + 2 * c + n], bc_parts[0:96])
                    last.then_inc(c_ready.sem, 1)
                    if c + 1 < STATES // 2:
                        pe.wait_ge(b_used.sem, b_used.at(b, c + 1))
                        spread_b(c + 1).then_inc(b_ready.sem, 1)
                if slot == MIX_OUT:
                    pe.wait_ge(y_summed.sem, y_summed.at(b))
                    for h in range(H):
                        at = b_ps[:, h * P:(h + 1) * P]
                        mm(at, y_sum[:, h * P:(h + 1) * P], w_out[:, 0], stop=False)
                        mm(at, xs[:, h * P:(h + 1) * P], w_skip[:], start=False, stop=False)
                        mm(at, x_t[:, h * P + 1:(h + 1) * P + 1], ident[:], start=False, stop=False)
                        mm(at, z[:, h * P:(h + 1) * P], w_out[:, 1], start=False, stop=False)
                        last = mm(at, ones[0:1], b_out[0:1], start=False)
                    last.then_inc(mix_done.sem, 1)

            def middle(b, slot):
                if slot == 0:
                    pe.wait_ge(x1_ready.sem, x1_ready.at(b))
                    pe.wait_ge(probs_ready.sem, probs_ready.at(b, 0))
                    to_columns(mid_acc, x1).then_inc(x1_transposed.sem, 1)
                if slot == LOGITS:
                    pe.wait_ge(x1_t_ready.sem, x1_t_ready.at(b))
                    for h in range(H):
                        last = mm(mid_acc[:, 8 * h:8 * h + 8], x1_t[:, h * P:(h + 1) * P], w_route[:])
                    last.then_inc(logits_done.sem, 1)
                for e in due(EXPERT_IN, slot):
                    if e == 0:
                        pe.wait_ge(x1_t_ready.sem, x1_t_ready.at(b))
                    if e < 2:
                        pe.wait_ge(attn_read.sem, attn_read.at(b, 0))
                    else:
                        pe.wait_ge(e_h_ready.sem, e_h_ready.at(b, e - 1))
                    for h in range(H):
                        last = mm(mid[e % 2][:, h * 2 * P:(h + 1) * 2 * P], x1_t[:, h * P:(h + 1) * P],
                                  moe_gu[:, e].rearrange("p a n -> p (a n)"))
                    last.then_inc(gu_done.sem, 1)
                for e in due(EXPERT_TURN, slot):
                    pe.wait_ge(e_w_ready.sem, e_w_ready.at(b, e + 1))
                    to_columns(mid[e % 2], e_w[:, e % 2]).then_inc(e_turned.sem, 1)
                for e in due(EXPERT_OUT, slot):
                    if e == 0:
                        pe.wait_ge(r_exp_ready.sem, r_exp_ready.at(b))
                        mm(mid_acc[:, 0:T], zero_row[0:1, 0:P], zero_row[0:1], stop=False)
                        for h in range(H):
                            mm(mid_acc[:, h * P:(h + 1) * P], x1_t[:, h * P:(h + 1) * P], ident[:],
                               start=False, stop=False)
                    pe.wait_ge(e_h_ready.sem, e_h_ready.at(b, e + 1))
                    for h in range(H):
                        last = mm(mid_acc[:, h * P:(h + 1) * P], e_h[:, e % E_RING, h * P:(h + 1) * P], moe_d[:, e],
                                  start=False, stop=e == EXPERTS - 1 and h == H - 1)
                    last.then_inc(expert_out.sem, 1)
                if slot == X2_TURN:
                    pe.wait_ge(x2_ready.sem, x2_ready.at(b))
                    to_columns(mid[0], x2).then_inc(x2_transposed.sem, 1)
                if slot == QKV:
                    pe.wait_ge(x2_t_ready.sem, x2_t_ready.at(b))
                    mm(mid[1][:, 0:T], wq[:], x2_t[:])
                    mm(mid[1][:, T:2 * T], wk[:], x2_t[:])
                    for h in range(H):
                        at = mid[0][:, h * P:(h + 1) * P]
                        mm(at, x2_t[:, h * P:(h + 1) * P], wv[:], stop=False)
                        last = mm(at, ones[0:1], bv[0:1], start=False)
                    last.then_inc(qkv_done.sem, 1)
                if slot == SCORES:
                    pe.wait_ge(qkv_ready.sem, qkv_ready.at(b))
                    mm(mid_acc[:, 0:T], k_t[:, 0:P], q_t[:])
                    mm(mid_acc[:, T:T + P], k_t[:, P:T], q_t[:, P:T]).then_inc(scores_done.sem, 1)
                if slot == ATTEND:
                    pe.wait_ge(probs_ready.sem, probs_ready.at(b))
                    mm(mid[0][:, 0:P + 1], probs[:, 0:P], v_1[:, 0])
                    mm(mid[0][:, T:T + P + 1], probs[:, P:T], v_1[:, 0], stop=False)
                    mm(mid[0][:, T:T + P + 1], probs[:, T:T + P], v_1[:, 1], start=False).then_inc(attn_done.sem, 1)

            def spread(b, n):
                h, q = divmod(n, QUADS)
                if n % QUADS == 0:
                    pe.wait_ge(picks_ready.sem, picks_ready.at(b, h + 1))
                if n < 2:
                    pe.wait_ge(m_h_ready.sem, m_h_ready.at(b, n + 3))
                else:
                    pe.wait_ge(coef_ready.sem, coef_ready.at(b, n - 1))
                for g in range(GROUPS // QUADS):
                    at = pick_ps[n % 2][:, g * 64:(g + 1) * 64]
                    token = q * (GROUPS // QUADS) + g
                    mm(at, hot_lo[:, :, token], pick_hi[:, :, token], stop=False)
                    last = mm(at, hot_lo[:, :, token], pick_lo[:, :, token], start=False)
                last.then_inc(spread_done.sem, 1)

            def sum_residual(h):
                mm(pick_sum[:, h * P:(h + 1) * P], x3_t[:, h * P:(h + 1) * P], ident[:], stop=False)

            def sum_experts(h, first):
                for a in range(first, first + 4):
                    last = mm(pick_sum[:, h * P:(h + 1) * P], dots[:, a, h * P:(h + 1) * P], w_up[:, a], start=False,
                              stop=a == BLOCKS - 1)
                return last

            def sum_mlp(h):
                for j in range(INTER // P):
                    mm(pick_sum[:, h * P:(h + 1) * P], m_h[:, j, h * P:(h + 1) * P], mlp_d[:, j], start=False, stop=False)

            def picks(b, slot):
                if slot == 0:
                    pe.wait_ge(x3_ready.sem, x3_ready.at(b))
                    pe.wait_ge(coef_ready.sem, coef_ready.at(b, 0))
                    to_columns(pick_ps[1], x3).then_inc(x3_transposed.sem, 1)
                for n in due(SIM, slot):
                    h, half = divmod(n, 2)
                    if n == 0:
                        pe.wait_ge(x3_t_ready.sem, x3_t_ready.at(b))
                    if n >= 2:
                        pe.wait_ge(sim_ready.sem, sim_ready.at(b, n - 1))
                    mm(pick_ps[half][:], x3_t[:, h * P:(h + 1) * P],
                       key_map[:, HEADS * half:HEADS * (half + 1)].rearrange("p c k -> p (c k)"))\
                        .then_inc(sim_done.sem, 1)
                for c in due(DOTS, slot):
                    if c < 2:
                        pe.wait_ge(sim_ready.sem, sim_ready.at(b, c + 3))
                    else:
                        pe.wait_ge(dots_ready.sem, dots_ready.at(b, c - 1))
                    for a in (2 * c, 2 * c + 1):
                        last = mm(pick_ps[c % 2][:, (a % 2) * T:(a % 2 + 1) * T], w_down[:, a * P:(a + 1) * P], x3_t[:])
                    last.then_inc(dots_done.sem, 1)
                for j in due(MLP_IN, slot):
                    if j < 2:
                        pe.wait_ge(dots_ready.sem, dots_ready.at(b, BLOCKS // 2 - 1 + j))
                    else:
                        pe.wait_ge(m_h_ready.sem, m_h_ready.at(b, j - 1))
                    mm(pick_ps[j % 2][:, 0:T], mlp_g[:, j * P:(j + 1) * P], x3_t[:])
                    mm(pick_ps[j % 2][:, T:2 * T], mlp_u[:, j * P:(j + 1) * P], x3_t[:]).then_inc(mlp_done.sem, 1)
                for n in due(SPREAD, slot):
                    spread(b, n)
                for h in due(SUM_START, slot):
                    if h == 0:
                        pe.wait_ge(m_h_ready.sem, m_h_ready.at(b))
                        pe.wait_ge(x4_ready.sem, x4_ready.at(b, 0))
                    sum_residual(h)
                    sum_mlp(h)
                for n in due(SUM_EXPERTS, slot):
                    h, part = divmod(n, 4)
                    if part == 0:
                        pe.wait_ge(coef_ready.sem, coef_ready.at(b, (h + 1) * QUADS))
                    last = sum_experts(h, part * 4)
                    if n == 7:
                        last.then_inc(peer_done.sem, 1)

            pe.wait_ge(*loads["conv"])
            pe.wait_ge(*loads["mixer"])
            pe.wait_ge(consts_vec.sem, consts_vec.at(0))
            pe.wait_ge(consts_pool.sem, consts_pool.at(0))
            steps = {stage: dict(mixer=mixer, middle=middle, picks=picks)[stage] for stage in PE_ORDER}
            weave(steps, -FIRST_ROUND, NB)
            pe.wait_ge(*loads["peer"])
            for part in range(2):
                for c in range(HEADS):
                    n = part * HEADS + c
                    last = mm(pick_ps[part][:, c * KEYS:(c + 1) * KEYS], peer_q[0:RANK, n], peer_keys[0:RANK, n])
                last.then_inc(map_ps.sem, 1)
            pe.wait_ge(map_copied.sem, map_copied.at(0))
            pe.wait_ge(*loads["moe"])
            pe.wait_ge(*loads["attention"])
            fill(steps, NB)
            run_and_drain(pe, steps, NB)

        @block.vector
        def _(vec):
            def wide(x, n):
                return x.unsqueeze(len(x.shape)).broadcast_to(list(x.shape) + [n])

            def normalize_in(own, r, norm, ready):
                st, mv = norm[:2]
                for h in range(H):
                    vec.bn_stats(st[:, h], r[:, h]).then_inc(own.sem, own.step())
                yield
                vec.wait_ge(own.sem, own.count())
                vec.sem_inc(passed.sem, 1)
                vec.bn_aggr(mv[:, 0], st[:, 0]).then_inc(own.sem, own.step())
                vec.bn_aggr(mv[:, 1], st[:, 1]).then_inc(ready.sem, 1)

            def scan_input(b, c):
                vec.wait_ge(b_ready.sem, b_ready.at(b, c + 1))
                vec.wait_ge(du_ready.sem, du_ready.at(b))
                vec.tensor_tensor(dBu[:, c % 2].rearrange("p (n t) -> p n t", n=2),
                                  b_ps[:].rearrange("p (n t) -> p n t", n=2),
                                  du[:].unsqueeze(1).broadcast_to([P, 2, T]), ALU.mult).then_inc(b_used.sem, 1)

            def mixer(b, slot):
                own = vec_a
                own.at(b)
                if slot == PROJ + 1:
                    vec.wait_ge(bc_hi_ready.sem, bc_hi_ready.at(b))
                    vec.tensor_tensor(bc_rest[0:96], b_ps[0:96, 0:T], bc_hi[0:96], ALU.subtract)\
                        .then_inc(bc_rest_ready.sem, 1)
                if slot == DELTA:
                    vec.wait_ge(bc_mid_ready.sem, bc_mid_ready.at(b))
                    vec.tensor_tensor(bc_parts[64:96], bc_rest[64:96], bc_mid[64:96], ALU.subtract)\
                        .then_inc(bc_parts_ready.sem, 1)
                    vec.wait_ge(dt_log_ready.sem, dt_log_ready.at(b))
                    vec.tensor_tensor(delta[:], dt_pos[:], dt_soft[:], ALU.add).then_inc(delta_ready.sem, 1)
                    yield
                    vec.wait_ge(delta_ready.sem, delta_ready.at(b))
                    vec.tensor_tensor(du[:], delta[:], xs[:], ALU.mult).then_inc(du_ready.sem, 1)
                if slot + 1 == SCAN[0]:
                    scan_input(b, 0)
                for c in due(SCAN, slot):
                    vec.wait_ge(dA_ready.sem, dA_ready.at(b, 2 * c + 2))
                    vec.wait_ge(b_used.sem, b_used.at(b, c + 1))
                    vec.wait_ge(c_used.sem, c_used.at(b, c))
                    vec.tensor_tensor_scan(state[:], dA[:, 2 * c:2 * c + 2].rearrange("p n t -> p (n t)"),
                                           dBu[:, c % 2], 0.0, ALU.mult, ALU.add).then_inc(scanned.sem, 1)
                    yield
                    if c + 1 < STATES // 2:
                        scan_input(b, c + 1)
                        yield
                    vec.wait_ge(c_ready.sem, c_ready.at(b, c + 1))
                    if c == 0:
                        vec.wait_ge(y_summed.sem, y_summed.at(b, 0))
                    if c >= RING:
                        vec.wait_ge(pair_added.sem, pair_added.at(b, max(c - RING, 1)))
                    vec.wait_ge(scanned.sem, scanned.at(b, c + 1))
                    vec.tensor_tensor(state_c[:, c % RING], state[:], c_ps[:], ALU.mult).then_inc(c_used.sem, 1)
                if slot == MIX_VAR:
                    own.begin()
                    vec.wait_ge(mix_done.sem, mix_done.at(b))
                    yield from normalize_in(own, b_tiles, norm_a, mix_var)
                    own.end()

            def middle(b, slot):
                own = vec_b
                own.at(b)
                if slot == DISTANCES:
                    own.begin()
                    vec.wait_ge(r_exp_ready.sem, r_exp_ready.at(b))
                    vec.tensor_scalar(r_exp1[:], r_exp[:], 1.0, None, ALU.add).then_inc(own.sem, own.step())
                    yield
                    vec.wait_ge(own.sem, own.count())
                    vec.reciprocal(inh[:], r_exp1[:]).then_inc(own.sem, own.step())
                    yield
                    vec.wait_ge(own.sem, own.count())
                    vec.tensor_scalar(off_center[:], inh[:], GOLDEN_CENTER, None, ALU.subtract)\
                        .then_inc(own.sem, own.step())
                    yield
                    vec.wait_ge(own.sem, own.count())
                    vec.scalar_tensor_tensor(dist[:], off_center[:], -1.0, off_center[:], ALU.mult, ALU.max)\
                        .then_inc(dist_ready.sem, 1)
                    vec.tensor_scalar(in_zone[:], inh[:], GOLDEN_LOWER, None, ALU.is_ge).then_inc(own.sem, own.step())
                if slot == WEIGHTS:
                    vec.wait_ge(fall_ready.sem, fall_ready.at(b))
                    vec.scalar_tensor_tensor(zone_w[:], inh[:], GOLDEN_UPPER, near[:], ALU.is_le, ALU.mult)\
                        .then_inc(own.sem, own.step())
                    yield
                    vec.wait_ge(own.sem, own.count())
                    vec.tensor_tensor(zone_w[:], zone_w[:], in_zone[:], ALU.mult).then_inc(own.sem, own.step())
                    yield
                    vec.wait_ge(own.sem, own.count())
                    vec.tensor_reduce(zone_sum[:], zone_w[:], AX, ALU.add).then_inc(own.sem, own.step())
                    for h in range(H):
                        vec.max(fall8[:, h], fall[:, h]).then_inc(own.sem, own.step())
                    yield
                    vec.wait_ge(own.sem, own.count())
                    vec.sem_inc(passed.sem, 1)
                    for h in range(H):
                        vec.max_index(fall_i[:, h], fall8[:, h], fall[:, h]).then_inc(own.sem, own.step())
                    yield
                    vec.wait_ge(own.sem, own.count())
                    vec.tensor_copy(fall_if[:], fall_i[:]).then_inc(own.sem, own.step())
                    yield
                    vec.wait_ge(own.sem, own.count())
                    numbers = iota8[:].unsqueeze(1).broadcast_to([P, H, 8])
                    vec.tensor_tensor(first[:], numbers, fall_if[:, :, 0:1].broadcast_to([P, H, 8]), ALU.is_equal)\
                        .then_inc(own.sem, own.step())
                    vec.tensor_tensor(two[:], numbers, fall_if[:, :, 1:2].broadcast_to([P, H, 8]), ALU.is_equal)\
                        .then_inc(own.sem, own.step())
                    yield
                    vec.wait_ge(own.sem, own.count())
                    vec.tensor_tensor(two[:], two[:], first[:], ALU.add).then_inc(own.sem, own.step())
                    yield
                    vec.wait_ge(own.sem, own.count())
                    vec.tensor_tensor(fb_w[:], fall[:], two[:], ALU.mult).then_inc(own.sem, own.step())
                    yield
                    vec.wait_ge(own.sem, own.count())
                    vec.tensor_reduce(fb_sum[:], fb_w[:], AX, ALU.add).then_inc(own.sem, own.step())
                    yield
                    vec.wait_ge(own.sem, own.count())
                    vec.tensor_scalar(fb_sum[:], fb_sum[:], 1e-8, None, ALU.max).then_inc(own.sem, own.step())
                    yield
                    vec.wait_ge(own.sem, own.count())
                    vec.reciprocal(fb_rec[:], fb_sum[:]).then_inc(own.sem, own.step())
                    yield
                    vec.wait_ge(own.sem, own.count())
                    vec.tensor_scalar(none_in[:], zone_sum[:], 1e-8, None, ALU.is_lt).then_inc(own.sem, own.step())
                    vec.tensor_tensor(fb_n[:], fb_w[:], wide(fb_rec[:], 8), ALU.mult).then_inc(own.sem, own.step())
                    yield
                    vec.wait_ge(own.sem, own.count())
                    vec.tensor_tensor(fb_d[:], fb_n[:], zone_w[:], ALU.subtract).then_inc(own.sem, own.step())
                    yield
                    vec.wait_ge(own.sem, own.count())
                    vec.tensor_tensor(fb_d[:], fb_d[:], wide(none_in[:], 8), ALU.mult).then_inc(own.sem, own.step())
                    yield
                    vec.wait_ge(own.sem, own.count())
                    vec.tensor_tensor(w_all[:], fb_d[:], zone_w[:], ALU.add).then_inc(own.sem, own.step())
                    yield
                    vec.wait_ge(own.sem, own.count())
                    vec.tensor_reduce(w_sum[:], w_all[:], AX, ALU.add).then_inc(own.sem, own.step())
                    yield
                    vec.wait_ge(own.sem, own.count())
                    vec.tensor_scalar(w_sum[:], w_sum[:], 1e-8, None, ALU.max).then_inc(own.sem, own.step())
                    yield
                    vec.wait_ge(own.sem, own.count())
                    vec.reciprocal(w_rec[:], w_sum[:]).then_inc(own.sem, own.step())
                    yield
                    vec.wait_ge(own.sem, own.count())
                    vec.wait_ge(e_w_ready.sem, e_w_ready.at(b, 0))
                    vec.tensor_tensor(w_tok[:], w_all[:], wide(w_rec[:], 8), ALU.mult).then_inc(weights_ready.sem, 1)
                for e in due(EXPERT_MUL, slot):
                    vec.wait_ge(e_silu_ready.sem, e_silu_ready.at(b, e + 1))
                    vec.wait_ge(e_turned.sem, e_turned.at(b, max(e - 1, 0)))
                    if e == 0:
                        vec.wait_ge(weights_ready.sem, weights_ready.at(b))
                    for h in range(H):
                        last = vec.scalar_tensor_tensor(e_w[:, e % 2, h], e_silu[:, e % 2, h], w_tok[:, h, e:e + 1],
                                                        mid_tiles[e % 2][:, h, 1], ALU.mult, ALU.mult)
                    last.then_inc(e_w_ready.sem, 1)
                    yield
                if slot == MOE_VAR:
                    vec.wait_ge(expert_out.sem, expert_out.at(b))
                    yield from normalize_in(own, mid_acc_tiles, norm_b, mid_var)
                if slot == PROBS:
                    vec.wait_ge(scores_done.sem, scores_done.at(b))
                    vec.tensor_tensor(probs[:], mid_acc[:, 0:T + P], decay[:], ALU.mult).then_inc(probs_ready.sem, 1)
                if slot == ATTN_VAR:
                    vec.wait_ge(attn_done.sem, attn_done.at(b))
                    vec.wait_ge(x2_ready.sem, x2_ready.at(b))
                    sums = mid[0][:].rearrange("p (h n) -> p h n", h=H)
                    vec.tensor_scalar(den[:], sums[:, :, P], ATTN_EPS, None, ALU.add).then_inc(own.sem, own.step())
                    yield
                    vec.wait_ge(own.sem, own.count())
                    vec.reciprocal(den_r[:], den[:]).then_inc(own.sem, own.step())
                    yield
                    vec.wait_ge(own.sem, own.count())
                    vec.wait_ge(x3_ready.sem, x3_ready.at(b, 0))
                    for h in range(H):
                        last = vec.scalar_tensor_tensor(mid_sum[:, h], sums[:, h, 0:P], den_r[:, h:h + 1], x2[:, h],
                                                        ALU.mult, ALU.add)
                    last.then_inc(attn_read.sem, 1)
                    yield
                    vec.wait_ge(attn_read.sem, attn_read.at(b))
                    yield from normalize_in(own, mid_sum, norm_b, mid_var)
                    own.end()

            def find_keys(b, h):
                own = vec_c
                vec.wait_ge(sim_ready.sem, sim_ready.at(b, 2 * h + 2))
                vec.sem_inc(passed.sem, 1)
                for c in range(2 * HEADS):
                    vec.max(top[:, h, c], sim[:, h, c]).then_inc(own.sem, own.step())
                    if c % 3 == 2:
                        yield

            def name_keys(b, h):
                own = vec_c
                yield
                vec.wait_ge(own.sem, own.count())
                vec.sem_inc(passed.sem, 1)
                for c in range(2 * HEADS):
                    vec.max_index(top_i[:, h, c], top[:, h, c], sim[:, h, c]).then_inc(own.sem, own.step())
                    if c % 3 == 2:
                        yield

            def find_pairs(b):
                own = vec_c
                for h in range(H):
                    square = [P, HEADS, TOPK, TOPK]
                    vec.tensor_tensor(pair[:, h].rearrange("p c (i j) -> p c i j", i=TOPK),
                                      top[:, h, 0:HEADS].unsqueeze(3).broadcast_to(square),
                                      top[:, h, HEADS:2 * HEADS].unsqueeze(2).broadcast_to(square), ALU.add)\
                        .then_inc(own.sem, own.step())
                yield
                vec.wait_ge(own.sem, own.count())
                vec.tensor_copy(key_16[:], top_i[:].rearrange("p h c i -> p i (h c)")).then_inc(own.sem, own.step())
                for h in range(H):
                    for c in range(HEADS):
                        vec.max(score[:, h, c], pair[:, h, c]).then_inc(own.sem, own.step())
                yield
                vec.wait_ge(own.sem, own.count())
                scores = score[:].rearrange("p h c k -> p (h c) k")
                vec.tensor_tensor(score_d[:], scores, scores[:, :, 0:1].broadcast_to([P, H * HEADS, TOPK]),
                                  ALU.subtract).then_inc(score_d_ready.sem, 1)
                for h in range(H):
                    for c in range(HEADS):
                        vec.max_index(pair_i[:, h, c], score[:, h, c], pair[:, h, c]).then_inc(own.sem, own.step())

            def name_experts(b):
                own = vec_c
                yield
                vec.wait_ge(own.sem, own.count())
                chosen = pair_i[:].rearrange("p h c k -> p k h c")
                vec.tensor_scalar(rank[:, :, :, 0], chosen, 3, None, ALU.logical_shift_right)\
                    .then_inc(own.sem, own.step())
                vec.tensor_scalar(rank[:, :, :, 1], chosen, 7, None, ALU.bitwise_and).then_inc(own.sem, own.step())
                yield
                vec.wait_ge(own.sem, own.count())
                vec.tensor_copy(rank_16[:], rank[:].rearrange("p k h a c -> p (k h a c)")).then_inc(own.sem, own.step())
                yield
                vec.wait_ge(own.sem, own.count())
                vec.tensor_tensor(rank_hot[:], iota_16[:], rank_16[:].unsqueeze(1).broadcast_to([P, TOPK, H * 2 * SLOTS]),
                                  ALU.is_equal).then_inc(own.sem, own.step())
                yield
                vec.wait_ge(own.sem, own.count())
                places = [P, TOPK, TOPK, H * 2 * HEADS]
                vec.tensor_tensor(rank_hot[:].rearrange("p i (k c) -> p i k c", k=TOPK),
                                  rank_hot[:].rearrange("p i (k c) -> p i k c", k=TOPK),
                                  key_16[:].unsqueeze(2).broadcast_to(places), ALU.mult).then_inc(own.sem, own.step())
                yield
                vec.wait_ge(own.sem, own.count())
                vec.tensor_tensor(key_sum4[:], rank_hot[:, 0:4], rank_hot[:, 4:8], ALU.add)\
                    .then_inc(own.sem, own.step())
                yield
                vec.wait_ge(own.sem, own.count())
                vec.tensor_tensor(key_sum2[:], key_sum4[:, 0:2], key_sum4[:, 2:4], ALU.add)\
                    .then_inc(own.sem, own.step())
                yield
                vec.wait_ge(own.sem, own.count())
                vec.tensor_tensor(slot_xy[:].rearrange("p k a c -> p (k a c)"), key_sum2[:, 0], key_sum2[:, 1], ALU.add)\
                    .then_inc(own.sem, own.step())
                yield
                vec.wait_ge(own.sem, own.count())
                vec.scalar_tensor_tensor(slot_e[:], slot_xy[:, :, 0], float(KEYS), slot_xy[:, :, 1], ALU.mult, ALU.add)\
                    .then_inc(own.sem, own.step())
                yield
                vec.wait_ge(own.sem, own.count())
                vec.tensor_scalar(slot_u[:], slot_e[:], float(TABLE - 1), None, ALU.min).then_inc(own.sem, own.step())
                yield
                vec.wait_ge(own.sem, own.count())
                named = slot_u[:].rearrange("p (k h) c -> p h k c", h=H)
                by_tile = slot_n[:].rearrange("p h a (k c) -> p h a k c", c=HEADS)
                vec.tensor_scalar(by_tile[:, :, 0], named, 7, None, ALU.logical_shift_right)\
                    .then_inc(own.sem, own.step())
                vec.tensor_scalar(by_tile[:, :, 1], named, P - 1, None, ALU.bitwise_and).then_inc(own.sem, own.step())

            def lay_out(b):
                own = vec_c
                yield
                vec.wait_ge(own.sem, own.count())
                vec.transpose(slot_nt[:].rearrange("p h a g -> p (h a g)"), slot_n[:].rearrange("p h a g -> p (h a g)"))\
                    .then_inc(own.sem, own.step())
                vec.wait_ge(score_e_ready.sem, score_e_ready.at(b))
                vec.tensor_reduce(score_s[:], score_e[:], AX, ALU.add).then_inc(own.sem, own.step())
                yield
                vec.wait_ge(own.sem, own.count())
                vec.reciprocal(score_r[:], score_s[:]).then_inc(own.sem, own.step())
                vec.tensor_scalar(hi_16[:], slot_nt[:, :, 0], quad_base[:], None, ALU.add).then_inc(own.sem, own.step())
                vec.tensor_copy(lo_16[:], slot_nt[:, :, 1]).then_inc(own.sem, own.step())
                yield
                vec.wait_ge(own.sem, own.count())
                by_head = slot_p[:].rearrange("p h k c -> p h c k")
                vec.tensor_tensor(by_head, score_e[:].rearrange("p (h c) k -> p h c k", h=H),
                                  wide(score_r[:].rearrange("p (h c) -> p h c", h=H), TOPK), ALU.mult)\
                    .then_inc(own.sem, own.step())
                yield
                vec.wait_ge(own.sem, own.count())
                vec.transpose(slot_pt[:].rearrange("p h g -> p (h g)"), slot_p[:].rearrange("p h k c -> p (h k c)"))\
                    .then_inc(own.sem, own.step())
                yield
                vec.wait_ge(own.sem, own.count())
                vec.tensor_copy(p_hi[:], slot_pt[:]).then_inc(own.sem, own.step())
                yield
                vec.wait_ge(own.sem, own.count())
                vec.tensor_tensor(p_lo[:], slot_pt[:], p_hi[:], ALU.subtract).then_inc(own.sem, own.step())

            def one_hot(b, h):
                own = vec_c
                if h == 0:
                    yield
                    vec.wait_ge(own.sem, own.count())
                vec.wait_ge(spread_done.sem, spread_done.at(b, h * QUADS))
                many = [P, QUADS * BLOCKS, GROUPS]
                vec.tensor_tensor(hot_hi[:], expert_hi[:], hi_16[:, h].unsqueeze(1).broadcast_to(many), ALU.is_equal)\
                    .then_inc(own.sem, own.step())
                yield
                vec.tensor_tensor(hot_lo[:], expert_lo[:], lo_16[:, h].unsqueeze(1).broadcast_to([P, P, GROUPS]),
                                  ALU.is_equal).then_inc(own.sem, own.step())

            def picked(b, h):
                own = vec_c
                many = [P, QUADS * BLOCKS, GROUPS]
                yield
                vec.wait_ge(own.sem, own.count() - 1)
                vec.tensor_tensor(pick_hi[:], hot_hi[:], p_hi[:, h].unsqueeze(1).broadcast_to(many), ALU.mult)\
                    .then_inc(own.sem, own.step())
                yield
                vec.tensor_tensor(pick_lo[:], hot_hi[:], p_lo[:, h].unsqueeze(1).broadcast_to(many), ALU.mult)\
                    .then_inc(picks_ready.sem, 1)

            def coefficients(b, n):
                h, q = divmod(n, QUADS)
                if n == 0:
                    vec.wait_ge(dots_ready.sem, dots_ready.at(b))
                vec.wait_ge(spread_done.sem, spread_done.at(b, n + 1))
                few = GROUPS // QUADS
                part = dots[:, :, h * P:(h + 1) * P].rearrange("p a (s g) -> p g s a", s=QUADS)[:, q * few:(q + 1) * few]
                vec.tensor_tensor(part, pick_ps[n % 2][:].rearrange("p (g s a) -> p g s a", g=few, s=QUADS), part,
                                  ALU.mult).then_inc(coef_ready.sem, 1)

            def picks(b, slot):
                own = vec_c
                own.at(b)
                for n in due(COEF, slot):
                    coefficients(b, n)
                    yield
                for h in due(KEYS_TOP, slot):
                    if h == 0:
                        own.begin()
                    yield from find_keys(b, h)
                for h in due(KEYS_NAME, slot):
                    yield from name_keys(b, h)
                if slot == PAIRS:
                    yield from find_pairs(b)
                if slot == NAME_EXPERTS:
                    yield from name_experts(b)
                if slot == TO_SLOTS:
                    yield from lay_out(b)
                for j in due(MLP_MUL, slot):
                    vec.wait_ge(m_silu_ready.sem, m_silu_ready.at(b, j + 1))
                    vec.tensor_tensor(m_h[:, j], m_silu[:, j % 2], pick_ps[j % 2][:, T:2 * T], ALU.mult)\
                        .then_inc(m_h_ready.sem, 1)
                    yield
                for h in due(HOT, slot):
                    yield from one_hot(b, h)
                for h in due(PICKED, slot):
                    yield from picked(b, h)
                if slot == PICKS_VAR:
                    vec.wait_ge(peer_done.sem, peer_done.at(b))
                    yield from normalize_in(own, pick_tiles, norm_c, pick_var)
                    own.end()

            vec.memset(x_t[:], 0.0).then_inc(consts_vec.sem, 1)
            vec.memset(dA[:], 0.0).then_inc(consts_vec.sem, 1)
            vec.memset(norm_a[1][:], 0.0).then_inc(consts_vec.sem, 1)
            vec.wait_ge(*loads["conv"])
            for k in range(TAPS):
                vec.tensor_tensor(w_conv[:, k], w_in[:], taps[:, k], ALU.mult).then_inc(consts_vec.sem, 1)
            vec.wait_ge(*loads["mixer"])
            vec.tensor_scalar(w_skip[:], w_out[:, 0], skip_d[:], None, ALU.mult).then_inc(consts_vec.sem, 1)
            vec.tensor_scalar(inv_dt2[:], inv_dt[:], 2.0, None, ALU.mult).then_inc(consts_vec.sem, 1)
            vec.wait_ge(consts_vec.sem, consts_vec.at(0))
            steps = {stage: dict(mixer=mixer, middle=middle, picks=picks)[stage] for stage in DVE_ORDER}
            weave(steps, -FIRST_ROUND, NB)
            vec.wait_ge(*loads["attention"])
            vec.tensor_copy(gamma_row, gamma[:].broadcast_to([P, T])).then_inc(made.sem, 1)
            vec.wait_ge(made.sem, made.at(0, 1))
            vec.tensor_tensor_scan(decay[:, 0:T], gamma_row, diagonal[:], 0.0, ALU.mult, ALU.add).then_inc(made.sem, 1)
            vec.wait_ge(made.sem, made.at(0, 2))
            vec.tensor_copy(decay[:, T:T + P], decay[:, 0:P]).then_inc(made.sem, 1)
            vec.wait_ge(*loads["moe"])
            vec.wait_ge(*loads["peer"])
            vec.reciprocal(neg_inv_temp[:], temperature[:]).then_inc(made.sem, 1)
            vec.wait_ge(made.sem, made.at(0, 4))
            vec.tensor_scalar(neg_inv_temp[:], neg_inv_temp[:], -1.0, None, ALU.mult).then_inc(made.sem, 1)
            vec.wait_ge(made.sem, made.at(0, 5))
            fill(steps, NB)
            run_and_drain(vec, steps, NB)


def kernel(**inputs):
    import concourse.bacc as bacc
    from concourse.bass_utils import run_bass_kernel_spmd

    A, M, C, D = "L0_attn_", "L0_ffn_", "L1_attn_", "L1_ffn_"
    i = {k: np.asarray(v) for k, v in inputs.items()}

    def flip(a):
        return np.ascontiguousarray(np.swapaxes(a, -1, -2))

    rows = np.arange(P)
    pick = (np.arange(6 * STATES)[:, None] % (2 * STATES) == np.arange(2 * STATES)[None, :])
    arrays = {
        "x": i[A + "x"], "W_in": i[A + "W_in"], "conv_x_w": i[A + "conv_x_w"][:, 0], "conv_z_w": i[A + "conv_z_w"][:, 0],
        "conv_x_b": i[A + "conv_x_b"], "conv_z_b": i[A + "conv_z_b"], "W_xdbl": i[A + "W_xdbl"],
        "W_dt": i[A + "W_dt"], "inv_dt": i[A + "inv_dt"], "D": i[A + "D"], "W_out": i[A + "W_out"],
        "b_out": i[A + "b_out"],
        "moe_Wg": i[M + "Wg"], "moe_Wu": i[M + "Wu"], "moe_Wd": i[M + "Wd"], "Wr": i[M + "Wr"],
        "temperature": i[M + "temperature"],
        "A_Wq_t": flip(i[C + "Wq"]), "A_Wk_t": flip(i[C + "Wk"]), "A_Wv_t": flip(i[C + "Wv"]),
        "bq": i[C + "bq"], "bk": i[C + "bk"], "bv": i[C + "bv"], "gamma": i[C + "gamma"].reshape(1),
        "Wq_p": i[D + "Wq"].reshape(2 * HEADS, RANK, P),
        "keys_p": i[D + "keys"].transpose(2, 0, 3, 1).reshape(2 * HEADS, RANK, KEYS),
        "down_t": flip(i[D + "down_embed"]), "up_embed": i[D + "up_embed"],
        "M_Wg_t": flip(i[D + "Wg"]), "M_Wu_t": flip(i[D + "Wu"]), "M_Wd_t": flip(i[D + "Wd"]),
        "ident": np.eye(P, dtype=np.float32),
        "diagonal": np.eye(P, T, dtype=np.float32),
        "iota8": np.tile(np.arange(8, dtype=np.float32), (P, 1)),
        "iota_16": np.tile(np.arange(TOPK, dtype=np.float16)[None, :, None], (P, 1, H * 2 * SLOTS)),
        "pick_state": np.repeat(pick[:, :, None], P, axis=2).astype(mybir.dt.np(BF16)),
        "expert_lo": np.tile(np.arange(P, dtype=np.float16)[None, :, None], (P, 1, GROUPS)),
        "expert_hi": np.tile(np.arange(QUADS * BLOCKS, dtype=np.float16)[None, :, None], (P, 1, GROUPS)),
        "quad_base": (rows // GROUPS * BLOCKS).astype(np.float32)[:, None],
    }
    nc = bacc.Bacc("TRN2", target_bir_lowering=False, num_devices=1)
    given, aps = {}, {}
    for name, a in arrays.items():
        a = np.ascontiguousarray(a)
        given["in_" + name] = a
        aps[name] = nc.dram_tensor("in_" + name, a.shape, mybir.dt.from_np(a.dtype), kind="ExternalInput").ap()
    shape = arrays["x"].shape
    out = nc.dram_tensor("out", shape, F32, kind="ExternalOutput").ap()
    build(nc, aps, out)
    r = run_bass_kernel_spmd(nc, [given], core_ids=[0])
    return r.results[0]["out"]
```
